# Optimizing a Trainium2 kernel written in Bass

```python
import numpy as np
import jax
import jax.numpy as jnp

def _softmax(x, axis=-1):
    return jax.nn.softmax(x, axis=axis)

def _gelu(x):
    return jax.nn.gelu(x, approximate=True)

def _silu(x):
    return jax.nn.silu(x)

def _sigmoid(x):
    return jax.nn.sigmoid(x)

def _layernorm(x, axis=-1, eps=1e-05):
    m = jnp.mean(x, axis=axis, keepdims=True)
    v = jnp.var(x, axis=axis, keepdims=True)
    return (x - m) / jnp.sqrt(v + eps)

def _scatter_add(tgt, idx, src, axis=0):
    return tgt.at[idx].add(src)

def _segment_sum(src, seg, n):
    return jax.ops.segment_sum(src, seg, n)
kernel_name = 'mk_flamingo_gated_d1_seqx_r4_503bc7'

def setup_inputs(seed: int=0):
    np.random.seed(seed)
    _w = jnp.asarray

    def _rec_inputs():
        import jax
        import jax.numpy as jnp
        _rk = jax.random.key(seed)
        x = 0.0002417 + 0.9998 * jax.random.normal(jax.random.fold_in(_rk, 1), (16, 256, 256), jnp.float32)
        _lenS = 256 - jax.random.randint(jax.random.fold_in(_rk, 7), (16,), 0, max(1, 256 // 4) + 1, jnp.int32)
        _lenS2 = 120 - jax.random.randint(jax.random.fold_in(_rk, 8), (16,), 0, max(1, 120 // 4) + 1, jnp.int32)
        _ctx_1024P = jax.random.normal(jax.random.fold_in(_rk, 11), (16, 16, 256), jnp.float32)
        _ctx_1024c = jax.random.dirichlet(jax.random.fold_in(_rk, 511), 0.3 * jnp.ones((16,), jnp.float32), (16, 120))
        _ctx_1024t = jnp.einsum('bsk,bkd->bsd', _ctx_1024c, _ctx_1024P)
        _ctx_1024t = _ctx_1024t * jax.lax.rsqrt(jnp.mean(jnp.square(_ctx_1024t)) + 1e-12) * 0.953939
        ctx_1024 = 7.22013e-05 + 1.00017 * (_ctx_1024t + 0.3 * jax.random.normal(jax.random.fold_in(_rk, 611), (16, 120, 256), jnp.float32))
        _g = jax.random.normal(jax.random.fold_in(_rk, 9001), (2, 1), jnp.float32)
        _g = jnp.sign(_g) * jnp.maximum(jnp.abs(_g), 1.0) + (_g == 0) * 1.0
        g_xattn = _g[0]
        g_ffn = _g[1]
        return (x, ctx_1024, g_xattn, g_ffn)
    x, ctx_1024, g_xattn, g_ffn = _rec_inputs()

    def _L0_xattn_setup():
        import jax, jax.numpy as jnp
        import numpy as np
        EMBED = 256
        HEADS = 16
        HEAD_DIM = EMBED // HEADS
        EXP_DIM = 2 * HEAD_DIM

        def _feature_map(x, fm_w, fm_b):
            z = jnp.einsum('nshd,ed->nshe', x, fm_w) + fm_b
            return jnp.concatenate([jnp.exp(z), jnp.exp(-z)], axis=-1)
        key = jax.random.key(seed)
        ks = jax.random.split(key, 7)
        N, S = (4, 512)
        values = jax.random.normal(ks[0], (N, S, EMBED), dtype=jnp.float32)
        keys_ = jax.random.normal(ks[1], (N, S, EMBED), dtype=jnp.float32)
        query = jax.random.normal(ks[2], (N, S, EMBED), dtype=jnp.float32)
        fm_w = jnp.eye(HEAD_DIM, dtype=jnp.float32) + 0.02 * jax.random.normal(ks[3], (HEAD_DIM, HEAD_DIM), dtype=jnp.float32)
        fm_b = 0.02 * jax.random.normal(ks[4], (HEAD_DIM,), dtype=jnp.float32)
        fc_w = jax.random.normal(ks[5], (EMBED, HEADS * EXP_DIM), dtype=jnp.float32) * (1.0 / np.sqrt(HEADS * EXP_DIM))
        fc_b = jnp.zeros((EMBED,), dtype=jnp.float32)
        return {'values': values, 'keys': keys_, 'query': query, 'fm_w': fm_w, 'fm_b': fm_b, 'fc_w': fc_w, 'fc_b': fc_b}
    _L0_xattn_all = _L0_xattn_setup()
    _L0_xattn_in = {k: v for k, v in _L0_xattn_all.items() if k in ('fm_w', 'fm_b', 'fc_w', 'fc_b')}
    del _L0_xattn_all

    def _L0_ffn_setup():
        import jax, jax.numpy as jnp
        import numpy as np
        B, N, D, E, DFF = (4, 512, 256, 16, 1024)
        CAPACITY_FACTOR = 2.0
        CAP = int(N * CAPACITY_FACTOR / E)
        SINKHORN_ITERS = 6

        def _sinkhorn(logits, n_iters=SINKHORN_ITERS, tau=1.0):
            t = logits / tau
            for _ in range(n_iters):
                t = t - jax.scipy.special.logsumexp(t, axis=-2, keepdims=True)
                t = t - jax.scipy.special.logsumexp(t, axis=-1, keepdims=True)
            return jnp.exp(t)
        key = jax.random.key(seed)
        ks = jax.random.split(key, 6)
        scaled = lambda k, sh, fan: (jax.random.normal(k, sh, jnp.float32) / np.sqrt(fan)).astype(jnp.float32)
        return {'x': jax.random.normal(ks[0], (B, N, D), jnp.float32), 'gate_query': scaled(ks[1], (E, D), D), 'log_temp': jnp.asarray(np.log(0.5), jnp.float32), 'w1': scaled(ks[2], (E, D, DFF), D), 'b1': jnp.zeros((E, DFF), jnp.float32), 'w2': scaled(ks[3], (E, DFF, D), DFF), 'b2': jnp.zeros((E, D), jnp.float32)}
    _L0_ffn_all = _L0_ffn_setup()
    _L0_ffn_in = {k: v for k, v in _L0_ffn_all.items() if k in ('gate_query', 'log_temp', 'w1', 'b1', 'w2', 'b2')}
    del _L0_ffn_all
    return {'x': x, 'ctx_1024': ctx_1024, 'g_xattn': g_xattn, 'g_ffn': g_ffn, 'L0_xattn_fm_w': _L0_xattn_in['fm_w'], 'L0_xattn_fm_b': _L0_xattn_in['fm_b'], 'L0_xattn_fc_w': _L0_xattn_in['fc_w'], 'L0_xattn_fc_b': _L0_xattn_in['fc_b'], 'L0_ffn_gate_query': _L0_ffn_in['gate_query'], 'L0_ffn_log_temp': _L0_ffn_in['log_temp'], 'L0_ffn_w1': _L0_ffn_in['w1'], 'L0_ffn_b1': _L0_ffn_in['b1'], 'L0_ffn_w2': _L0_ffn_in['w2'], 'L0_ffn_b2': _L0_ffn_in['b2']}

def reference(x, ctx_1024, g_xattn, g_ffn, L0_xattn_fm_w, L0_xattn_fm_b, L0_xattn_fc_w, L0_xattn_fc_b, L0_ffn_gate_query, L0_ffn_log_temp, L0_ffn_w1, L0_ffn_b1, L0_ffn_w2, L0_ffn_b2):
    import jax
    import jax.numpy as jnp

    def _L0_xattn_ref(values, keys, query, fm_w, fm_b, fc_w, fc_b):
        import jax, jax.numpy as jnp
        import numpy as np
        EMBED = 256
        HEADS = 16
        HEAD_DIM = EMBED // HEADS
        EXP_DIM = 2 * HEAD_DIM

        def _feature_map(x, fm_w, fm_b):
            z = jnp.einsum('nshd,ed->nshe', x, fm_w) + fm_b
            return jnp.concatenate([jnp.exp(z), jnp.exp(-z)], axis=-1)
        N, S, _ = query.shape
        v = values.reshape(N, -1, HEADS, HEAD_DIM)
        k = keys.reshape(N, -1, HEADS, HEAD_DIM)
        q = query.reshape(N, -1, HEADS, HEAD_DIM)
        v, k, q = (_feature_map(x, fm_w, fm_b) for x in (v, k, q))
        scores = jnp.einsum('nqhd,nkhd->nhqk', q, k) / jnp.sqrt(jnp.float32(EMBED))
        attn = jax.nn.softmax(scores, axis=-1)
        out = jnp.einsum('nhql,nlhd->nqhd', attn, v)
        out = out.reshape(N, S, HEADS * EXP_DIM)
        return out @ fc_w.T + fc_b

    def _L0_ffn_ref(x, gate_query, log_temp, w1, b1, w2, b2):
        import jax, jax.numpy as jnp
        import numpy as np
        B, N, D, E, DFF = (4, 512, 256, 16, 1024)
        CAPACITY_FACTOR = 2.0
        CAP = int(N * CAPACITY_FACTOR / E)
        SINKHORN_ITERS = 6

        def _sinkhorn(logits, n_iters=SINKHORN_ITERS, tau=1.0):
            t = logits / tau
            for _ in range(n_iters):
                t = t - jax.scipy.special.logsumexp(t, axis=-2, keepdims=True)
                t = t - jax.scipy.special.logsumexp(t, axis=-1, keepdims=True)
            return jnp.exp(t)
        b, n, d = x.shape
        gate_logits = jnp.einsum('bnd,ed->ben', x, gate_query)
        affinity_logits = gate_logits / jnp.exp(log_temp)
        affinity = _sinkhorn(affinity_logits)
        gates, idx = jax.lax.top_k(affinity, CAP)
        expert_in = jnp.take_along_axis(x[:, None, :, :], idx[..., None], axis=2)
        h = jax.nn.gelu(jnp.einsum('becd,edf->becf', expert_in, w1) + b1[None, :, None, :])
        expert_out = jnp.einsum('becf,efd->becd', h, w2) + b2[None, :, None, :]
        out = jnp.zeros_like(x)
        out = out.at[jnp.arange(b)[:, None, None], idx].add(gates[..., None] * expert_out)
        return out
    x = x + jnp.tanh(g_xattn[0]) * _L0_xattn_ref(ctx_1024, ctx_1024, _layernorm(x, axis=-1), L0_xattn_fm_w, L0_xattn_fm_b, L0_xattn_fc_w, L0_xattn_fc_b)
    x = x + jnp.tanh(g_ffn[0]) * _L0_ffn_ref(_layernorm(x, axis=-1), L0_ffn_gate_query, L0_ffn_log_temp, L0_ffn_w1, L0_ffn_b1, L0_ffn_w2, L0_ffn_b2)
    return x

_drawn_inputs = setup_inputs


def setup_inputs(seed=0):
    import zlib

    import numpy as np

    out = dict(_drawn_inputs(seed))
    spreads = {'L0_xattn_fc_b': (0.0, 0.698), 'L0_ffn_b1': (0.0, 0.8), 'L0_ffn_b2': (0.0, 0.8)}
    factors = {'L0_ffn_gate_query': 8.0, 'L0_ffn_w1': 8.0, 'L0_ffn_w2': 8.0}
    for name, (base, spread) in spreads.items():
        noise = np.random.default_rng([zlib.crc32(name.encode()), seed]).standard_normal(out[name].shape)
        drawn = base * np.exp(spread * noise) if base else spread * noise
        out[name] = jnp.asarray(drawn.astype(out[name].dtype))
    for name, factor in factors.items():
        out[name] = (out[name] * factor).astype(out[name].dtype)
    return out
```

```python
from contextlib import ExitStack

import numpy as np

import concourse.bass as bass
from concourse import mybir

F32 = mybir.dt.float32
F32R = mybir.dt.float32r
I32 = mybir.dt.int32
U32 = mybir.dt.uint32
ALU = mybir.AluOpType
ACT = mybir.ActivationFunctionType
AX = mybir.AxisListType.X

P = 128
B, N, D = 16, 256, 256
KC = 120
HEADS, HD = 16, 16
EXP = 2 * HD
HG = P // EXP
G = HEADS // HG
T = N // P
KD = D // P
UNITS = T * G
E, FF = 16, 1024
M = FF // P
CAP = int(512 * 2.0 / E)
HB = 8
SINKHORN = 6
EPS = 1e-5
SCALE = 1.0 / 16.0


class Arena:

    def __init__(self, nc, start, end):
        self.nc, self.at, self.end = nc, start, end

    def take(self, name, shape, dt=F32):
        size = 4 * int(np.prod(shape[1:]))
        size += -size % 32
        assert self.at + size <= self.end, (name, self.at + size, self.end)
        tensor = self.nc.alloc_sbuf_tensor_at(name, shape, dt, offset=self.at)
        self.at += size
        return tensor



A_STEPS = [(0, "x2T", 0, -1), (1, "cT", 0, 1), (1, "oT", 1, -1), (2, "xnT", 0, 1), (3, "z", 0, 1), (4, "z", 1, 1),
           (5, "z", 2, 1), (5, "oT", 0, 0), (6, "z", 3, 1), (6, "x2T", 1, -1)]
B_STEPS = [(1, "logits", 0, -1), (3, "fc", 1, -1), (6, "fc", 0, 0), (7, "logits", 1, -1), (7, "v", 0, 1)]


def kept(steps, b):
    if not isinstance(b, int):
        return steps
    return [s for s in steps if 0 <= b + s[3] < B and (b < B or s[3] < 0)]


def order_in(steps, prologue, b, step, part, offset):
    names = [s[1:] for s in kept(steps, b)]
    if isinstance(b, int) and b == 0:
        before = prologue
    else:
        before = prologue + len(kept(steps, 0)) + len(steps) * (b - 1)
        if isinstance(b, int) and b == B:
            before = prologue + len(kept(steps, 0)) + len(steps) * (B - 2) + len(kept(steps, B - 1))
    return before + names.index((step, part, offset))


A_PROLOGUE = ["cT", "xnT", "z0", "z1", "z2", "z3"]
B_PROLOGUE = ["v"]


def use_a(b, step, part, offset):
    if b is None:
        return A_PROLOGUE.index(step if step != "z" else f"z{part}")
    return order_in(A_STEPS, len(A_PROLOGUE), b, step, part, offset)


def use_b(b, step, part, offset):
    if b is None:
        return 0
    return order_in(B_STEPS, len(B_PROLOGUE), b, step, part, offset)


def over_batches(eng, body):
    body(0, 0)
    body(1, 1)
    with eng.Fori(2, B - 2, 2) as i:
        body(i, 0)
        body(i + 1, 1)
    body(B - 2, 0)
    body(B - 1, 1)


def attention(nc, dram, keep, arena):
    with ExitStack() as ctx:
        sb = arena.take

        def ps(name):
            return ctx.enter_context(nc.psum_tensor(name, [P, 512], F32))

        def sem(name):
            return ctx.enter_context(nc.semaphore(name))

        ident, x2_all, logits = keep["ident"], keep["x2_all"], keep["logits"]

        block_w = sb("block_w", [P, 2, P])
        sign = sb("sign", [P, 1])
        sign_bits = sb("sign_bits", [P, 1], I32)
        bias_b = sb("bias_b", [P, 1])
        sign_bias = sb("sign_bias", [P, 1])
        head_mask = sb("head_mask", [P, HG])
        fc_w = sb("fc_w", [P, G, D])
        fc_bias = sb("fc_bias", [P, D])
        gate_in = sb("gate_in", [P, 2])
        tanh_x = sb("tanh_x", [P, 1])
        log_temp = sb("log_temp", [P, 1])
        inv_temp = sb("inv_temp", [P, 1])
        router_w = sb("router_w", [P, KD, E])
        neg_half = sb("neg_half", [P, T])
        eps = sb("eps", [P, T])
        x_in = [sb(f"x_in{p}", [P, T, D]) for p in range(2)]
        ctx_in = [sb(f"ctx_in{p}", [KC, D]) for p in range(2)]
        x_bias = [sb(f"x_bias{p}", [P, T, D]) for p in range(2)]
        feat = [sb(f"feat{p}", [P, G, N + KC]) for p in range(2)]
        k_block = [sb(f"k_block{p}", [P, G, HG * KC]) for p in range(2)]
        v_one = [sb(f"v_one{p}", [KC, HEADS, EXP + 1]) for p in range(2)]
        x1_out = [sb(f"x1_out{p}", [P, T, D]) for p in range(2)]
        stat1 = sb("stat1", [P, T, 6])
        mean_var1 = sb("mean_var1", [P, T, 2])
        var_eps1 = sb("var_eps1", [P, T])
        rstd1 = sb("rstd1", [P, T])
        xn = sb("xn", [P, T, D])
        xnT = sb("xnT", [P, KD, N])
        cT = sb("cT", [P, KD, KC])
        row_max = [sb(f"row_max{i}", [P, HG]) for i in range(2)]
        prob = [sb(f"prob{i}", [P, HG * KC]) for i in range(4)]
        probT = [sb(f"probT{i}", [KC, HG * P]) for i in range(2)]
        recip = [sb(f"recip{i}", [P, HG]) for i in range(2)]
        attn = [sb(f"attn{t}", [P, G * P]) for t in range(T)]
        attnT = sb("attnT", [P, G * P])
        stat2 = sb("stat2", [P, 6])
        mean_var2 = [sb(f"mean_var2{t}", [P, 2]) for t in range(T)]
        var_eps2 = sb("var_eps2", [P, 1])
        rstd2 = [sb(f"rstd2{t}", [P, 1]) for t in range(T)]
        x2 = [sb(f"x2{t}", [P, D]) for t in range(T)]
        x2T = sb("x2T", [P, KD * P])

        score_ps = [ps(f"score_ps{i}") for i in range(2)]
        probT_ps = [ps(f"probT_ps{i}") for i in range(2)]
        value_ps = [ps(f"value_ps{i}") for i in range(2)]
        bank_a = ps("bank_a")
        bank_b = ps("bank_b")

        weights_in = sem("weights_in")
        zeroed = sem("zeroed")
        blocks_in = sem("blocks_in")
        made = sem("made")
        masks_made = sem("masks_made")
        dve_const = sem("dve_const")
        act_const = sem("act_const")
        x_loaded = [sem(f"x_loaded{p}") for p in range(2)]
        x1_stored = [sem(f"x1_stored{p}") for p in range(2)]
        stats1_raw, stats1_done = sem("stats1_raw"), sem("stats1_done")
        var1_done, rstd1_done, xn_done = sem("var1_done"), sem("rstd1_done"), sem("xn_done")
        x_bias_done = sem("x_bias_done")
        k_block_done = sem("k_block_done")
        a_filled, a_emptied = sem("a_filled"), sem("a_emptied")
        b_filled, b_emptied = sem("b_filled"), sem("b_emptied")
        scored, max_done, shifted, exp_done = sem("scored"), sem("max_done"), sem("shifted"), sem("exp_done")
        turned, turned_out = sem("turned"), sem("turned_out")
        valued, recip_done, normed = sem("valued"), sem("recip_done"), sem("normed")
        x1_done, stats2_raw, stats2_done = sem("x1_done"), sem("stats2_raw"), sem("stats2_done")
        var2_done, rstd2_done, x2_done, x2_kept = sem("var2_done"), sem("rstd2_done"), sem("x2_done"), sem("x2_kept")

        block = ctx.enter_context(nc.Block())

        @block.sync
        def _(sp):
            def load(b, p):
                if not (isinstance(b, int) and b < 2):
                    sp.wait_ge(xn_done, b - 1)
                    sp.wait_ge(x_bias_done, b - 1)
                    home, first = (None, 0) if isinstance(b, int) and b == 2 else (b - 3, 1)
                    sp.wait_ge(a_filled, use_a(home, "cT", 0, first) + 1)
                sp.dma_start(x_in[p][:, :, :], dram["x"][bass.ds(b * N, N), :].rearrange("(t p) d -> p t d", p=P)
                             ).then_inc(x_loaded[p], 16)
                sp.dma_start(ctx_in[p][:, :], dram["ctx"][bass.ds(b * KC, KC), :]).then_inc(x_loaded[p], 16)

            def store(b, p):
                sp.wait_ge(x1_done, T * b + T)
                sp.dma_start(dram["x1"][bass.ds(b * P, P), :], x1_out[p][:, :, :].rearrange("p t d -> p (t d)")
                             ).then_inc(x1_stored[p], 16)

            load(0, 0)
            sp.wait_ge(zeroed, 1)
            for j in range(2 * HG):
                sp.dma_start(block_w[HD * j:HD * j + HD, j // HG, EXP * (j % HG):EXP * (j % HG) + EXP]
                             .rearrange("d (s e) -> d s e", s=2),
                             dram["fm_wT"].rearrange("d (s e) -> d s e", s=1).to_broadcast([HD, 2, HD])
                             ).then_inc(blocks_in, 16)
                sp.dma_start(bias_b[HD * j:HD * j + HD, :], dram["fm_b"]).then_inc(blocks_in, 16)
            load(1, 1)
            sp.dma_start(gate_in[:, 0:1], dram["g_xattn"].partition_broadcast(P)).then_inc(weights_in, 16)
            sp.dma_start(gate_in[:, 1:2], dram["g_ffn"].partition_broadcast(P)).then_inc(weights_in, 16)
            sp.dma_start(log_temp[:, :], dram["log_temp"].partition_broadcast(P)).then_inc(weights_in, 16)
            sp.dma_start(fc_bias[:, :], dram["fc_b"].partition_broadcast(P)).then_inc(weights_in, 16)
            sp.dma_start(fc_w[:, :, :], dram["fc_wT"].rearrange("(g p) d -> p g d", p=P)).then_inc(weights_in, 16)
            sp.dma_start(router_w[:, :, :], dram["gate_queryT"].rearrange("(k p) e -> p k e", p=P)
                         ).then_inc(weights_in, 16)
            load(2, 0)
            load(3, 1)
            store(0, 0)
            with sp.Fori(2, B - 3, 2) as i:
                load(i + 2, 0)
                store(i - 1, 1)
                load(i + 3, 1)
                store(i, 0)
            for b in range(B - 3, B):
                store(b, b % 2)
            for p in range(2):
                sp.wait_ge(x1_stored[p], 16 * B // 2)

        @block.gpsimd
        def _(pool):
            pool.memset(block_w[:, :, :], 0.0).then_inc(zeroed, 1)
            pool.memset(ident[:, :], 0.0).then_inc(zeroed, 1)
            pool.wait_ge(zeroed, 2)
            pool.affine_select(out=ident[:, :], in_=ident[:, :], compare_op=ALU.not_equal, fill=1.0, base=0,
                               pattern=[[-1, P]], channel_multiplier=1).then_inc(made, 1)
            pool.iota(sign_bits[:, :], [[0, 1]], base=0, channel_multiplier=1).then_inc(made, 1)
            pool.memset(eps[:, :], EPS).then_inc(zeroed, 1)
            pool.memset(neg_half[:, :], -0.5).then_inc(made, 1)
            pool.wait_ge(made, 3)
            pool.wait_ge(zeroed, 3)

            def inv_std1(b):
                pool.wait_ge(stats1_done, b + 1)
                pool.tensor_tensor(var_eps1[:, :], mean_var1[:, :, 1], eps[:, 0:T], ALU.add).then_inc(var1_done, 1)
                pool.wait_ge(var1_done, b + 1)
                pool.tensor_tensor(rstd1[:, :], var_eps1[:, :], neg_half[:, 0:T], ALU.pow).then_inc(rstd1_done, 1)

            def inv_std2(b, t):
                n = T * b + t + 1
                pool.wait_ge(stats2_done, n)
                pool.tensor_tensor(var_eps2[:, :], mean_var2[t][:, 1:2], eps[:, 0:1], ALU.add).then_inc(var2_done, 1)
                pool.wait_ge(var2_done, n)
                pool.tensor_tensor(rstd2[t][:, :], var_eps2[:, :], neg_half[:, 0:1], ALU.pow).then_inc(rstd2_done, 1)

            def add_bias(b, p):
                pool.wait_ge(x_loaded[p], 16 * b + 32 - 16 * p)
                if not (isinstance(b, int) and b < 2):
                    pool.wait_ge(x1_done, T * (b - 1))
                for t in range(T):
                    ins = pool.tensor_tensor(x_bias[p][:, t, :], x_in[p][:, t, :], fc_bias[:, :], ALU.add)
                ins.then_inc(x_bias_done, 1)

            def block_keys(b, p, g, home):
                n = use_a(home, "z", g, 1)
                pool.wait_ge(a_emptied, n + 1)
                if not (isinstance(b, int) and b < 2):
                    pool.wait_ge(scored, UNITS * (b - 1))
                pool.tensor_tensor(
                    k_block[p][:, g, :].rearrange("p (h k) -> p h k", h=HG),
                    feat[p][:, g, N:].rearrange("p (h k) -> p h k", h=1).to_broadcast([P, HG, KC]),
                    head_mask[:, :].rearrange("p (h k) -> p h k", k=1).to_broadcast([P, HG, KC]),
                    ALU.mult).then_inc(k_block_done, 1)

            def keep_x2(b, t):
                pool.wait_ge(x2_done, T * b + t + 1)
                pool.tensor_copy(x2_all[:, bass.ds(T * b + t, 1), :], x2[t][:, :].rearrange("p (a d) -> p a d", a=1)
                                 ).then_inc(x2_kept, 1)

            inv_std1(0)
            pool.wait_ge(dve_const, 3)
            add_bias(0, 0)
            for g in range(G):
                block_keys(0, 0, g, None)

            def batch(b, p):
                first, last = isinstance(b, int) and b == 0, isinstance(b, int) and b == B - 1
                if not first:
                    keep_x2(b - 1, 0)
                if not last:
                    inv_std1(b + 1)
                if not last:
                    block_keys(b + 1, 1 - p, 0, b)
                if not first:
                    inv_std2(b - 1, 1)
                if not last:
                    for g in range(1, G):
                        block_keys(b + 1, 1 - p, g, b)
                if not first:
                    keep_x2(b - 1, 1)
                inv_std2(b, 0)
                if not last:
                    add_bias(b + 1, 1 - p)

            over_batches(pool, batch)
            keep_x2(B - 1, 0)
            inv_std2(B - 1, 1)
            keep_x2(B - 1, 1)

        @block.scalar
        def _(act):
            act.wait_ge(weights_in, 6 * 16)
            act.activation(tanh_x[:, :], gate_in[:, 0:1], ACT.Tanh).then_inc(act_const, 1)
            act.activation(keep["tanh_f"][:, :], gate_in[:, 1:2], ACT.Tanh)
            act.preload_act_table_set("natural_log_exp_and_others")
            act.activation(inv_temp[:, :], log_temp[:, :], ACT.Exp, scale=-1.0).then_inc(act_const, 1)
            act.wait_ge(dve_const, 2)

            def exponent(s, b):
                u = UNITS * b + s
                act.wait_ge(shifted, u + 1)
                act.activation(prob[s % 4][:, :], prob[s % 4][:, :], ACT.Exp, scale=SCALE).then_inc(exp_done, 1)

            def copy_turned(s, b):
                u = UNITS * b + s
                act.wait_ge(turned, u + 1)
                if not (isinstance(b, int) and u < 2):
                    act.wait_ge(valued, u - 1)
                act.activation(probT[s % 2][:, :], probT_ps[s % 2][0:KC, :], ACT.Copy).then_inc(turned_out, 1)

            def empty_a(home, q, step, part, offset):
                act.wait_ge(a_filled, use_a(home, step, part, offset) + 1)
                if step == "cT":
                    ins = act.activation(cT[:, :, :].rearrange("p k c -> p (k c)"), bank_a[:, 0:KD * KC], ACT.Copy)
                elif step == "xnT":
                    ins = act.activation(xnT[:, :, :].rearrange("p k c -> p (k c)"), bank_a[:, :], ACT.Copy)
                elif step == "z":
                    ins = act.activation(feat[q][:, part, :], bank_a[:, 0:N + KC], ACT.Exp,
                                         bias=sign_bias[:, :], scale=sign[:, :])
                elif step == "oT":
                    ins = act.activation(attnT[:, :], bank_a[:, :], ACT.Copy)
                else:
                    ins = act.activation(x2T[:, :], bank_a[:, 0:KD * P], ACT.Copy)
                ins.then_inc(a_emptied, 1)

            for step, part in (("cT", 0), ("xnT", 0), ("z", 0), ("z", 1), ("z", 2), ("z", 3)):
                empty_a(None, 0, step, part, 1)
            exponent(0, 0)

            def batch(b, p):
                for s in range(UNITS):
                    if s < UNITS - 1:
                        exponent(s + 1, b)
                    elif not (isinstance(b, int) and b == B - 1):
                        exponent(0, b + 1)
                    steps = [x for x in kept(A_STEPS, b) if x[0] == s]
                    for n, (_, step, part, offset) in enumerate(steps):
                        if n == 1:
                            copy_turned(s, b)
                        empty_a(b, (p + offset) % 2, step, part, offset)
                    if len(steps) < 2:
                        copy_turned(s, b)

            over_batches(act, batch)
            for _, step, part, offset in kept(A_STEPS, B):
                empty_a(B, 1, step, part, offset)

        @block.tensor
        def _(pe):
            def scores(s, b, p):
                u, g, t = UNITS * b + s, s % G, s // G
                if not (isinstance(b, int) and u < 2):
                    pe.wait_ge(shifted, u - 1)
                if t == 0:
                    pe.wait_ge(k_block_done, G * b + g + 1)
                pe.matmul(score_ps[s % 2][:, 0:HG * KC], feat[p][:, g, t * P:t * P + P], k_block[p][:, g, :],
                          start=True, stop=True).then_inc(scored, 1)

            def turn(s, b):
                u = UNITS * b + s
                pe.wait_ge(exp_done, u + 1)
                if not (isinstance(b, int) and u < 2):
                    pe.wait_ge(turned_out, u - 1)
                for h in range(HG):
                    ins = pe.transpose(probT_ps[s % 2][0:KC, h * P:h * P + P],
                                       prob[s % 4][:, h * KC:h * KC + KC], ident[:, :])
                ins.then_inc(turned, 1)

            def values(s, b, p):
                u, g = UNITS * b + s, s % G
                pe.wait_ge(turned_out, u + 1)
                if not (isinstance(b, int) and u < 2):
                    pe.wait_ge(normed, u - 1)
                if s == 0:
                    home = None if isinstance(b, int) and b == 0 else b - 1
                    pe.wait_ge(b_emptied, use_b(home, "v", 0, 1) + 1)
                for h in range(HG):
                    ins = pe.matmul(value_ps[s % 2][:, h * (EXP + 1):(h + 1) * (EXP + 1)],
                                    probT[s % 2][:, h * P:h * P + P], v_one[p][:, HG * g + h, :],
                                    start=True, stop=True)
                ins.then_inc(valued, 1)

            def fill_a(home, step, part, b, q):
                offset = 1 if home is None else {"x2T": -1, "cT": 1, "xnT": 1, "z": 1, "oT": -part}[step]
                n = use_a(home, step, part, offset)
                if not (isinstance(n, int) and n == 0):
                    pe.wait_ge(a_emptied, n)
                if step == "cT":
                    pe.wait_ge(x_loaded[q], 16 * b + 32 - 16 * q)
                    for k in range(KD):
                        ins = pe.transpose(bank_a[:, k * KC:k * KC + KC], ctx_in[q][:, k * P:k * P + P],
                                           ident[0:KC, 0:KC])
                elif step == "xnT":
                    pe.wait_ge(xn_done, b + 1)
                    for k in range(KD):
                        for t in range(T):
                            ins = pe.transpose(bank_a[:, k * N + t * P:k * N + t * P + P],
                                               xn[:, t, k * P:k * P + P], ident[:, :])
                elif step == "z":
                    k, w = part // 2, part % 2
                    pe.matmul(bank_a[:, 0:N], block_w[:, w, :], xnT[:, k, :], start=True, stop=True)
                    ins = pe.matmul(bank_a[:, N:N + KC], block_w[:, w, :], cT[:, k, :], start=True, stop=True)
                elif step == "oT":
                    pe.wait_ge(normed, UNITS * b + G * (part + 1))
                    for g in range(G):
                        ins = pe.transpose(bank_a[:, g * P:g * P + P], attn[part][:, g * P:g * P + P], ident[:, :])
                else:
                    pe.wait_ge(x2_done, T * b + part + 1)
                    for k in range(KD):
                        ins = pe.transpose(bank_a[:, k * P:k * P + P], x2[part][:, k * P:k * P + P], ident[:, :])
                ins.then_inc(a_filled, 1)

            def fill_b(home, step, part, b, q, a_home):
                offset = 1 if home is None else {"v": 1, "logits": -1, "fc": -part}[step]
                n = use_b(home, step, part, offset)
                if not (isinstance(n, int) and n == 0):
                    pe.wait_ge(b_emptied, n)
                if step == "v":
                    pe.wait_ge(a_emptied, use_a(a_home, "z", G - 1, 1) + 1)
                    for g in range(G):
                        ins = pe.transpose(bank_b[0:KC, g * P:g * P + P], feat[q][:, g, N:], ident[:, :])
                elif step == "fc":
                    pe.wait_ge(a_emptied, use_a(a_home, "oT", part, -part) + 1)
                    for g in range(G):
                        ins = pe.matmul(bank_b[:, 0:D], attnT[:, g * P:g * P + P], fc_w[:, g, :],
                                        start=(g == 0), stop=(g == G - 1))
                else:
                    pe.wait_ge(a_emptied, use_a(a_home, "x2T", part, -1) + 1)
                    for k in range(KD):
                        ins = pe.matmul(bank_b[:, 0:E], x2T[:, k * P:k * P + P], router_w[:, k, :],
                                        start=(k == 0), stop=(k == KD - 1))
                ins.then_inc(b_filled, 1)

            pe.wait_ge(made, 3)
            pe.wait_ge(masks_made, 1 + HG + 2)
            pe.wait_ge(blocks_in, 2 * HG * 2 * 16)
            pe.wait_ge(weights_in, 6 * 16)
            for step, part in (("cT", 0), ("xnT", 0), ("z", 0), ("z", 1), ("z", 2), ("z", 3)):
                fill_a(None, step, part, 0, 0)
            fill_b(None, "v", 0, 0, 0, None)
            scores(0, 0, 0)
            scores(1, 0, 0)

            def batch(b, p):
                first, last = isinstance(b, int) and b == 0, isinstance(b, int) and b == B - 1
                for s in range(UNITS):
                    if s < UNITS - 2:
                        scores(s + 2, b, p)
                    elif not last:
                        scores(s + 2 - UNITS, b + 1, 1 - p)
                    steps = [x for x in kept(A_STEPS, b) if x[0] == s]
                    for n, (_, step, part, offset) in enumerate(steps[:1]):
                        fill_a(b, step, part, b + offset, (p + offset) % 2)
                    turn(s, b)
                    if s > 0:
                        values(s - 1, b, p)
                    elif not first:
                        values(UNITS - 1, b - 1, 1 - p)
                    for _, step, part, offset in [x for x in kept(B_STEPS, b) if x[0] == s]:
                        fill_b(b, step, part, b + offset, (p + offset) % 2, b)
                    for _, step, part, offset in steps[1:]:
                        fill_a(b, step, part, b + offset, (p + offset) % 2)

            over_batches(pe, batch)
            values(UNITS - 1, B - 1, 1)
            for _, step, part, offset in kept(A_STEPS, B):
                fill_a(B, step, part, B - 1, 1)
                if step == "x2T":
                    fill_b(B, "logits", part, B - 1, 1, B)
                else:
                    fill_b(B, "fc", part, B - 1, 1, B)

        @block.vector
        def _(dve):
            dve.memset(head_mask[:, :], 0.0).then_inc(masks_made, 1)
            dve.wait_ge(masks_made, 1)
            for h in range(HG):
                dve.memset(head_mask[EXP * h:EXP * h + EXP, h:h + 1], 1.0).then_inc(masks_made, 1)
            for p in range(2):
                dve.memset(v_one[p][:, :, EXP:EXP + 1], 1.0).then_inc(masks_made, 1)
            dve.wait_ge(made, 3)
            dve.tensor_scalar(sign_bits[:, :], sign_bits[:, :], 4, 1, ALU.logical_shift_right, ALU.bitwise_and
                              ).then_inc(stats1_raw, 1)
            dve.wait_ge(stats1_raw, 1)
            dve.tensor_scalar(sign[:, :], sign_bits[:, :], -2.0, 1.0, ALU.mult, ALU.add).then_inc(dve_const, 1)
            dve.wait_ge(dve_const, 1)
            dve.wait_ge(blocks_in, 2 * HG * 2 * 16)
            dve.tensor_tensor(sign_bias[:, :], bias_b[:, :], sign[:, :], ALU.mult).then_inc(dve_const, 1)
            dve.wait_ge(act_const, 2)
            dve.wait_ge(weights_in, 6 * 16)
            dve.tensor_scalar(fc_bias[:, :], fc_bias[:, :], tanh_x[:, 0:1], None, ALU.mult).then_inc(dve_const, 1)

            def stats(b, p):
                dve.wait_ge(x_loaded[p], 16 * b + 32 - 16 * p)
                for t in range(T):
                    dve.bn_stats(stat1[:, t, :], x_in[p][:, t, :]).then_inc(stats1_raw, 1)
                dve.wait_ge(stats1_raw, 1 + T * b + T)
                dve.memset(keep["spare_dve"][:, :], 0.0)
                for t in range(T):
                    ins = dve.bn_aggr(mean_var1[:, t, :], stat1[:, t, :])
                ins.then_inc(stats1_done, 1)

            def norm_x(b, p):
                dve.wait_ge(rstd1_done, b + 1)
                for t in range(T):
                    ins = dve.tensor_scalar(xn[:, t, :], x_in[p][:, t, :], mean_var1[:, t, 0:1], rstd1[:, t:t + 1],
                                            ALU.subtract, ALU.mult)
                ins.then_inc(xn_done, 1)

            def shift(s, b):
                u = UNITS * b + s
                tile = score_ps[s % 2][:, 0:HG * KC].rearrange("p (h k) -> p h k", h=HG)
                dve.wait_ge(scored, u + 1)
                dve.tensor_reduce(row_max[s % 2][:, :], tile, AX, ALU.max).then_inc(max_done, 1)
                dve.wait_ge(max_done, u + 1)
                if not (isinstance(b, int) and u < 4):
                    dve.wait_ge(turned, u - 3)
                dve.tensor_tensor(prob[s % 4][:, :].rearrange("p (h k) -> p h k", h=HG), tile,
                                  row_max[s % 2][:, :].rearrange("p (h k) -> p h k", k=1).to_broadcast([P, HG, KC]),
                                  ALU.subtract).then_inc(shifted, 1)

            def normalise(s, b):
                u, g, t = UNITS * b + s, s % G, s // G
                tile = value_ps[s % 2][:, 0:HG * (EXP + 1)].rearrange("p (h e) -> p h e", h=HG)
                dve.wait_ge(valued, u + 1)
                dve.reciprocal(recip[s % 2][:, :].rearrange("p (h k) -> p h k", k=1), tile[:, :, EXP:EXP + 1]
                               ).then_inc(recip_done, 1)
                dve.wait_ge(recip_done, u + 1)
                dve.tensor_tensor(attn[t][:, g * P:g * P + P].rearrange("p (h e) -> p h e", h=HG), tile[:, :, 0:EXP],
                                  recip[s % 2][:, :].rearrange("p (h k) -> p h k", k=1).to_broadcast([P, HG, EXP]),
                                  ALU.mult).then_inc(normed, 1)

            def empty_b(home, step, part, b, q):
                offset = 1 if home is None else {"v": 1, "logits": -1, "fc": -part}[step]
                dve.wait_ge(b_filled, use_b(home, step, part, offset) + 1)
                if step == "v":
                    dve.tensor_copy(v_one[q][:, :, 0:EXP], bank_b[0:KC, :].rearrange("p (h e) -> p h e", e=EXP)
                                    ).then_inc(b_emptied, 1)
                elif step == "logits":
                    dve.tensor_scalar(logits[:, part, bass.ds(b, 1), :],
                                      bank_b[:, 0:E].rearrange("p (a e) -> p a e", a=1), inv_temp[:, 0:1], None,
                                      ALU.mult).then_inc(b_emptied, 1)
                else:
                    n = T * b + part + 1
                    dve.wait_ge(x_bias_done, b + 1)
                    if part == 0 and not (isinstance(b, int) and b < 2):
                        dve.wait_ge(x1_stored[q], 8 * b - 8 * q)
                    dve.scalar_tensor_tensor(x1_out[q][:, part, :], bank_b[:, 0:D], tanh_x[:, 0:1],
                                             x_bias[q][:, part, :], ALU.mult, ALU.add).then_inc(b_emptied, 1)
                    dve.wait_ge(b_emptied, use_b(home, step, part, offset) + 1)
                    dve.bn_stats(stat2[:, :], x1_out[q][:, part, :]).then_inc(x1_done, 1)
                    dve.wait_ge(x1_done, n)
                    dve.memset(keep["spare_dve"][:, :], 0.0)
                    dve.bn_aggr(mean_var2[part][:, :], stat2[:, :]).then_inc(stats2_done, 1)

            def norm_x2(b, t, q):
                n = T * b + t + 1
                dve.wait_ge(rstd2_done, n)
                if not (isinstance(b, int) and b == 0):
                    dve.wait_ge(x2_kept, n - T)
                    dve.wait_ge(a_filled, use_a(b, "x2T", t, -1) + 1)
                dve.tensor_scalar(x2[t][:, :], x1_out[q][:, t, :], mean_var2[t][:, 0:1], rstd2[t][:, 0:1],
                                  ALU.subtract, ALU.mult).then_inc(x2_done, 1)

            stats(0, 0)
            norm_x(0, 0)
            empty_b(None, "v", 0, 0, 0)
            shift(0, 0)

            def batch(b, p):
                first, last = isinstance(b, int) and b == 0, isinstance(b, int) and b == B - 1
                for s in range(UNITS):
                    if s < UNITS - 1:
                        shift(s + 1, b)
                    elif not last:
                        shift(0, b + 1)
                    if s > 0:
                        normalise(s - 1, b)
                    elif not first:
                        normalise(UNITS - 1, b - 1)
                    for _, step, part, offset in [x for x in kept(B_STEPS, b) if x[0] == s]:
                        empty_b(b, step, part, b + offset, (p + offset) % 2)
                    if s == 0 and not last:
                        stats(b + 1, 1 - p)
                    if s == 1 and not last:
                        norm_x(b + 1, 1 - p)
                    if s == 4 and not first:
                        norm_x2(b - 1, 1, 1 - p)
                    if s == 7:
                        norm_x2(b, 0, p)

            over_batches(dve, batch)
            normalise(UNITS - 1, B - 1)
            for _, step, part, offset in kept(A_STEPS, B):
                if step == "x2T":
                    empty_b(B, "logits", part, B - 1, 1)
                else:
                    empty_b(B, "fc", part, B - 1, 1)
                    norm_x2(B - 1, 1, 1)



def route(nc, dram, keep, arena):
    with ExitStack() as ctx:
        def sb2(name, shape, dt=F32):
            return [arena.take(f"{name}{h}", shape, dt) for h in range(2)]

        def sem(name):
            return ctx.enter_context(nc.semaphore(name))

        ident, logits = keep["ident"], keep["logits"]
        slot_index, slot_gate = keep["slot_index"], keep["slot_gate"]
        Q = T * HB
        over_e = sb2("over_e", [P, Q, E])
        over_e_max = sb2("over_e_max", [P, Q])
        over_e_exp = sb2("over_e_exp", [P, Q, E])
        over_e_sum = sb2("over_e_sum", [P, Q])
        over_e_log = sb2("over_e_log", [P, Q])
        over_e_out = sb2("over_e_out", [P, Q, E])
        neg_max = sb2("neg_max", [P, 1])
        over_n_exp = sb2("over_n_exp", [P, N])
        over_n_sum = sb2("over_n_sum", [P, 1])
        over_n_log = sb2("over_n_log", [P, 1])
        over_n = sb2("over_n", [P, N])
        affinity = sb2("affinity", [P, N])
        top = sb2("top", [P, CAP])
        top_at = sb2("top_at", [P, CAP], U32)
        top_twice = sb2("top_twice", [P, 2, CAP])
        at_twice = sb2("at_twice", [P, 2, CAP])
        to_n_ps = [ctx.enter_context(nc.psum_tensor(f"to_n_ps{h}", [P, 512], F32)) for h in range(2)]
        to_e_ps = [ctx.enter_context(nc.psum_tensor(f"to_e_ps{h}", [P, 512], F32)) for h in range(2)]
        slot_ps = [ctx.enter_context(nc.psum_tensor(f"slot_ps{h}", [P, 512], F32)) for h in range(2)]

        e_max, e_shift, e_exp, e_sum, e_log, e_done = (sem("e_" + n) for n in ("max", "shift", "exp", "sum", "log", "done"))
        in_n, n_max, n_exp, n_log, n_done, in_e = (sem(n) for n in ("in_n", "n_max", "n_exp", "n_log", "n_done", "in_e"))
        gates_done, topped, listed, slots_turned, slots_kept, index_out = (
            sem(n) for n in ("gates_done", "topped", "listed", "slots_turned", "slots_kept", "index_out"))

        block = ctx.enter_context(nc.Block())

        def groups(tile):
            return tile.rearrange("p (q e) -> p q e", e=E)

        def wide(small):
            return small.rearrange("p (q e) -> p q e", e=1).to_broadcast([P, Q, E])

        def over_rounds(eng, body):
            body(0)
            with eng.Fori(1, SINKHORN, 1) as i:
                body(i)

        @block.vector
        def _(dve):
            def body(i):
                for h in range(2):
                    n = 2 * i + h + 1
                    if isinstance(i, int):
                        for t in range(T):
                            ins = dve.tensor_reduce(over_e_max[h][:, HB * t:HB * t + HB],
                                                    logits[:, t, HB * h:HB * h + HB, :], AX, ALU.max)
                        ins.then_inc(e_max, 1)
                        dve.wait_ge(e_max, n)
                        for t in range(T):
                            ins = dve.tensor_tensor(
                                over_e[h][:, HB * t:HB * t + HB, :], logits[:, t, HB * h:HB * h + HB, :],
                                wide(over_e_max[h][:, :])[:, HB * t:HB * t + HB, :], ALU.subtract)
                        ins.then_inc(e_shift, 1)
                    else:
                        dve.wait_ge(in_e, n - 2)
                        src = groups(to_e_ps[h][:, 0:N])
                        dve.tensor_reduce(over_e_max[h][:, :], src, AX, ALU.max).then_inc(e_max, 1)
                        dve.wait_ge(e_max, n)
                        dve.tensor_tensor(over_e[h][:, :, :], src, wide(over_e_max[h][:, :]), ALU.subtract
                                          ).then_inc(e_shift, 1)
                for h in range(2):
                    n = 2 * i + h + 1
                    dve.wait_ge(e_exp, n)
                    dve.tensor_reduce(over_e_sum[h][:, :], over_e_exp[h][:, :, :], AX, ALU.add).then_inc(e_sum, 1)
                for h in range(2):
                    n = 2 * i + h + 1
                    dve.wait_ge(e_log, n)
                    dve.tensor_tensor(over_e_out[h][:, :, :], over_e[h][:, :, :], wide(over_e_log[h][:, :]),
                                      ALU.subtract).then_inc(e_done, 1)
                for h in range(2):
                    n = 2 * i + h + 1
                    dve.wait_ge(in_n, n)
                    dve.tensor_reduce(neg_max[h][:, :], to_n_ps[h][:, 0:N], AX, ALU.max, negate=True
                                      ).then_inc(n_max, 1)
                for h in range(2):
                    n = 2 * i + h + 1
                    dve.wait_ge(n_log, n)
                    dve.tensor_scalar(over_n[h][:, :], to_n_ps[h][:, 0:N], neg_max[h][:, 0:1], over_n_log[h][:, 0:1],
                                      ALU.add, ALU.subtract).then_inc(n_done, 1)

            over_rounds(dve, body)
            steps = 0
            dve.wait_ge(gates_done, 2)
            for r in range(CAP // 8):
                eight = slice(8 * r, 8 * r + 8)
                for h in range(2):
                    if r > 0:
                        dve.wait_ge(topped, steps - 1)
                    dve.max(top[h][:, eight], affinity[h][:, :]).then_inc(topped, 1)
                    steps += 1
                for h in range(2):
                    dve.wait_ge(topped, steps - 1 + h)
                    dve.max_index(top_at[h][:, eight], top[h][:, eight], affinity[h][:, :])
                    dve.match_replace(affinity[h][:, :], top[h][:, eight], affinity[h][:, :], -1.0
                                      ).then_inc(topped, 1)
                steps += 2
            dve.wait_ge(topped, steps)
            for h in range(2):
                dve.tensor_copy(at_twice[h][:, :, :], top_at[h][:, :].rearrange("p (a c) -> p a c", a=1)
                                .to_broadcast([P, 2, CAP])).then_inc(listed, 1)
                dve.tensor_copy(top_twice[h][:, :, :], top[h][:, :].rearrange("p (a c) -> p a c", a=1)
                                .to_broadcast([P, 2, CAP])).then_inc(listed, 1)
            for h in range(2):
                dve.wait_ge(slots_turned, h + 1)
                for k, table in enumerate((slot_index, slot_gate)):
                    for r in range(2):
                        half = slice(CAP * r, CAP * r + CAP)
                        ins = dve.tensor_copy(
                            table[half, :, HB // 2 * h:HB // 2 * (h + 1)].rearrange("p e j -> p j e"),
                            slot_ps[h][half, k * P:k * P + P].rearrange("p (j r e) -> p j r e", r=2, e=E)[:, :, r, :])
                ins.then_inc(slots_kept, 1)

        @block.scalar
        def _(act):
            def body(i):
                for h in range(2):
                    act.wait_ge(e_shift, 2 * i + h + 1)
                    act.activation(over_e_exp[h][:, :, :], over_e[h][:, :, :], ACT.Exp).then_inc(e_exp, 1)
                for h in range(2):
                    act.wait_ge(e_sum, 2 * i + h + 1)
                    act.activation(over_e_log[h][:, :], over_e_sum[h][:, :], ACT.Ln).then_inc(e_log, 1)
                for h in range(2):
                    n = 2 * i + h + 1
                    act.wait_ge(n_max, n)
                    act.activation(over_n_exp[h][:, :], to_n_ps[h][:, 0:N], ACT.Exp, bias=neg_max[h][:, :],
                                   accum_out=over_n_sum[h][:, :]).then_inc(n_exp, 1)
                    act.wait_ge(n_exp, n)
                    act.activation(over_n_log[h][:, :], over_n_sum[h][:, :], ACT.Ln).then_inc(n_log, 1)

            over_rounds(act, body)
            for h in range(2):
                act.wait_ge(n_done, 2 * SINKHORN - 1 + h)
                act.activation(affinity[h][:, :], over_n[h][:, :], ACT.Exp).then_inc(gates_done, 1)

        @block.tensor
        def _(pe):
            def body(i):
                for h in range(2):
                    pe.wait_ge(e_done, 2 * i + h + 1)
                    flat = over_e_out[h][:, :, :].rearrange("p q e -> p (q e)")
                    for t in range(T):
                        ins = pe.transpose(to_n_ps[h][:, t * P:t * P + P], flat[:, t * P:t * P + P], ident[:, :])
                    ins.then_inc(in_n, 1)
                for h in range(2):
                    pe.wait_ge(n_done, 2 * i + h + 1)
                    for t in range(T):
                        ins = pe.transpose(to_e_ps[h][:, t * P:t * P + P], over_n[h][:, t * P:t * P + P], ident[:, :])
                    ins.then_inc(in_e, 1)

            over_rounds(pe, body)
            for h in range(2):
                pe.wait_ge(listed, 2 * h + 2)
                for k, twice in enumerate((at_twice, top_twice)):
                    ins = pe.transpose(slot_ps[h][:, k * P:k * P + P],
                                       twice[h][:, :, :].rearrange("p a c -> p (a c)"), ident[:, :])
                ins.then_inc(slots_turned, 1)

        @block.sync
        def _(sp):
            for h in range(2):
                sp.wait_ge(listed, 2 * h + 1)
                sp.dma_start(dram["slot_index"][h * P:h * P + P, :], at_twice[h][:, 0, :]).then_inc(index_out, 16)
            sp.wait_ge(index_out, 32)
            sp.wait_ge(slots_kept, 2)



def gather(nc, dram, keep, arena):
    with ExitStack() as ctx:
        def sem(name):
            return ctx.enter_context(nc.semaphore(name))

        x2_all, expert_x = keep["x2_all"], keep["expert_x"]
        token_no = arena.take("token_no", [P, T])
        index_all = [arena.take(f"index_all{p}", [P, E * CAP]) for p in range(2)]
        pick = [arena.take(f"pick{p}", [P, T, E * CAP], F32R) for p in range(2)]
        x_hi = [arena.take(f"x_hi{p}", [P, T, D], F32R) for p in range(2)]
        x_lo = [arena.take(f"x_lo{p}", [P, T, D], F32R) for p in range(2)]
        out_ps = [ctx.enter_context(nc.psum_tensor(f"gather_ps{i}", [P, 512], F32)) for i in range(8)]
        EC = E * CAP // 512
        EB = E // EC

        numbered = sem("numbered")
        index_in = [sem(f"index_in{p}") for p in range(2)]
        picked, hi_done, lo_done, gathered = sem("picked"), sem("hi_done"), sem("lo_done"), sem("gathered")
        out_act, out_dve = sem("out_act"), sem("out_dve")

        block = ctx.enter_context(nc.Block())

        def early(b):
            return isinstance(b, int) and b < 2

        def over(eng, body):
            body(0, 0)
            body(1, 1)
            with eng.Fori(2, B - 1, 2) as i:
                body(i, 0)
                body(i + 1, 1)

        @block.gpsimd
        def _(pool):
            pool.iota(token_no[:, :], [[P, T]], base=0, channel_multiplier=1, allow_small_or_imprecise_dtypes=True
                      ).then_inc(numbered, 1)

        @block.sync
        def _(sp):
            def body(b, p):
                if not early(b):
                    sp.wait_ge(picked, b - 1)
                sp.dma_start(index_all[p][:, :], dram["slot_index"].rearrange("(b e) c -> b (e c)", e=E)
                             [bass.ds(b, 1), :].to_broadcast([P, E * CAP])).then_inc(index_in[p], 16)
            over(sp, body)

        @block.scalar
        def _(act):
            def body(b, p):
                if not early(b):
                    act.wait_ge(gathered, KD * EC * (b - 1))
                act.activation(x_hi[p][:, :, :], x2_all[:, bass.ds(T * b, T), :], ACT.Copy).then_inc(hi_done, 1)
                if not (isinstance(b, int) and b == 0):
                    copy_out(b - 1, 1 - p)

            def copy_out(b, p):
                for k in range(KD):
                    act.wait_ge(gathered, KD * EC * b + EC * k + 1)
                    act.activation(expert_x[:, 0:EB, bass.ds(b, 1), k, :].rearrange("p e b c -> p (e b) c"),
                                   out_ps[4 * p + EC * k][:, :].rearrange("p (e c) -> p e c", c=CAP), ACT.Copy
                                   ).then_inc(out_act, 1)

            over(act, body)
            copy_out(B - 1, 1)

        @block.vector
        def _(dve):
            dve.wait_ge(numbered, 1)

            def body(b, p):
                dve.wait_ge(index_in[p], 8 * b + 16 - 8 * p)
                if not early(b):
                    dve.wait_ge(gathered, KD * EC * (b - 1))
                for t in range(T):
                    ins = dve.tensor_scalar(pick[p][:, t, :], index_all[p][:, :], token_no[:, t:t + 1], None,
                                            ALU.is_equal)
                ins.then_inc(picked, 1)
                dve.wait_ge(hi_done, b + 1)
                dve.tensor_tensor(x_lo[p][:, :, :], x2_all[:, bass.ds(T * b, T), :], x_hi[p][:, :, :].bitcast(F32),
                                  ALU.subtract).then_inc(lo_done, 1)
                if not (isinstance(b, int) and b == 0):
                    copy_out(b - 1, 1 - p)

            def copy_out(b, p):
                for k in range(KD):
                    dve.wait_ge(gathered, KD * EC * b + EC * k + 2)
                    dve.tensor_copy(expert_x[:, EB:E, bass.ds(b, 1), k, :].rearrange("p e b c -> p (e b) c"),
                                    out_ps[4 * p + EC * k + 1][:, :].rearrange("p (e c) -> p e c", c=CAP)
                                    ).then_inc(out_dve, 1)

            over(dve, body)
            copy_out(B - 1, 1)

        @block.tensor
        def _(pe):
            def body(b, p):
                pe.wait_ge(picked, b + 1)
                pe.wait_ge(lo_done, b + 1)
                for k in range(KD):
                    for c, out in enumerate((out_act, out_dve)):
                        if not early(b):
                            pe.wait_ge(out, KD * (b - 2) + k + 1)
                        for n, (t, part) in enumerate((t, part) for t in range(T) for part in (x_hi, x_lo)):
                            ins = pe.matmul(out_ps[4 * p + EC * k + c][:, :], part[p][:, t, k * P:k * P + P],
                                            pick[p][:, t, c * 512:c * 512 + 512], start=(n == 0), stop=(n == 2 * T - 1))
                        ins.then_inc(gathered, 1)
            over(pe, body)



def experts(nc, dram, keep, arena):
    with ExitStack() as ctx:
        def sem(name):
            return ctx.enter_context(nc.semaphore(name))

        def bank(name):
            return ctx.enter_context(nc.psum_tensor(name, [P, 512], F32))

        expert_x, slot_gate = keep["expert_x"], keep["slot_gate"]
        expert_out = expert_x[:, :, :, :, :].rearrange("p e b k c -> p e (b k c)")
        HS = E * CAP // 2
        TS = HS // P
        HALF = KD * HS
        STEPS = 2 * M
        RING = 4
        w_in = [arena.take(f"w_in{i}", [P, 2 * D]) for i in range(RING)]
        w_hi = arena.take("w_hi", [P, M, 2 * D], F32R)
        w_lo = arena.take("w_lo", [P, M, 2 * D], F32R)
        x_hi = [arena.take(f"ex_hi{h}", [P, KD, HS], F32R) for h in range(2)]
        x_lo = [arena.take(f"ex_lo{h}", [P, KD, HS], F32R) for h in range(2)]
        hidden = [arena.take(f"hidden{i}", [P, HS]) for i in range(2)]
        h_hi = [arena.take(f"h_hi{i}", [P, HS], F32R) for i in range(4)]
        h_lo = [arena.take(f"h_lo{i}", [P, HS], F32R) for i in range(4)]
        b1 = arena.take("b1", [P, E * M])
        b2 = arena.take("b2", [P, D])
        b1_now = [arena.take(f"b1_now{h}", [P, M]) for h in range(2)]
        hidden_ps = [bank(f"hidden_ps{i}") for i in range(4)]
        out_ps = [[bank(f"out_ps{h}{i}") for i in range(2)] for h in range(2)]

        w_loaded = [sem(f"w_loaded{i}") for i in range(RING)]
        b1_in, b2_in, b1_ready = sem("b1_in"), sem("b2_in"), sem("b1_ready")
        w_hi_done, w_done = sem("w_hi_done"), sem("w_done")
        ex_hi_done, ex_done = sem("ex_hi_done"), sem("ex_done")
        hidden_done, gelu_done = sem("hidden_done"), sem("gelu_done")
        h_hi_done, h_done = sem("h_hi_done"), sem("h_done")
        out_added, biased, out_done = sem("out_added"), sem("biased"), sem("out_done")

        block = ctx.enter_context(nc.Block())

        def over(eng, body):
            body(0)
            with eng.Fori(1, E - 1, 1) as i:
                body(i)
            body(E - 1)

        def is0(e):
            return isinstance(e, int) and e == 0

        @block.sync
        def _(sp):
            sp.dma_start(b1[:, :], dram["b1"]).then_inc(b1_in, 16)

            def body(e):
                for m in range(M):
                    if not (is0(e) and m < RING):
                        sp.wait_ge(w_done, M * e + m + 1 - RING)
                    sp.dma_start(w_in[m % RING][:, 0:D].rearrange("p (k f) -> p k f", k=KD),
                                 dram["w1"][bass.ds(e * D, D), m * P:m * P + P].rearrange("(k p) f -> p k f", p=P)
                                 ).then_inc(w_loaded[m % RING], 16)
                    sp.dma_start(w_in[m % RING][:, D:2 * D], dram["w2"][bass.ds(e * FF + m * P, P), :]
                                 ).then_inc(w_loaded[m % RING], 16)
            over(sp, body)

        @block.gpsimd
        def _(pool):
            def body(e):
                for m in range(M):
                    pool.wait_ge(w_hi_done, M * e + m + 1)
                    pool.tensor_tensor(w_lo[:, m, :], w_in[m % RING][:, :], w_hi[:, m, :].bitcast(F32), ALU.subtract
                                       ).then_inc(w_done, 1)
            over(pool, body)

        @block.scalar
        def _(act):
            def split_w_hi(e, m):
                act.wait_ge(w_loaded[m % RING], 32 * (M // RING) * e + 32 * (m // RING + 1))
                if not is0(e):
                    act.wait_ge(out_added, STEPS * (e - 1) + M + m + 1)
                act.activation(w_hi[:, m, :], w_in[m % RING][:, :], ACT.Copy).then_inc(w_hi_done, 1)

            for m in range(M):
                split_w_hi(0, m)

            def body(e):
                for k in range(STEPS):
                    if k < 3 and not is0(e):
                        split_w_hi(e, M - 3 + k)
                    if k >= M + 3 and not (isinstance(e, int) and e == E - 1):
                        split_w_hi(e + 1, k - M - 3)
                    if k % M == 0:
                        act.wait_ge(b1_ready, 2 * e + k // M + 1)
                    act.wait_ge(hidden_done, STEPS * e + k + 1)
                    if not (is0(e) and k < 2):
                        act.wait_ge(h_done, STEPS * e + k - 1)
                    act.activation(hidden[k % 2][:, :], hidden_ps[k % 4][:, :], ACT.Gelu_apprx_tanh,
                                   bias=b1_now[k // M][:, k % M:k % M + 1]).then_inc(gelu_done, 1)
                    if k == 3:
                        if not is0(e):
                            act.wait_ge(out_done, 2 * e)
                        act.dma_start(b2[:, :], dram["b2"][bass.ds(e, 1), :].to_broadcast([P, D])
                                      ).then_inc(b2_in, 16)
            over(act, body)

        @block.vector
        def _(dve):
            def tokens(tile):
                return tile[:, :, :].rearrange("p k (b c) -> p k b c", c=CAP)

            def split_x_hi(e, h):
                src = expert_out[:, bass.ds(e, 1), h * HALF:(h + 1) * HALF].rearrange(
                    "p a (b k c) -> p (a k) b c", k=KD, c=CAP)
                dve.tensor_copy(tokens(x_hi[h]), src).then_inc(ex_hi_done, 1)

            def split_x_lo(e, h):
                src = expert_out[:, bass.ds(e, 1), h * HALF:(h + 1) * HALF].rearrange(
                    "p a (b k c) -> p (a k) b c", k=KD, c=CAP)
                dve.wait_ge(ex_hi_done, 2 * e + h + 1)
                dve.tensor_tensor(tokens(x_lo[h]), src, tokens(x_hi[h]).bitcast(F32), ALU.subtract
                                  ).then_inc(ex_done, 1)

            def split_hidden(e, k):
                q = STEPS * e + k
                dve.wait_ge(gelu_done, q + 1)
                if not (is0(e) and k < 4):
                    dve.wait_ge(out_added, q - 3)
                dve.tensor_copy(h_hi[k % 4][:, :], hidden[k % 2][:, :]).then_inc(h_hi_done, 1)
                dve.wait_ge(h_hi_done, q + 1)
                dve.tensor_tensor(h_lo[k % 4][:, :], hidden[k % 2][:, :], h_hi[k % 4][:, :].bitcast(F32), ALU.subtract
                                  ).then_inc(h_done, 1)

            def finish(e, h):
                dve.wait_ge(out_added, STEPS * e + M * h + M)
                dve.wait_ge(b2_in, 16 * e + 16)
                for i in range(2):
                    at = h * HALF + i * 512
                    dve.tensor_tensor(
                        expert_out[:, bass.ds(e, 1), at:at + 512].rearrange("p a (t d) -> p (a t) d", d=D),
                        out_ps[h][i][:, :].rearrange("p (t d) -> p t d", d=D),
                        b2[:, :].rearrange("p (t d) -> p t d", t=1).to_broadcast([P, 2, D]), ALU.add
                    ).then_inc(biased, 1)
                dve.wait_ge(biased, 4 * e + 2 * h + 2)
                for t in range(TS):
                    at = h * HALF + t * D
                    tile = expert_out[:, bass.ds(e, 1), at:at + D].rearrange("p a d -> p (a d)")
                    ins = dve.tensor_scalar(tile, tile, slot_gate[:, bass.ds(e, 1), TS * h + t], None, ALU.mult)
                ins.then_inc(out_done, 1)

            def take_b1(e, h):
                dve.tensor_copy(b1_now[h][:, :], b1[:, bass.ds(e * M, M)]).then_inc(b1_ready, 1)

            dve.wait_ge(b1_in, 16)
            take_b1(0, 0)
            split_x_hi(0, 0)
            split_x_lo(0, 0)

            def body(e):
                for k in range(STEPS):
                    split_hidden(e, k)
                    if k == 1 and not is0(e):
                        finish(e - 1, 1)
                    if k == M + 1:
                        finish(e, 0)
                    if k == 3:
                        if not is0(e):
                            dve.wait_ge(hidden_done, STEPS * e)
                        split_x_hi(e, 1)
                    if k == 2:
                        take_b1(e, 1)
                    if k == 4:
                        split_x_lo(e, 1)
                    if not (isinstance(e, int) and e == E - 1):
                        if k == M + 2:
                            take_b1(e + 1, 0)
                        if k == M + 3:
                            dve.wait_ge(hidden_done, STEPS * e + M)
                            split_x_hi(e + 1, 0)
                        if k == M + 4:
                            split_x_lo(e + 1, 0)
            over(dve, body)
            finish(E - 1, 1)

        @block.tensor
        def _(pe):
            def hidden_step(e, k):
                q, h, m = STEPS * e + k, k // M, k % M
                if h == 0:
                    pe.wait_ge(w_done, M * e + m + 1)
                if m == 0:
                    pe.wait_ge(ex_done, 2 * e + h + 1)
                if not (is0(e) and k < 4):
                    pe.wait_ge(gelu_done, q - 3)
                for n, (d, w, x) in enumerate((d, w, x) for d in range(KD)
                                              for w, x in ((w_hi, x_hi), (w_hi, x_lo), (w_lo, x_hi))):
                    ins = pe.matmul(hidden_ps[k % 4][:, :], w[:, m, d * P:d * P + P], x[h][:, d, :],
                                    start=(n == 0), stop=(n == 3 * KD - 1))
                ins.then_inc(hidden_done, 1)

            def out_step(e, k):
                q, h, m = STEPS * e + k, k // M, k % M
                pe.wait_ge(h_done, q + 1)
                if m == 0 and not is0(e):
                    pe.wait_ge(out_done, 2 * e + h - 1)
                for t in range(TS):
                    for n, (x, w) in enumerate(((h_hi, w_hi), (h_hi, w_lo), (h_lo, w_hi))):
                        ins = pe.matmul(out_ps[h][t // 2][:, (t % 2) * D:(t % 2) * D + D],
                                        x[k % 4][:, t * P:t * P + P], w[:, m, D:2 * D],
                                        start=(m == 0 and n == 0 and t % 2 == 0), stop=(m == M - 1 and n == 2),
                                        skip_group_check=True)
                ins.then_inc(out_added, 1)

            def body(e):
                for k in range(STEPS):
                    hidden_step(e, k)
                    if k >= 2:
                        out_step(e, k - 2)
                    elif not is0(e):
                        out_step(e - 1, STEPS + k - 2)
            over(pe, body)
            out_step(E - 1, STEPS - 2)
            out_step(E - 1, STEPS - 1)



def scatter(nc, dram, keep, arena):
    with ExitStack() as ctx:
        def sem(name):
            return ctx.enter_context(nc.semaphore(name))

        expert_out = keep["expert_x"][:, :, :, :, :].rearrange("p e b k c -> p e (b k c)")
        slot_index, tanh_f = keep["slot_index"], keep["tanh_f"]
        EH = E // 2
        column_no = arena.take("column_no", [P, N])
        out_hi = [arena.take(f"out_hi{v}", [P, EH, D], F32R) for v in range(2)]
        out_lo = [arena.take(f"out_lo{v}", [P, EH, D], F32R) for v in range(2)]
        place = [arena.take(f"place{v}", [P, EH, N], F32R) for v in range(2)]
        x1 = [arena.take(f"x1_back{p}", [P, 2 * T, D]) for p in range(2)]
        sum_ps = [[ctx.enter_context(nc.psum_tensor(f"sum_ps{p}{i}", [P, 512], F32)) for i in range(2 * T)]
                  for p in range(2)]

        numbered, split_hi, split_done, placed, summed, out_ready = (
            sem(n) for n in ("columns_numbered", "split_hi", "split_done", "placed", "summed", "out_ready"))
        x1_in = [sem(f"x1_in{p}") for p in range(2)]
        stored = [sem(f"stored{p}") for p in range(2)]

        block = ctx.enter_context(nc.Block())
        PAIRS = B // 2

        def over(eng, body):
            body(0, 0)
            with eng.Fori(1, PAIRS - 1, 2) as i:
                body(i, 1)
                body(i + 1, 0)
            body(PAIRS - 1, 1)

        def is0(j):
            return isinstance(j, int) and j == 0

        @block.gpsimd
        def _(pool):
            pool.iota(column_no[:, :], [[1, N]], base=0, channel_multiplier=0, allow_small_or_imprecise_dtypes=True
                      ).then_inc(numbered, 1)

        @block.sync
        def _(sp):
            def load(j, p, wait):
                if wait:
                    sp.wait_ge(stored[p], 8 * j - 8 * p)
                sp.dma_start(x1[p][:, :, :].rearrange("p (r t) d -> p r (t d)", r=2),
                             dram["x1"][bass.ds(2 * j * P, 2 * P), :].rearrange("(r p) n -> p r n", p=P)
                             ).then_inc(x1_in[p], 16)

            def store(j, p):
                sp.wait_ge(out_ready, j + 1)
                sp.dma_start(dram["out"][bass.ds(2 * j * N, 2 * N), :].rearrange("(r p) d -> p r d", p=P),
                             x1[p][:, :, :]).then_inc(stored[p], 16)

            load(0, 0, False)
            load(1, 1, False)
            store(0, 0)
            with sp.Fori(2, PAIRS - 1, 2) as i:
                load(i, 0, True)
                store(i - 1, 1)
                load(i + 1, 1, True)
                store(i, 0)
            store(PAIRS - 1, 1)
            for p in range(2):
                sp.wait_ge(stored[p], 16 * PAIRS // 2)

        def half(j, v):
            return expert_out[:, EH * v:EH * v + EH, bass.ds(j * D, D)]

        @block.scalar
        def _(act):
            def body(j, p):
                for v in range(2):
                    if not is0(j):
                        act.wait_ge(summed, 2 * j + v - 1)
                    act.activation(out_hi[v][:, :, :], half(j, v), ACT.Copy).then_inc(split_hi, 1)
            over(act, body)

        @block.vector
        def _(dve):
            dve.wait_ge(numbered, 1)

            def split(j, v):
                if not is0(j):
                    dve.wait_ge(summed, 2 * j + v - 1)
                for e in range(EH):
                    ins = dve.tensor_scalar(place[v][:, e, :], column_no[:, :],
                                            slot_index[:, EH * v + e, bass.ds(j, 1)], None, ALU.is_equal)
                ins.then_inc(placed, 1)
                dve.wait_ge(split_hi, 2 * j + v + 1)
                dve.tensor_tensor(out_lo[v][:, :, :], half(j, v), out_hi[v][:, :, :].bitcast(F32), ALU.subtract
                                  ).then_inc(split_done, 1)

            def finish(j, p):
                dve.wait_ge(summed, 2 * j + 2)
                dve.wait_ge(x1_in[p], 8 * j + 16 - 8 * p)
                for i in range(2 * T):
                    ins = dve.scalar_tensor_tensor(x1[p][:, i, :], sum_ps[p][i][:, 0:D], tanh_f[:, 0:1], x1[p][:, i, :],
                                                   ALU.mult, ALU.add)
                ins.then_inc(out_ready, 1)

            def body(j, p):
                split(j, 0)
                if not is0(j):
                    finish(j - 1, 1 - p)
                split(j, 1)
            over(dve, body)
            finish(PAIRS - 1, 1)

        @block.tensor
        def _(pe):
            def body(j, p):
                for v in range(2):
                    pe.wait_ge(placed, 2 * j + v + 1)
                    pe.wait_ge(split_done, 2 * j + v + 1)
                    if v == 0 and not (isinstance(j, int) and j < 2):
                        pe.wait_ge(out_ready, j - 1)
                    for e in range(EH):
                        for n, part in enumerate((out_hi, out_lo)):
                            for t in range(T):
                                for r in range(2):
                                    rows = slice(CAP * r, CAP * r + CAP)
                                    ins = pe.matmul(sum_ps[p][T * r + t][:, 0:D], place[v][rows, e, t * P:t * P + P],
                                                    part[v][rows, e, :], start=(v == 0 and e == 0 and n == 0),
                                                    stop=(v == 1 and e == EH - 1 and n == 1))
                    ins.then_inc(summed, 1)
            over(pe, body)


def flamingo_layer(nc, dram):
    start = nc.sbuf_base + -nc.sbuf_base % 32
    end = nc.sbuf_usable_end
    tables = Arena(nc, start, end)
    keep = {
        "ident": tables.take("ident", [P, P]),
        "slot_index": tables.take("slot_index_sb", [P, E, B // 2]),
        "slot_gate": tables.take("slot_gate", [P, E, B // 2]),
        "tanh_f": tables.take("tanh_f", [P, 1]),
        "spare_dve": tables.take("spare_dve", [P, 1]),
    }
    middle = tables.at
    keep["expert_x"] = tables.take("expert_x", [P, E, B, KD, CAP])
    rest = tables.at
    phase3 = Arena(nc, rest, end)
    keep["x2_all"] = phase3.take("x2_all", [P, B * T, D])
    keep["logits"] = phase3.take("logits", [P, T, B, E])
    attention(nc, dram, keep, Arena(nc, middle, rest))
    route(nc, dram, keep, Arena(nc, middle, rest))
    gather(nc, dram, keep, phase3)
    experts(nc, dram, keep, Arena(nc, rest, end))
    scatter(nc, dram, keep, Arena(nc, rest, end))


def kernel(**inputs):
    import concourse.bacc as bacc
    from concourse.bass_utils import run_bass_kernel_spmd

    def a(name):
        return np.asarray(inputs[name])

    arrays = {
        "x": a("x").reshape(B * N, D),
        "ctx": a("ctx_1024").reshape(B * KC, D),
        "g_xattn": a("g_xattn").reshape(1),
        "g_ffn": a("g_ffn").reshape(1),
        "fm_wT": a("L0_xattn_fm_w").T,
        "fm_b": a("L0_xattn_fm_b").reshape(HD, 1),
        "fc_wT": a("L0_xattn_fc_w").T,
        "fc_b": a("L0_xattn_fc_b"),
        "gate_queryT": a("L0_ffn_gate_query").T,
        "log_temp": a("L0_ffn_log_temp").reshape(1),
        "w1": a("L0_ffn_w1").reshape(E * D, FF),
        "b1": a("L0_ffn_b1").reshape(E * M, P).T,
        "w2": a("L0_ffn_w2").reshape(E * FF, D),
        "b2": a("L0_ffn_b2"),
    }
    arrays = {f"in_{n}": np.ascontiguousarray(v) for n, v in arrays.items()}
    nc = bacc.Bacc("TRN2", target_bir_lowering=False, num_devices=1)
    dram = {n[3:]: nc.dram_tensor(n, v.shape, mybir.dt.from_np(v.dtype), kind="ExternalInput").ap()
            for n, v in arrays.items()}
    dram["x1"] = nc.dram_tensor("x1_scratch", (B * P, T * D), F32, kind="Internal").ap()
    dram["slot_index"] = nc.dram_tensor("slot_index_scratch", (B * E, CAP), F32, kind="Internal").ap()
    dram["out"] = nc.dram_tensor("out_x", (B * N, D), F32, kind="ExternalOutput").ap()
    flamingo_layer(nc, dram)
    result = run_bass_kernel_spmd(nc, [arrays], core_ids=[0])
    return result.results[0]["out_x"].reshape(B, N, D)
```

```python
from contextlib import ExitStack

import numpy as np

import concourse.bass as bass
from concourse import mybir

F32 = mybir.dt.float32
F32R = mybir.dt.float32r
I32 = mybir.dt.int32
U32 = mybir.dt.uint32
ALU = mybir.AluOpType
ACT = mybir.ActivationFunctionType
AX = mybir.AxisListType.X

P = 128
B, N, D = 16, 256, 256
KC = 120
HEADS, HD = 16, 16
EXP = 2 * HD
HG = P // EXP
G = HEADS // HG
T = N // P
KD = D // P
UNITS = T * G
E, FF = 16, 1024
M = FF // P
CAP = int(512 * 2.0 / E)
HB = 8
SINKHORN = 6
EPS = 1e-5
SCALE = 1.0 / 16.0


class Arena:

    def __init__(self, nc, start, end):
        self.nc, self.at, self.end = nc, start, end

    def take(self, name, shape, dt=F32):
        size = 4 * int(np.prod(shape[1:]))
        size += -size % 32
        assert self.at + size <= self.end, (name, self.at + size, self.end)
        tensor = self.nc.alloc_sbuf_tensor_at(name, shape, dt, offset=self.at)
        self.at += size
        return tensor



A_STEPS = [(0, "cT", 0, 1), (2, "oT", 1, -1), (2, "xnT", 0, 1), (3, "z", 0, 1), (3, "x2T", 0, -1), (4, "z", 1, 1),
           (5, "z", 2, 1), (6, "x2T", 1, -1), (6, "z", 3, 1), (7, "oT", 0, 0)]
B_STEPS = [(0, "fc", 0, -1), (3, "fc", 1, -1), (4, "logits", 0, -1), (6, "logits", 1, -1), (7, "v", 0, 1)]
A_PROLOGUE = [("cT", 0), ("xnT", 0), ("z", 0), ("z", 1), ("z", 2), ("z", 3)]
B_PROLOGUE = [("v", 0)]


def kept(steps, home):
    if not isinstance(home, int):
        return steps
    return [s for s in steps if 0 <= home + s[3] < B and (home < B or s[3] < 0)]


def in_slot(steps, home, slot):
    return [s[1:] for s in kept(steps, home) if s[0] == slot]


def uses_before(steps, prologue, step, part, b):
    offset = next(s[3] for s in steps if s[1:3] == (step, part))
    home = b - offset
    if isinstance(home, int) and home < 0:
        return prologue.index((step, part))
    before = len(prologue)
    if isinstance(home, int):
        before += sum(len(kept(steps, h)) for h in range(home))
    else:
        before += len(kept(steps, 0)) + len(steps) * (home - 1)
    return before + [s[1:3] for s in kept(steps, home)].index((step, part))


def use_a(step, part, b):
    return uses_before(A_STEPS, A_PROLOGUE, step, part, b)


def use_b(step, part, b):
    return uses_before(B_STEPS, B_PROLOGUE, step, part, b)


def over_batches(eng, body):
    body(0, 0)
    body(1, 1)
    with eng.Fori(2, B - 2, 2) as i:
        body(i, 0)
        body(i + 1, 1)
    body(B - 2, 0)
    body(B - 1, 1)


def attention(nc, dram, keep, arena):
    with ExitStack() as ctx:
        sb = arena.take

        def ps(name):
            return ctx.enter_context(nc.psum_tensor(name, [P, 512], F32))

        def sem(name):
            return ctx.enter_context(nc.semaphore(name))

        ident, x2_all, logits = keep["ident"], keep["x2_all"], keep["logits"]

        block_w = sb("block_w", [P, 2, P])
        sign = sb("sign", [P, 1])
        sign_bits = sb("sign_bits", [P, 1], I32)
        bias_b = sb("bias_b", [P, 1])
        sign_bias = sb("sign_bias", [P, 1])
        head_mask = sb("head_mask", [P, HG])
        fc_w = sb("fc_w", [P, G, D])
        fc_bias = sb("fc_bias", [P, D])
        gate_in = sb("gate_in", [P, 2])
        tanh_x = sb("tanh_x", [P, 1])
        log_temp = sb("log_temp", [P, 1])
        inv_temp = sb("inv_temp", [P, 1])
        router_w = sb("router_w", [P, KD, E])
        neg_half = sb("neg_half", [P, T])
        eps = sb("eps", [P, T])
        x_in = [sb(f"x_in{p}", [P, T, D]) for p in range(2)]
        ctx_in = [sb(f"ctx_in{p}", [KC, D]) for p in range(2)]
        x_bias = [sb(f"x_bias{p}", [P, T, D]) for p in range(2)]
        feat = [sb(f"feat{p}", [P, G, N + KC]) for p in range(2)]
        k_block = [sb(f"k_block{p}", [P, G, HG * KC]) for p in range(2)]
        v_one = [sb(f"v_one{p}", [KC, HEADS, EXP + 1]) for p in range(2)]
        x1_out = [sb(f"x1_out{p}", [P, T, D]) for p in range(2)]
        stat1 = sb("stat1", [P, T, 6])
        mean_var1 = sb("mean_var1", [P, T, 2])
        var_eps1 = sb("var_eps1", [P, T])
        rstd1 = sb("rstd1", [P, T])
        xn = sb("xn", [P, T, D])
        xnT = sb("xnT", [P, KD, N])
        cT = sb("cT", [P, KD, KC])
        row_max = [sb(f"row_max{i}", [P, HG]) for i in range(2)]
        prob = [sb(f"prob{i}", [P, HG * KC]) for i in range(4)]
        probT = [sb(f"probT{i}", [KC, HG * P]) for i in range(2)]
        recip = [sb(f"recip{i}", [P, HG]) for i in range(2)]
        attn = [sb(f"attn{t}", [P, G * P]) for t in range(T)]
        attnT = sb("attnT", [P, G * P])
        stat2 = sb("stat2", [P, 6])
        mean_var2 = [sb(f"mean_var2{t}", [P, 2]) for t in range(T)]
        var_eps2 = sb("var_eps2", [P, 1])
        rstd2 = [sb(f"rstd2{t}", [P, 1]) for t in range(T)]
        x2 = [sb(f"x2{t}", [P, D]) for t in range(T)]
        x2T = sb("x2T", [P, KD * P])

        score_ps = [ps(f"score_ps{i}") for i in range(2)]
        probT_ps = [ps(f"probT_ps{i}") for i in range(2)]
        value_ps = [ps(f"value_ps{i}") for i in range(2)]
        bank_a = ps("bank_a")
        bank_b = ps("bank_b")

        weights_in = sem("weights_in")
        zeroed = sem("zeroed")
        blocks_in = sem("blocks_in")
        made = sem("made")
        masks_made = sem("masks_made")
        dve_const = sem("dve_const")
        act_const = sem("act_const")
        x_loaded = [sem(f"x_loaded{p}") for p in range(2)]
        x1_stored = [sem(f"x1_stored{p}") for p in range(2)]
        stats1_raw, stats1_done = sem("stats1_raw"), sem("stats1_done")
        var1_done, rstd1_done, xn_done = sem("var1_done"), sem("rstd1_done"), sem("xn_done")
        x_bias_done = sem("x_bias_done")
        k_block_done = sem("k_block_done")
        a_filled, a_emptied = sem("a_filled"), sem("a_emptied")
        b_filled, b_emptied = sem("b_filled"), sem("b_emptied")
        scored, max_done, shifted, exp_done = sem("scored"), sem("max_done"), sem("shifted"), sem("exp_done")
        turned, turned_out = sem("turned"), sem("turned_out")
        valued, recip_done, normed = sem("valued"), sem("recip_done"), sem("normed")
        x1_done, stats2_raw, stats2_done = sem("x1_done"), sem("stats2_raw"), sem("stats2_done")
        var2_done, rstd2_done, x2_done, x2_kept = sem("var2_done"), sem("rstd2_done"), sem("x2_done"), sem("x2_kept")

        block = ctx.enter_context(nc.Block())

        @block.sync
        def _(sp):
            def load(b, p):
                if not (isinstance(b, int) and b < 2):
                    sp.wait_ge(xn_done, b - 1)
                    sp.wait_ge(x_bias_done, b - 1)
                    sp.wait_ge(a_filled, use_a("cT", 0, b - 2) + 1)
                sp.dma_start(x_in[p][:, :, :], dram["x"][bass.ds(b * N, N), :].rearrange("(t p) d -> p t d", p=P)
                             ).then_inc(x_loaded[p], 16)
                sp.dma_start(ctx_in[p][:, :], dram["ctx"][bass.ds(b * KC, KC), :]).then_inc(x_loaded[p], 16)

            def store(b, p):
                sp.wait_ge(x1_done, T * b + T)
                sp.dma_start(dram["x1"][bass.ds(b * P, P), :], x1_out[p][:, :, :].rearrange("p t d -> p (t d)")
                             ).then_inc(x1_stored[p], 16)

            load(0, 0)
            sp.wait_ge(zeroed, 1)
            for j in range(2 * HG):
                sp.dma_start(block_w[HD * j:HD * j + HD, j // HG, EXP * (j % HG):EXP * (j % HG) + EXP]
                             .rearrange("d (s e) -> d s e", s=2),
                             dram["fm_wT"].rearrange("d (s e) -> d s e", s=1).to_broadcast([HD, 2, HD])
                             ).then_inc(blocks_in, 16)
                sp.dma_start(bias_b[HD * j:HD * j + HD, :], dram["fm_b"]).then_inc(blocks_in, 16)
            load(1, 1)
            sp.dma_start(gate_in[:, 0:1], dram["g_xattn"].partition_broadcast(P)).then_inc(weights_in, 16)
            sp.dma_start(gate_in[:, 1:2], dram["g_ffn"].partition_broadcast(P)).then_inc(weights_in, 16)
            sp.dma_start(log_temp[:, :], dram["log_temp"].partition_broadcast(P)).then_inc(weights_in, 16)
            sp.dma_start(fc_bias[:, :], dram["fc_b"].partition_broadcast(P)).then_inc(weights_in, 16)
            sp.dma_start(fc_w[:, :, :], dram["fc_wT"].rearrange("(g p) d -> p g d", p=P)).then_inc(weights_in, 16)
            sp.dma_start(router_w[:, :, :], dram["gate_queryT"].rearrange("(k p) e -> p k e", p=P)
                         ).then_inc(weights_in, 16)
            load(2, 0)
            load(3, 1)
            store(0, 0)
            with sp.Fori(2, B - 3, 2) as i:
                load(i + 2, 0)
                store(i - 1, 1)
                load(i + 3, 1)
                store(i, 0)
            for b in range(B - 3, B):
                store(b, b % 2)
            for p in range(2):
                sp.wait_ge(x1_stored[p], 16 * B // 2)

        @block.gpsimd
        def _(pool):
            pool.memset(block_w[:, :, :], 0.0).then_inc(zeroed, 1)
            pool.memset(ident[:, :], 0.0).then_inc(zeroed, 1)
            pool.wait_ge(zeroed, 2)
            pool.affine_select(out=ident[:, :], in_=ident[:, :], compare_op=ALU.not_equal, fill=1.0, base=0,
                               pattern=[[-1, P]], channel_multiplier=1).then_inc(made, 1)
            pool.iota(sign_bits[:, :], [[0, 1]], base=0, channel_multiplier=1).then_inc(made, 1)
            pool.memset(eps[:, :], EPS).then_inc(zeroed, 1)
            pool.memset(neg_half[:, :], -0.5).then_inc(made, 1)
            pool.wait_ge(made, 3)
            pool.wait_ge(zeroed, 3)

            def inv_std1(b):
                pool.wait_ge(stats1_done, b + 1)
                pool.tensor_tensor(var_eps1[:, :], mean_var1[:, :, 1], eps[:, 0:T], ALU.add).then_inc(var1_done, 1)
                pool.wait_ge(var1_done, b + 1)
                pool.tensor_tensor(rstd1[:, :], var_eps1[:, :], neg_half[:, 0:T], ALU.pow).then_inc(rstd1_done, 1)

            def inv_std2(b, t):
                n = T * b + t + 1
                pool.wait_ge(stats2_done, n)
                pool.tensor_tensor(var_eps2[:, :], mean_var2[t][:, 1:2], eps[:, 0:1], ALU.add).then_inc(var2_done, 1)
                pool.wait_ge(var2_done, n)
                pool.tensor_tensor(rstd2[t][:, :], var_eps2[:, :], neg_half[:, 0:1], ALU.pow).then_inc(rstd2_done, 1)

            def add_bias(b, p):
                pool.wait_ge(x_loaded[p], 16 * b + 32 - 16 * p)
                if not (isinstance(b, int) and b < 2):
                    pool.wait_ge(x1_done, T * (b - 1))
                for t in range(T):
                    ins = pool.tensor_tensor(x_bias[p][:, t, :], x_in[p][:, t, :], fc_bias[:, :], ALU.add)
                ins.then_inc(x_bias_done, 1)

            def block_keys(b, p, g):
                pool.wait_ge(a_emptied, use_a("z", g, b) + 1)
                if not (isinstance(b, int) and b < 2):
                    pool.wait_ge(scored, UNITS * (b - 1))
                pool.tensor_tensor(
                    k_block[p][:, g, :].rearrange("p (h k) -> p h k", h=HG),
                    feat[p][:, g, N:].rearrange("p (h k) -> p h k", h=1).to_broadcast([P, HG, KC]),
                    head_mask[:, :].rearrange("p (h k) -> p h k", k=1).to_broadcast([P, HG, KC]),
                    ALU.mult).then_inc(k_block_done, 1)

            def keep_x2(b, t):
                pool.wait_ge(x2_done, T * b + t + 1)
                pool.tensor_copy(x2_all[:, bass.ds(T * b + t, 1), :], x2[t][:, :].rearrange("p (a d) -> p a d", a=1)
                                 ).then_inc(x2_kept, 1)

            inv_std1(0)
            pool.wait_ge(dve_const, 3)
            add_bias(0, 0)
            for g in range(G):
                block_keys(0, 0, g)

            def batch(b, p):
                first, last = isinstance(b, int) and b == 0, isinstance(b, int) and b == B - 1
                if not last:
                    inv_std1(b + 1)
                if not first:
                    inv_std2(b - 1, 0)
                    keep_x2(b - 1, 0)
                if not last:
                    for g in range(2):
                        block_keys(b + 1, 1 - p, g)
                if not first:
                    inv_std2(b - 1, 1)
                if not last:
                    block_keys(b + 1, 1 - p, 2)
                if not first:
                    keep_x2(b - 1, 1)
                if not last:
                    block_keys(b + 1, 1 - p, 3)
                    add_bias(b + 1, 1 - p)

            over_batches(pool, batch)
            for t in range(T):
                inv_std2(B - 1, t)
                keep_x2(B - 1, t)

        @block.scalar
        def _(act):
            act.wait_ge(weights_in, 6 * 16)
            act.activation(tanh_x[:, :], gate_in[:, 0:1], ACT.Tanh).then_inc(act_const, 1)
            act.activation(keep["tanh_f"][:, :], gate_in[:, 1:2], ACT.Tanh)
            act.preload_act_table_set("natural_log_exp_and_others")
            act.activation(inv_temp[:, :], log_temp[:, :], ACT.Exp, scale=-1.0).then_inc(act_const, 1)
            act.wait_ge(dve_const, 2)

            def exponent(s, b):
                u = UNITS * b + s
                act.wait_ge(shifted, u + 1)
                act.activation(prob[s % 4][:, :], prob[s % 4][:, :], ACT.Exp, scale=SCALE).then_inc(exp_done, 1)

            def copy_turned(s, b):
                u = UNITS * b + s
                act.wait_ge(turned, u + 1)
                if not (isinstance(b, int) and u < 2):
                    act.wait_ge(valued, u - 1)
                act.activation(probT[s % 2][:, :], probT_ps[s % 2][0:KC, :], ACT.Copy).then_inc(turned_out, 1)

            def empty_a(step, part, b, q):
                act.wait_ge(a_filled, use_a(step, part, b) + 1)
                if step == "cT":
                    ins = act.activation(cT[:, :, :].rearrange("p k c -> p (k c)"), bank_a[:, 0:KD * KC], ACT.Copy)
                elif step == "xnT":
                    ins = act.activation(xnT[:, :, :].rearrange("p k c -> p (k c)"), bank_a[:, :], ACT.Copy)
                elif step == "z":
                    ins = act.activation(feat[q][:, part, :], bank_a[:, 0:N + KC], ACT.Exp,
                                         bias=sign_bias[:, :], scale=sign[:, :])
                elif step == "oT":
                    ins = act.activation(attnT[:, :], bank_a[:, :], ACT.Copy)
                else:
                    ins = act.activation(x2T[:, :], bank_a[:, 0:KD * P], ACT.Copy)
                ins.then_inc(a_emptied, 1)

            for step, part in A_PROLOGUE:
                empty_a(step, part, 0, 0)
            exponent(0, 0)

            def batch(b, p):
                for s in range(UNITS):
                    steps = in_slot(A_STEPS, b, s)
                    for step, part, offset in steps[:1]:
                        empty_a(step, part, b + offset, (p + offset) % 2)
                    if s < UNITS - 1:
                        exponent(s + 1, b)
                    elif not (isinstance(b, int) and b == B - 1):
                        exponent(0, b + 1)
                    copy_turned(s, b)
                    for step, part, offset in steps[1:]:
                        empty_a(step, part, b + offset, (p + offset) % 2)

            over_batches(act, batch)
            for _, step, part, _ in kept(A_STEPS, B):
                empty_a(step, part, B - 1, 1)

        @block.tensor
        def _(pe):
            def scores(s, b, p):
                u, g, t = UNITS * b + s, s % G, s // G
                if not (isinstance(b, int) and u < 2):
                    pe.wait_ge(shifted, u - 1)
                if t == 0:
                    pe.wait_ge(k_block_done, G * b + g + 1)
                pe.matmul(score_ps[s % 2][:, 0:HG * KC], feat[p][:, g, t * P:t * P + P], k_block[p][:, g, :],
                          start=True, stop=True).then_inc(scored, 1)

            def turn(s, b):
                u = UNITS * b + s
                pe.wait_ge(exp_done, u + 1)
                if not (isinstance(b, int) and u < 2):
                    pe.wait_ge(turned_out, u - 1)
                for h in range(HG):
                    ins = pe.transpose(probT_ps[s % 2][0:KC, h * P:h * P + P],
                                       prob[s % 4][:, h * KC:h * KC + KC], ident[:, :])
                ins.then_inc(turned, 1)

            def values(s, b, p):
                u, g = UNITS * b + s, s % G
                pe.wait_ge(turned_out, u + 1)
                if not (isinstance(b, int) and u < 2):
                    pe.wait_ge(normed, u - 1)
                if s == 0:
                    pe.wait_ge(b_emptied, use_b("v", 0, b) + 1)
                for h in range(HG):
                    ins = pe.matmul(value_ps[s % 2][:, h * (EXP + 1):(h + 1) * (EXP + 1)],
                                    probT[s % 2][:, h * P:h * P + P], v_one[p][:, HG * g + h, :],
                                    start=True, stop=True)
                ins.then_inc(valued, 1)

            def fill_a(step, part, b, q):
                n = use_a(step, part, b)
                if not (isinstance(n, int) and n == 0):
                    pe.wait_ge(a_emptied, n)
                if step == "cT":
                    pe.wait_ge(x_loaded[q], 16 * b + 32 - 16 * q)
                    for k in range(KD):
                        ins = pe.transpose(bank_a[:, k * KC:k * KC + KC], ctx_in[q][:, k * P:k * P + P],
                                           ident[0:KC, 0:KC])
                elif step == "xnT":
                    pe.wait_ge(xn_done, b + 1)
                    for k in range(KD):
                        for t in range(T):
                            ins = pe.transpose(bank_a[:, k * N + t * P:k * N + t * P + P],
                                               xn[:, t, k * P:k * P + P], ident[:, :])
                elif step == "z":
                    k, w = part // 2, part % 2
                    pe.matmul(bank_a[:, 0:N], block_w[:, w, :], xnT[:, k, :], start=True, stop=True)
                    ins = pe.matmul(bank_a[:, N:N + KC], block_w[:, w, :], cT[:, k, :], start=True, stop=True)
                elif step == "oT":
                    pe.wait_ge(normed, UNITS * b + G * (part + 1))
                    for g in range(G):
                        ins = pe.transpose(bank_a[:, g * P:g * P + P], attn[part][:, g * P:g * P + P], ident[:, :])
                else:
                    pe.wait_ge(x2_done, T * b + part + 1)
                    for k in range(KD):
                        ins = pe.transpose(bank_a[:, k * P:k * P + P], x2[part][:, k * P:k * P + P], ident[:, :])
                ins.then_inc(a_filled, 1)

            def fill_b(step, part, b, q):
                n = use_b(step, part, b)
                if not (isinstance(n, int) and n == 0):
                    pe.wait_ge(b_emptied, n)
                if step == "v":
                    pe.wait_ge(a_emptied, use_a("z", G - 1, b) + 1)
                    for g in range(G):
                        ins = pe.transpose(bank_b[0:KC, g * P:g * P + P], feat[q][:, g, N:], ident[:, :])
                elif step == "fc":
                    pe.wait_ge(a_emptied, use_a("oT", part, b) + 1)
                    for g in range(G):
                        ins = pe.matmul(bank_b[:, 0:D], attnT[:, g * P:g * P + P], fc_w[:, g, :],
                                        start=(g == 0), stop=(g == G - 1))
                else:
                    pe.wait_ge(a_emptied, use_a("x2T", part, b) + 1)
                    for k in range(KD):
                        ins = pe.matmul(bank_b[:, 0:E], x2T[:, k * P:k * P + P], router_w[:, k, :],
                                        start=(k == 0), stop=(k == KD - 1))
                ins.then_inc(b_filled, 1)

            pe.wait_ge(made, 3)
            pe.wait_ge(masks_made, 1 + HG + 2)
            pe.wait_ge(blocks_in, 2 * HG * 2 * 16)
            pe.wait_ge(weights_in, 6 * 16)
            for step, part in A_PROLOGUE:
                fill_a(step, part, 0, 0)
            fill_b("v", 0, 0, 0)
            scores(0, 0, 0)
            scores(1, 0, 0)

            def batch(b, p):
                first, last = isinstance(b, int) and b == 0, isinstance(b, int) and b == B - 1
                for s in range(UNITS):
                    if s < UNITS - 2:
                        scores(s + 2, b, p)
                    elif not last:
                        scores(s + 2 - UNITS, b + 1, 1 - p)
                    steps = in_slot(A_STEPS, b, s)
                    for step, part, offset in steps[:1]:
                        fill_a(step, part, b + offset, (p + offset) % 2)
                    turn(s, b)
                    if s > 0:
                        values(s - 1, b, p)
                    elif not first:
                        values(UNITS - 1, b - 1, 1 - p)
                    for step, part, offset in in_slot(B_STEPS, b, s):
                        fill_b(step, part, b + offset, (p + offset) % 2)
                    for step, part, offset in steps[1:]:
                        fill_a(step, part, b + offset, (p + offset) % 2)

            over_batches(pe, batch)
            values(UNITS - 1, B - 1, 1)
            for s in range(UNITS):
                for step, part, _ in in_slot(A_STEPS, B, s):
                    fill_a(step, part, B - 1, 1)
                for step, part, _ in in_slot(B_STEPS, B, s):
                    fill_b(step, part, B - 1, 1)

        @block.vector
        def _(dve):
            dve.memset(head_mask[:, :], 0.0).then_inc(masks_made, 1)
            dve.wait_ge(masks_made, 1)
            for h in range(HG):
                dve.memset(head_mask[EXP * h:EXP * h + EXP, h:h + 1], 1.0).then_inc(masks_made, 1)
            for p in range(2):
                dve.memset(v_one[p][:, :, EXP:EXP + 1], 1.0).then_inc(masks_made, 1)
            dve.wait_ge(made, 3)
            dve.tensor_scalar(sign_bits[:, :], sign_bits[:, :], 4, 1, ALU.logical_shift_right, ALU.bitwise_and
                              ).then_inc(stats1_raw, 1)
            dve.wait_ge(stats1_raw, 1)
            dve.tensor_scalar(sign[:, :], sign_bits[:, :], -2.0, 1.0, ALU.mult, ALU.add).then_inc(dve_const, 1)
            dve.wait_ge(dve_const, 1)
            dve.wait_ge(blocks_in, 2 * HG * 2 * 16)
            dve.tensor_tensor(sign_bias[:, :], bias_b[:, :], sign[:, :], ALU.mult).then_inc(dve_const, 1)
            dve.wait_ge(act_const, 2)
            dve.wait_ge(weights_in, 6 * 16)
            dve.tensor_scalar(fc_bias[:, :], fc_bias[:, :], tanh_x[:, 0:1], None, ALU.mult).then_inc(dve_const, 1)

            def stats(b, p):
                dve.wait_ge(x_loaded[p], 16 * b + 32 - 16 * p)
                for t in range(T):
                    dve.bn_stats(stat1[:, t, :], x_in[p][:, t, :]).then_inc(stats1_raw, 1)
                dve.wait_ge(stats1_raw, 1 + T * b + T)
                dve.memset(keep["spare_dve"][:, :], 0.0)
                for t in range(T):
                    ins = dve.bn_aggr(mean_var1[:, t, :], stat1[:, t, :])
                ins.then_inc(stats1_done, 1)

            def norm_x(b, p):
                dve.wait_ge(rstd1_done, b + 1)
                for t in range(T):
                    ins = dve.tensor_scalar(xn[:, t, :], x_in[p][:, t, :], mean_var1[:, t, 0:1], rstd1[:, t:t + 1],
                                            ALU.subtract, ALU.mult)
                ins.then_inc(xn_done, 1)

            def shift(s, b):
                u = UNITS * b + s
                tile = score_ps[s % 2][:, 0:HG * KC].rearrange("p (h k) -> p h k", h=HG)
                dve.wait_ge(scored, u + 1)
                dve.tensor_reduce(row_max[s % 2][:, :], tile, AX, ALU.max).then_inc(max_done, 1)
                dve.wait_ge(max_done, u + 1)
                if not (isinstance(b, int) and u < 4):
                    dve.wait_ge(turned, u - 3)
                dve.tensor_tensor(prob[s % 4][:, :].rearrange("p (h k) -> p h k", h=HG), tile,
                                  row_max[s % 2][:, :].rearrange("p (h k) -> p h k", k=1).to_broadcast([P, HG, KC]),
                                  ALU.subtract).then_inc(shifted, 1)

            def normalise(s, b):
                u, g, t = UNITS * b + s, s % G, s // G
                tile = value_ps[s % 2][:, 0:HG * (EXP + 1)].rearrange("p (h e) -> p h e", h=HG)
                dve.wait_ge(valued, u + 1)
                dve.reciprocal(recip[s % 2][:, :].rearrange("p (h k) -> p h k", k=1), tile[:, :, EXP:EXP + 1]
                               ).then_inc(recip_done, 1)
                dve.wait_ge(recip_done, u + 1)
                dve.tensor_tensor(attn[t][:, g * P:g * P + P].rearrange("p (h e) -> p h e", h=HG), tile[:, :, 0:EXP],
                                  recip[s % 2][:, :].rearrange("p (h k) -> p h k", k=1).to_broadcast([P, HG, EXP]),
                                  ALU.mult).then_inc(normed, 1)

            def empty_b(step, part, b, q):
                dve.wait_ge(b_filled, use_b(step, part, b) + 1)
                if step == "v":
                    dve.tensor_copy(v_one[q][:, :, 0:EXP], bank_b[0:KC, :].rearrange("p (h e) -> p h e", e=EXP)
                                    ).then_inc(b_emptied, 1)
                elif step == "logits":
                    dve.tensor_scalar(logits[:, part, bass.ds(b, 1), :],
                                      bank_b[:, 0:E].rearrange("p (a e) -> p a e", a=1), inv_temp[:, 0:1], None,
                                      ALU.mult).then_inc(b_emptied, 1)
                else:
                    n = T * b + part + 1
                    dve.wait_ge(x_bias_done, b + 1)
                    if part == 0 and not (isinstance(b, int) and b < 2):
                        dve.wait_ge(x1_stored[q], 8 * b - 8 * q)
                    dve.scalar_tensor_tensor(x1_out[q][:, part, :], bank_b[:, 0:D], tanh_x[:, 0:1],
                                             x_bias[q][:, part, :], ALU.mult, ALU.add).then_inc(b_emptied, 1)
                    dve.wait_ge(b_emptied, use_b(step, part, b) + 1)
                    dve.bn_stats(stat2[:, :], x1_out[q][:, part, :]).then_inc(x1_done, 1)
                    dve.wait_ge(x1_done, n)
                    dve.memset(keep["spare_dve"][:, :], 0.0)
                    dve.bn_aggr(mean_var2[part][:, :], stat2[:, :]).then_inc(stats2_done, 1)

            def norm_x2(b, t, q):
                n = T * b + t + 1
                dve.wait_ge(rstd2_done, n)
                if not (isinstance(b, int) and b == 0):
                    dve.wait_ge(x2_kept, n - T)
                    dve.wait_ge(a_filled, use_a("x2T", t, b - 1) + 1)
                dve.tensor_scalar(x2[t][:, :], x1_out[q][:, t, :], mean_var2[t][:, 0:1], rstd2[t][:, 0:1],
                                  ALU.subtract, ALU.mult).then_inc(x2_done, 1)

            stats(0, 0)
            norm_x(0, 0)
            empty_b("v", 0, 0, 0)
            shift(0, 0)

            def batch(b, p):
                first, last = isinstance(b, int) and b == 0, isinstance(b, int) and b == B - 1
                for s in range(UNITS):
                    if s < UNITS - 1:
                        shift(s + 1, b)
                    elif not last:
                        shift(0, b + 1)
                    for step, part, offset in in_slot(B_STEPS, b, s - 1):
                        empty_b(step, part, b + offset, (p + offset) % 2)
                    if s == 0 and not first:
                        empty_b("v", 0, b, p)
                    if s > 1:
                        normalise(s - 2, b)
                    elif not first:
                        normalise(UNITS + s - 2, b - 1)
                    if s == 0 and not last:
                        stats(b + 1, 1 - p)
                    if s == 1 and not last:
                        norm_x(b + 1, 1 - p)
                    if s == 2 and not first:
                        norm_x2(b - 1, 0, 1 - p)
                    if s == 5 and not first:
                        norm_x2(b - 1, 1, 1 - p)

            over_batches(dve, batch)
            normalise(UNITS - 2, B - 1)
            normalise(UNITS - 1, B - 1)
            for _, step, part, _ in kept(B_STEPS, B):
                empty_b(step, part, B - 1, 1)
                if step == "fc":
                    norm_x2(B - 1, part, 1)



def route(nc, dram, keep, arena):
    with ExitStack() as ctx:
        def sb2(name, shape, dt=F32):
            return [arena.take(f"{name}{h}", shape, dt) for h in range(2)]

        def sem(name):
            return ctx.enter_context(nc.semaphore(name))

        ident, logits = keep["ident"], keep["logits"]
        slot_index, slot_gate = keep["slot_index"], keep["slot_gate"]
        Q = T * HB
        over_e = sb2("over_e", [P, Q, E])
        over_e_max = sb2("over_e_max", [P, Q])
        over_e_exp = sb2("over_e_exp", [P, Q, E])
        over_e_sum = sb2("over_e_sum", [P, Q])
        over_e_log = sb2("over_e_log", [P, Q])
        over_e_out = sb2("over_e_out", [P, Q, E])
        neg_max = sb2("neg_max", [P, 1])
        over_n_exp = sb2("over_n_exp", [P, N])
        over_n_sum = sb2("over_n_sum", [P, 1])
        over_n_log = sb2("over_n_log", [P, 1])
        over_n = sb2("over_n", [P, N])
        affinity = sb2("affinity", [P, N])
        top = sb2("top", [P, CAP])
        top_at = sb2("top_at", [P, CAP], U32)
        top_twice = sb2("top_twice", [P, 2, CAP])
        at_twice = sb2("at_twice", [P, 2, CAP])
        to_n_ps = [ctx.enter_context(nc.psum_tensor(f"to_n_ps{h}", [P, 512], F32)) for h in range(2)]
        to_e_ps = [ctx.enter_context(nc.psum_tensor(f"to_e_ps{h}", [P, 512], F32)) for h in range(2)]
        slot_ps = [ctx.enter_context(nc.psum_tensor(f"slot_ps{h}", [P, 512], F32)) for h in range(2)]

        e_max, e_shift, e_exp, e_sum, e_log, e_done = (sem("e_" + n) for n in ("max", "shift", "exp", "sum", "log", "done"))
        in_n, n_max, n_exp, n_log, n_done, in_e = (sem(n) for n in ("in_n", "n_max", "n_exp", "n_log", "n_done", "in_e"))
        gates_done, topped, listed, slots_turned, slots_kept, index_out = (
            sem(n) for n in ("gates_done", "topped", "listed", "slots_turned", "slots_kept", "index_out"))

        block = ctx.enter_context(nc.Block())

        def groups(tile):
            return tile.rearrange("p (q e) -> p q e", e=E)

        def wide(small):
            return small.rearrange("p (q e) -> p q e", e=1).to_broadcast([P, Q, E])

        def over_rounds(eng, body):
            body(0)
            with eng.Fori(1, SINKHORN, 1) as i:
                body(i)

        @block.vector
        def _(dve):
            def body(i):
                for h in range(2):
                    n = 2 * i + h + 1
                    if isinstance(i, int):
                        for t in range(T):
                            ins = dve.tensor_reduce(over_e_max[h][:, HB * t:HB * t + HB],
                                                    logits[:, t, HB * h:HB * h + HB, :], AX, ALU.max)
                        ins.then_inc(e_max, 1)
                        dve.wait_ge(e_max, n)
                        for t in range(T):
                            ins = dve.tensor_tensor(
                                over_e[h][:, HB * t:HB * t + HB, :], logits[:, t, HB * h:HB * h + HB, :],
                                wide(over_e_max[h][:, :])[:, HB * t:HB * t + HB, :], ALU.subtract)
                        ins.then_inc(e_shift, 1)
                    else:
                        dve.wait_ge(in_e, n - 2)
                        src = groups(to_e_ps[h][:, 0:N])
                        dve.tensor_reduce(over_e_max[h][:, :], src, AX, ALU.max).then_inc(e_max, 1)
                        dve.wait_ge(e_max, n)
                        dve.tensor_tensor(over_e[h][:, :, :], src, wide(over_e_max[h][:, :]), ALU.subtract
                                          ).then_inc(e_shift, 1)
                for h in range(2):
                    n = 2 * i + h + 1
                    dve.wait_ge(e_exp, n)
                    dve.tensor_reduce(over_e_sum[h][:, :], over_e_exp[h][:, :, :], AX, ALU.add).then_inc(e_sum, 1)
                for h in range(2):
                    n = 2 * i + h + 1
                    dve.wait_ge(e_log, n)
                    dve.tensor_tensor(over_e_out[h][:, :, :], over_e[h][:, :, :], wide(over_e_log[h][:, :]),
                                      ALU.subtract).then_inc(e_done, 1)
                for h in range(2):
                    n = 2 * i + h + 1
                    dve.wait_ge(in_n, n)
                    dve.tensor_reduce(neg_max[h][:, :], to_n_ps[h][:, 0:N], AX, ALU.max, negate=True
                                      ).then_inc(n_max, 1)
                for h in range(2):
                    n = 2 * i + h + 1
                    dve.wait_ge(n_log, n)
                    dve.tensor_scalar(over_n[h][:, :], to_n_ps[h][:, 0:N], neg_max[h][:, 0:1], over_n_log[h][:, 0:1],
                                      ALU.add, ALU.subtract).then_inc(n_done, 1)

            over_rounds(dve, body)
            steps = 0
            dve.wait_ge(gates_done, 2)
            for r in range(CAP // 8):
                eight = slice(8 * r, 8 * r + 8)
                for h in range(2):
                    if r > 0:
                        dve.wait_ge(topped, steps - 1)
                    dve.max(top[h][:, eight], affinity[h][:, :]).then_inc(topped, 1)
                    steps += 1
                for h in range(2):
                    dve.wait_ge(topped, steps - 1 + h)
                    dve.max_index(top_at[h][:, eight], top[h][:, eight], affinity[h][:, :])
                    dve.match_replace(affinity[h][:, :], top[h][:, eight], affinity[h][:, :], -1.0
                                      ).then_inc(topped, 1)
                steps += 2
            dve.wait_ge(topped, steps)
            for h in range(2):
                dve.tensor_copy(at_twice[h][:, :, :], top_at[h][:, :].rearrange("p (a c) -> p a c", a=1)
                                .to_broadcast([P, 2, CAP])).then_inc(listed, 1)
                dve.tensor_copy(top_twice[h][:, :, :], top[h][:, :].rearrange("p (a c) -> p a c", a=1)
                                .to_broadcast([P, 2, CAP])).then_inc(listed, 1)
            for h in range(2):
                dve.wait_ge(slots_turned, h + 1)
                for k, table in enumerate((slot_index, slot_gate)):
                    for u in range(2):
                        half = slice(CAP * u, CAP * u + CAP)
                        for q in range(2):
                            batch, expert = (q, q ^ u) if table is slot_index else (q ^ u, q)
                            ins = dve.tensor_copy(
                                table[half, :, HB // 2 * h:HB // 2 * (h + 1)].rearrange(
                                    "p (i q) j -> p j i q", q=2)[:, :, :, q],
                                slot_ps[h][half, k * P:k * P + P].rearrange(
                                    "p (j r i q) -> p j r i q", r=2, q=2, i=E // 2)[:, :, batch, :, expert])
                ins.then_inc(slots_kept, 1)

        @block.scalar
        def _(act):
            def body(i):
                for h in range(2):
                    act.wait_ge(e_shift, 2 * i + h + 1)
                    act.activation(over_e_exp[h][:, :, :], over_e[h][:, :, :], ACT.Exp).then_inc(e_exp, 1)
                for h in range(2):
                    act.wait_ge(e_sum, 2 * i + h + 1)
                    act.activation(over_e_log[h][:, :], over_e_sum[h][:, :], ACT.Ln).then_inc(e_log, 1)
                for h in range(2):
                    n = 2 * i + h + 1
                    act.wait_ge(n_max, n)
                    act.activation(over_n_exp[h][:, :], to_n_ps[h][:, 0:N], ACT.Exp, bias=neg_max[h][:, :],
                                   accum_out=over_n_sum[h][:, :]).then_inc(n_exp, 1)
                    act.wait_ge(n_exp, n)
                    act.activation(over_n_log[h][:, :], over_n_sum[h][:, :], ACT.Ln).then_inc(n_log, 1)

            over_rounds(act, body)
            for h in range(2):
                act.wait_ge(n_done, 2 * SINKHORN - 1 + h)
                act.activation(affinity[h][:, :], over_n[h][:, :], ACT.Exp).then_inc(gates_done, 1)

        @block.tensor
        def _(pe):
            def body(i):
                for h in range(2):
                    pe.wait_ge(e_done, 2 * i + h + 1)
                    flat = over_e_out[h][:, :, :].rearrange("p q e -> p (q e)")
                    for t in range(T):
                        ins = pe.transpose(to_n_ps[h][:, t * P:t * P + P], flat[:, t * P:t * P + P], ident[:, :])
                    ins.then_inc(in_n, 1)
                for h in range(2):
                    pe.wait_ge(n_done, 2 * i + h + 1)
                    for t in range(T):
                        ins = pe.transpose(to_e_ps[h][:, t * P:t * P + P], over_n[h][:, t * P:t * P + P], ident[:, :])
                    ins.then_inc(in_e, 1)

            over_rounds(pe, body)
            for h in range(2):
                pe.wait_ge(listed, 2 * h + 2)
                for k, twice in enumerate((at_twice, top_twice)):
                    ins = pe.transpose(slot_ps[h][:, k * P:k * P + P],
                                       twice[h][:, :, :].rearrange("p a c -> p (a c)"), ident[:, :])
                ins.then_inc(slots_turned, 1)

        @block.sync
        def _(sp):
            for h in range(2):
                sp.wait_ge(listed, 2 * h + 1)
                sp.dma_start(dram["slot_index"][h * P:h * P + P, :], at_twice[h][:, 0, :]).then_inc(index_out, 16)
            sp.wait_ge(index_out, 32)
            sp.wait_ge(slots_kept, 2)



def gather(nc, dram, keep, arena):
    with ExitStack() as ctx:
        def sem(name):
            return ctx.enter_context(nc.semaphore(name))

        x2_all, expert_x = keep["x2_all"], keep["expert_x"]
        token_no = arena.take("token_no", [P, T])
        index_all = [arena.take(f"index_all{p}", [P, E * CAP]) for p in range(2)]
        pick = [arena.take(f"pick{p}", [P, T, E * CAP], F32R) for p in range(2)]
        x_hi = [arena.take(f"x_hi{p}", [P, T, D], F32R) for p in range(2)]
        x_lo = [arena.take(f"x_lo{p}", [P, T, D], F32R) for p in range(2)]
        out_ps = [ctx.enter_context(nc.psum_tensor(f"gather_ps{i}", [P, 512], F32)) for i in range(8)]
        EC = E * CAP // 512
        EB = E // EC

        numbered = sem("numbered")
        index_in = [sem(f"index_in{p}") for p in range(2)]
        picked, hi_done, lo_done, gathered = sem("picked"), sem("hi_done"), sem("lo_done"), sem("gathered")
        out_act, out_dve = sem("out_act"), sem("out_dve")

        block = ctx.enter_context(nc.Block())

        def early(b):
            return isinstance(b, int) and b < 2

        def over(eng, body):
            body(0, 0)
            body(1, 1)
            with eng.Fori(2, B - 1, 2) as i:
                body(i, 0)
                body(i + 1, 1)

        def home(c, b, p, k, q):
            at = b + q * (1 - 2 * p)
            return expert_x[:, EB * c:EB * c + EB, bass.ds(at, 1), k, :].rearrange(
                "p (i q) b c -> p i q (b c)", q=2)[:, :, q, :]

        def slots(bank, q):
            return out_ps[bank][:, :].rearrange("p (i q c) -> p i q c", q=2, c=CAP)[:, :, q, :]

        @block.gpsimd
        def _(pool):
            pool.iota(token_no[:, :], [[P, T]], base=0, channel_multiplier=1, allow_small_or_imprecise_dtypes=True
                      ).then_inc(numbered, 1)

        @block.sync
        def _(sp):
            def body(b, p):
                if not early(b):
                    sp.wait_ge(picked, b - 1)
                sp.dma_start(index_all[p][:, :], dram["slot_index"].rearrange("(b e) c -> b (e c)", e=E)
                             [bass.ds(b, 1), :].to_broadcast([P, E * CAP])).then_inc(index_in[p], 16)
            over(sp, body)

        @block.scalar
        def _(act):
            def body(b, p):
                if not early(b):
                    act.wait_ge(gathered, KD * EC * (b - 1))
                act.activation(x_hi[p][:, :, :], x2_all[:, bass.ds(T * b, T), :], ACT.Copy).then_inc(hi_done, 1)
                if not (isinstance(b, int) and b == 0):
                    copy_out(b - 1, 1 - p)

            def copy_out(b, p):
                for k in range(KD):
                    act.wait_ge(gathered, KD * EC * b + EC * k + 1)
                    for q in range(2):
                        ins = act.activation(home(0, b, p, k, q), slots(4 * p + EC * k, q), ACT.Copy)
                    ins.then_inc(out_act, 1)

            over(act, body)
            copy_out(B - 1, 1)

        @block.vector
        def _(dve):
            dve.wait_ge(numbered, 1)

            def body(b, p):
                dve.wait_ge(index_in[p], 8 * b + 16 - 8 * p)
                if not early(b):
                    dve.wait_ge(gathered, KD * EC * (b - 1))
                for t in range(T):
                    ins = dve.tensor_scalar(pick[p][:, t, :], index_all[p][:, :], token_no[:, t:t + 1], None,
                                            ALU.is_equal)
                ins.then_inc(picked, 1)
                dve.wait_ge(hi_done, b + 1)
                dve.tensor_tensor(x_lo[p][:, :, :], x2_all[:, bass.ds(T * b, T), :], x_hi[p][:, :, :].bitcast(F32),
                                  ALU.subtract).then_inc(lo_done, 1)
                if not (isinstance(b, int) and b == 0):
                    copy_out(b - 1, 1 - p)

            def copy_out(b, p):
                for k in range(KD):
                    dve.wait_ge(gathered, KD * EC * b + EC * k + 2)
                    for q in range(2):
                        ins = dve.tensor_copy(home(1, b, p, k, q), slots(4 * p + EC * k + 1, q))
                    ins.then_inc(out_dve, 1)

            over(dve, body)
            copy_out(B - 1, 1)

        @block.tensor
        def _(pe):
            def body(b, p):
                pe.wait_ge(picked, b + 1)
                pe.wait_ge(lo_done, b + 1)
                for k in range(KD):
                    for c, out in enumerate((out_act, out_dve)):
                        if not early(b):
                            pe.wait_ge(out, KD * (b - 2) + k + 1)
                        for n, (t, part) in enumerate((t, part) for t in range(T) for part in (x_hi, x_lo)):
                            ins = pe.matmul(out_ps[4 * p + EC * k + c][:, :], part[p][:, t, k * P:k * P + P],
                                            pick[p][:, t, c * 512:c * 512 + 512], start=(n == 0), stop=(n == 2 * T - 1))
                        ins.then_inc(gathered, 1)
            over(pe, body)



def experts(nc, dram, keep, arena):
    with ExitStack() as ctx:
        def sem(name):
            return ctx.enter_context(nc.semaphore(name))

        def bank(name):
            return ctx.enter_context(nc.psum_tensor(name, [P, 512], F32))

        expert_x, slot_gate = keep["expert_x"], keep["slot_gate"]
        expert_out = expert_x[:, :, :, :, :].rearrange("p e b k c -> p e (b k c)")
        HS = E * CAP // 2
        TS = HS // P
        HALF = KD * HS
        STEPS = 2 * M
        RING = 4
        w_in = [arena.take(f"w_in{i}", [P, 2 * D]) for i in range(RING)]
        w_hi = arena.take("w_hi", [P, M, 2 * D], F32R)
        w_lo = arena.take("w_lo", [P, M, 2 * D], F32R)
        x_hi = [arena.take(f"ex_hi{h}", [P, KD, HS], F32R) for h in range(2)]
        x_lo = [arena.take(f"ex_lo{h}", [P, KD, HS], F32R) for h in range(2)]
        hidden = [arena.take(f"hidden{i}", [P, HS]) for i in range(2)]
        h_hi = [arena.take(f"h_hi{i}", [P, HS], F32R) for i in range(4)]
        h_lo = [arena.take(f"h_lo{i}", [P, HS], F32R) for i in range(4)]
        b1 = arena.take("b1", [P, E * M])
        b2 = arena.take("b2", [P, D])
        b1_now = [arena.take(f"b1_now{h}", [P, M]) for h in range(2)]
        hidden_ps = [bank(f"hidden_ps{i}") for i in range(4)]
        out_ps = [[bank(f"out_ps{h}{i}") for i in range(2)] for h in range(2)]

        w_loaded = [sem(f"w_loaded{i}") for i in range(RING)]
        b1_in, b2_in, b1_ready = sem("b1_in"), sem("b2_in"), sem("b1_ready")
        w_hi_done, w_done = sem("w_hi_done"), sem("w_done")
        ex_hi_done, ex_done = sem("ex_hi_done"), sem("ex_done")
        hidden_done, gelu_done = sem("hidden_done"), sem("gelu_done")
        h_hi_done, h_done = sem("h_hi_done"), sem("h_done")
        out_added, biased, out_done = sem("out_added"), sem("biased"), sem("out_done")

        block = ctx.enter_context(nc.Block())

        def over(eng, body):
            body(0, 0)
            with eng.Fori(1, E - 2, 2) as i:
                body(i, 1)
                body(i + 1, 0)
            body(E - 1, 1)

        def is0(e):
            return isinstance(e, int) and e == 0

        @block.sync
        def _(sp):
            sp.dma_start(b1[:, :], dram["b1"]).then_inc(b1_in, 16)

            def body(e, odd):
                for m in range(M):
                    if not (is0(e) and m < RING):
                        sp.wait_ge(w_done, M * e + m + 1 - RING)
                    sp.dma_start(w_in[m % RING][:, 0:D].rearrange("p (k f) -> p k f", k=KD),
                                 dram["w1"][bass.ds(e * D, D), m * P:m * P + P].rearrange("(k p) f -> p k f", p=P)
                                 ).then_inc(w_loaded[m % RING], 16)
                    sp.dma_start(w_in[m % RING][:, D:2 * D], dram["w2"][bass.ds(e * FF + m * P, P), :]
                                 ).then_inc(w_loaded[m % RING], 16)
            over(sp, body)

        @block.gpsimd
        def _(pool):
            def body(e, odd):
                for m in range(M):
                    pool.wait_ge(w_hi_done, M * e + m + 1)
                    pool.tensor_tensor(w_lo[:, m, :], w_in[m % RING][:, :], w_hi[:, m, :].bitcast(F32), ALU.subtract
                                       ).then_inc(w_done, 1)
            over(pool, body)

        @block.scalar
        def _(act):
            def split_w_hi(e, m):
                act.wait_ge(w_loaded[m % RING], 32 * (M // RING) * e + 32 * (m // RING + 1))
                if not is0(e):
                    act.wait_ge(out_added, STEPS * (e - 1) + M + m + 1)
                act.activation(w_hi[:, m, :], w_in[m % RING][:, :], ACT.Copy).then_inc(w_hi_done, 1)

            for m in range(M):
                split_w_hi(0, m)

            def body(e, odd):
                for k in range(STEPS):
                    if k < 3 and not is0(e):
                        split_w_hi(e, M - 3 + k)
                    if k >= M + 3 and not (isinstance(e, int) and e == E - 1):
                        split_w_hi(e + 1, k - M - 3)
                    if k % M == 0:
                        act.wait_ge(b1_ready, 2 * e + k // M + 1)
                    act.wait_ge(hidden_done, STEPS * e + k + 1)
                    if not (is0(e) and k < 2):
                        act.wait_ge(h_done, STEPS * e + k - 1)
                    act.activation(hidden[k % 2][:, :], hidden_ps[k % 4][:, :], ACT.Gelu_apprx_tanh,
                                   bias=b1_now[k // M][:, k % M:k % M + 1]).then_inc(gelu_done, 1)
                    if k == 5:
                        if not is0(e):
                            act.wait_ge(out_done, 2 * e)
                        act.dma_start(b2[:, :], dram["b2"][bass.ds(e, 1), :].to_broadcast([P, D])
                                      ).then_inc(b2_in, 16)
            over(act, body)

        @block.vector
        def _(dve):
            def tokens(tile):
                return tile[:, :, :].rearrange("p k (b c) -> p k b c", c=CAP)

            def split_x_hi(e, h):
                src = expert_out[:, bass.ds(e, 1), h * HALF:(h + 1) * HALF].rearrange(
                    "p a (b k c) -> p (a k) b c", k=KD, c=CAP)
                dve.tensor_copy(tokens(x_hi[h]), src).then_inc(ex_hi_done, 1)

            def split_x_lo(e, h):
                src = expert_out[:, bass.ds(e, 1), h * HALF:(h + 1) * HALF].rearrange(
                    "p a (b k c) -> p (a k) b c", k=KD, c=CAP)
                dve.wait_ge(ex_hi_done, 2 * e + h + 1)
                dve.tensor_tensor(tokens(x_lo[h]), src, tokens(x_hi[h]).bitcast(F32), ALU.subtract
                                  ).then_inc(ex_done, 1)

            def split_hidden(e, k):
                q = STEPS * e + k
                dve.wait_ge(gelu_done, q + 1)
                if not (is0(e) and k < 4):
                    dve.wait_ge(out_added, q - 3)
                dve.tensor_copy(h_hi[k % 4][:, :], hidden[k % 2][:, :]).then_inc(h_hi_done, 1)
                dve.wait_ge(h_hi_done, q + 1)
                dve.tensor_tensor(h_lo[k % 4][:, :], hidden[k % 2][:, :], h_hi[k % 4][:, :].bitcast(F32), ALU.subtract
                                  ).then_inc(h_done, 1)

            def finish(e, h, odd, part):
                lower, upper = slice(0, CAP), slice(CAP, 2 * CAP)
                if part == 0 and odd:
                    dve.wait_ge(out_done, 2 * e + h - 1)
                    dve.tensor_copy(expert_out[upper, bass.ds(e, 1), h * HALF:(h + 1) * HALF],
                                    expert_out[upper, bass.ds(e - 1, 1), h * HALF:(h + 1) * HALF])
                if part == 0:
                    dve.wait_ge(out_added, STEPS * e + M * h + M)
                    dve.wait_ge(b2_in, 16 * e + 16)
                    for i in range(2):
                        tiles = out_ps[h][i][:, :].rearrange("p (t d) -> p t d", d=D)
                        dve.tensor_tensor(tiles, tiles, b2[:, :].rearrange("p (t d) -> p t d", t=1)
                                          .to_broadcast([P, 2, D]), ALU.add).then_inc(biased, 1)
                    return
                if part == 1:
                    dve.wait_ge(biased, 4 * e + 2 * h + 2)
                for t in range(2 * part - 2, 2 * part):
                    at = h * HALF + t * D
                    for rows, home in ((lower, e), (upper, e - 1)) if odd else ((slice(0, P), e),):
                        ins = dve.tensor_scalar(
                            expert_out[rows, bass.ds(home, 1), at:at + D].rearrange("p a d -> p (a d)"),
                            out_ps[h][t // 2][rows, t % 2 * D:t % 2 * D + D],
                            slot_gate[rows, bass.ds(e, 1), TS * h + t], None, ALU.mult)
                if part == 2:
                    ins.then_inc(out_done, 1)

            def take_b1(e, h):
                dve.tensor_copy(b1_now[h][:, :], b1[:, bass.ds(e * M, M)]).then_inc(b1_ready, 1)

            dve.wait_ge(b1_in, 16)
            take_b1(0, 0)
            split_x_hi(0, 0)
            split_x_lo(0, 0)

            def body(e, odd):
                for k in range(STEPS):
                    split_hidden(e, k)
                    if 1 <= k <= 3 and not is0(e):
                        finish(e - 1, 1, 1 - odd, k - 1)
                    if M + 1 <= k <= M + 3:
                        finish(e, 0, odd, k - M - 1)
                    if k == 4:
                        if not is0(e):
                            dve.wait_ge(hidden_done, STEPS * e)
                        split_x_hi(e, 1)
                    if k == 2:
                        take_b1(e, 1)
                    if k == 5:
                        split_x_lo(e, 1)
                    if not (isinstance(e, int) and e == E - 1):
                        if k == M + 2:
                            take_b1(e + 1, 0)
                        if k == M + 4:
                            dve.wait_ge(hidden_done, STEPS * e + M)
                            split_x_hi(e + 1, 0)
                        if k == M + 5:
                            split_x_lo(e + 1, 0)
            over(dve, body)
            for part in range(3):
                finish(E - 1, 1, 1, part)

        @block.tensor
        def _(pe):
            def hidden_step(e, k):
                q, h, m = STEPS * e + k, k // M, k % M
                if h == 0:
                    pe.wait_ge(w_done, M * e + m + 1)
                if m == 0:
                    pe.wait_ge(ex_done, 2 * e + h + 1)
                if not (is0(e) and k < 4):
                    pe.wait_ge(gelu_done, q - 3)
                for n, (d, w, x) in enumerate((d, w, x) for d in range(KD)
                                              for w, x in ((w_hi, x_hi), (w_hi, x_lo), (w_lo, x_hi))):
                    ins = pe.matmul(hidden_ps[k % 4][:, :], w[:, m, d * P:d * P + P], x[h][:, d, :],
                                    start=(n == 0), stop=(n == 3 * KD - 1))
                ins.then_inc(hidden_done, 1)

            def out_step(e, k):
                q, h, m = STEPS * e + k, k // M, k % M
                pe.wait_ge(h_done, q + 1)
                if m == 0 and not is0(e):
                    pe.wait_ge(out_done, 2 * e + h - 1)
                for t in range(TS):
                    for n, (x, w) in enumerate(((h_hi, w_hi), (h_hi, w_lo), (h_lo, w_hi))):
                        ins = pe.matmul(out_ps[h][t // 2][:, (t % 2) * D:(t % 2) * D + D],
                                        x[k % 4][:, t * P:t * P + P], w[:, m, D:2 * D],
                                        start=(m == 0 and n == 0 and t % 2 == 0), stop=(m == M - 1 and n == 2),
                                        skip_group_check=True)
                ins.then_inc(out_added, 1)

            def body(e, odd):
                for k in range(STEPS):
                    hidden_step(e, k)
                    if k >= 2:
                        out_step(e, k - 2)
                    elif not is0(e):
                        out_step(e - 1, STEPS + k - 2)
            over(pe, body)
            out_step(E - 1, STEPS - 2)
            out_step(E - 1, STEPS - 1)



def scatter(nc, dram, keep, arena):
    with ExitStack() as ctx:
        def sem(name):
            return ctx.enter_context(nc.semaphore(name))

        expert_out = keep["expert_x"][:, :, :, :, :].rearrange("p e b k c -> p e (b k c)")
        slot_index, tanh_f = keep["slot_index"], keep["tanh_f"]
        V = 4
        EQ = E // V
        column_no = arena.take("column_no", [P, N])
        out_hi = [arena.take(f"out_hi{v}", [P, EQ, D], F32R) for v in range(V)]
        out_lo = [arena.take(f"out_lo{v}", [P, EQ, D], F32R) for v in range(V)]
        place = [arena.take(f"place{v}", [P, EQ, N], F32R) for v in range(V)]
        x1 = [arena.take(f"x1_back{p}", [P, 2 * T, D]) for p in range(2)]
        sum_ps = [[ctx.enter_context(nc.psum_tensor(f"sum_ps{p}{i}", [P, 512], F32)) for i in range(2 * T)]
                  for p in range(2)]

        numbered, split_hi, split_dve, split_pool, placed, summed, out_ready = (
            sem(n) for n in ("columns_numbered", "split_hi", "split_dve", "split_pool", "placed", "summed", "out_ready"))
        x1_in = [sem(f"x1_in{p}") for p in range(2)]
        stored = [sem(f"stored{p}") for p in range(2)]

        block = ctx.enter_context(nc.Block())
        PAIRS = B // 2

        def over(eng, body):
            body(0, 0)
            with eng.Fori(1, PAIRS - 1, 2) as i:
                body(i, 1)
                body(i + 1, 0)
            body(PAIRS - 1, 1)

        def is0(j):
            return isinstance(j, int) and j == 0

        def quarter(j, v):
            return expert_out[:, EQ * v:EQ * v + EQ, bass.ds(j * D, D)]

        @block.gpsimd
        def _(pool):
            pool.iota(column_no[:, :], [[1, N]], base=0, channel_multiplier=0, allow_small_or_imprecise_dtypes=True
                      ).then_inc(numbered, 1)

            def body(j, p):
                for v in range(1, V):
                    if not is0(j):
                        pool.wait_ge(summed, V * (j - 1) + v + 1)
                    pool.wait_ge(split_hi, V * j + v + 1)
                    pool.tensor_tensor(out_lo[v][:, :, :], quarter(j, v), out_hi[v][:, :, :].bitcast(F32),
                                       ALU.subtract).then_inc(split_pool, 1)
            over(pool, body)

        @block.sync
        def _(sp):
            def load(j, p, wait):
                if wait:
                    sp.wait_ge(stored[p], 8 * j - 8 * p)
                sp.dma_start(x1[p][:, :, :].rearrange("p (r t) d -> p r (t d)", r=2),
                             dram["x1"][bass.ds(2 * j * P, 2 * P), :].rearrange("(r p) n -> p r n", p=P)
                             ).then_inc(x1_in[p], 16)

            def store(j, p):
                sp.wait_ge(out_ready, j + 1)
                sp.dma_start(dram["out"][bass.ds(2 * j * N, 2 * N), :].rearrange("(r p) d -> p r d", p=P),
                             x1[p][:, :, :]).then_inc(stored[p], 16)

            load(0, 0, False)
            load(1, 1, False)
            store(0, 0)
            with sp.Fori(2, PAIRS - 1, 2) as i:
                load(i, 0, True)
                store(i - 1, 1)
                load(i + 1, 1, True)
                store(i, 0)
            store(PAIRS - 1, 1)
            for p in range(2):
                sp.wait_ge(stored[p], 16 * PAIRS // 2)

        @block.scalar
        def _(act):
            def body(j, p):
                for v in range(V):
                    if not is0(j):
                        act.wait_ge(summed, V * (j - 1) + v + 1)
                    act.activation(out_hi[v][:, :, :], quarter(j, v), ACT.Copy).then_inc(split_hi, 1)
            over(act, body)

        @block.vector
        def _(dve):
            dve.wait_ge(numbered, 1)

            def find_places(j, v):
                if not is0(j):
                    dve.wait_ge(summed, V * (j - 1) + v + 1)
                for e in range(EQ):
                    ins = dve.tensor_scalar(place[v][:, e, :], column_no[:, :],
                                            slot_index[:, EQ * v + e, bass.ds(j, 1)], None, ALU.is_equal)
                ins.then_inc(placed, 1)
                if v == 0:
                    dve.wait_ge(split_hi, V * j + 1)
                    dve.tensor_tensor(out_lo[0][:, :, :], quarter(j, 0), out_hi[0][:, :, :].bitcast(F32), ALU.subtract
                                      ).then_inc(split_dve, 1)

            def finish(j, p):
                dve.wait_ge(summed, V * j + V)
                dve.wait_ge(x1_in[p], 8 * j + 16 - 8 * p)
                for i in range(2 * T):
                    ins = dve.scalar_tensor_tensor(x1[p][:, i, :], sum_ps[p][i][:, 0:D], tanh_f[:, 0:1], x1[p][:, i, :],
                                                   ALU.mult, ALU.add)
                ins.then_inc(out_ready, 1)

            def body(j, p):
                for v in range(V):
                    find_places(j, v)
                    if v == 1 and not is0(j):
                        finish(j - 1, 1 - p)
            over(dve, body)
            finish(PAIRS - 1, 1)

        @block.tensor
        def _(pe):
            def body(j, p):
                for v in range(V):
                    pe.wait_ge(placed, V * j + v + 1)
                    if v == 0:
                        pe.wait_ge(split_dve, j + 1)
                    else:
                        pe.wait_ge(split_pool, (V - 1) * j + v)
                    if v == 0 and not (isinstance(j, int) and j < 2):
                        pe.wait_ge(out_ready, j - 1)
                    for e in range(EQ):
                        for n, part in enumerate((out_hi, out_lo)):
                            for t in range(T):
                                ins = pe.matmul(sum_ps[p][T * (e % 2) + t][:, 0:D], place[v][:, e, t * P:t * P + P],
                                                part[v][:, e, :], start=(v == 0 and e < 2 and n == 0),
                                                stop=(v == V - 1 and e >= EQ - 2 and n == 1))
                    ins.then_inc(summed, 1)
            over(pe, body)


def flamingo_layer(nc, dram):
    start = nc.sbuf_base + -nc.sbuf_base % 32
    end = nc.sbuf_usable_end
    tables = Arena(nc, start, end)
    keep = {
        "ident": tables.take("ident", [P, P]),
        "slot_index": tables.take("slot_index_sb", [P, E, B // 2]),
        "slot_gate": tables.take("slot_gate", [P, E, B // 2]),
        "tanh_f": tables.take("tanh_f", [P, 1]),
        "spare_dve": tables.take("spare_dve", [P, 1]),
    }
    middle = tables.at
    keep["expert_x"] = tables.take("expert_x", [P, E, B, KD, CAP])
    rest = tables.at
    phase3 = Arena(nc, rest, end)
    keep["x2_all"] = phase3.take("x2_all", [P, B * T, D])
    keep["logits"] = phase3.take("logits", [P, T, B, E])
    attention(nc, dram, keep, Arena(nc, middle, rest))
    route(nc, dram, keep, Arena(nc, middle, rest))
    gather(nc, dram, keep, phase3)
    experts(nc, dram, keep, Arena(nc, rest, end))
    scatter(nc, dram, keep, Arena(nc, rest, end))


def kernel(**inputs):
    import concourse.bacc as bacc
    from concourse.bass_utils import run_bass_kernel_spmd

    def a(name):
        return np.asarray(inputs[name])

    arrays = {
        "x": a("x").reshape(B * N, D),
        "ctx": a("ctx_1024").reshape(B * KC, D),
        "g_xattn": a("g_xattn").reshape(1),
        "g_ffn": a("g_ffn").reshape(1),
        "fm_wT": a("L0_xattn_fm_w").T,
        "fm_b": a("L0_xattn_fm_b").reshape(HD, 1),
        "fc_wT": a("L0_xattn_fc_w").T,
        "fc_b": a("L0_xattn_fc_b"),
        "gate_queryT": a("L0_ffn_gate_query").T,
        "log_temp": a("L0_ffn_log_temp").reshape(1),
        "w1": a("L0_ffn_w1").reshape(E * D, FF),
        "b1": a("L0_ffn_b1").reshape(E * M, P).T,
        "w2": a("L0_ffn_w2").reshape(E * FF, D),
        "b2": a("L0_ffn_b2"),
    }
    arrays = {f"in_{n}": np.ascontiguousarray(v) for n, v in arrays.items()}
    nc = bacc.Bacc("TRN2", target_bir_lowering=False, num_devices=1)
    dram = {n[3:]: nc.dram_tensor(n, v.shape, mybir.dt.from_np(v.dtype), kind="ExternalInput").ap()
            for n, v in arrays.items()}
    dram["x1"] = nc.dram_tensor("x1_scratch", (B * P, T * D), F32, kind="Internal").ap()
    dram["slot_index"] = nc.dram_tensor("slot_index_scratch", (B * E, CAP), F32, kind="Internal").ap()
    dram["out"] = nc.dram_tensor("out_x", (B * N, D), F32, kind="ExternalOutput").ap()
    flamingo_layer(nc, dram)
    result = run_bass_kernel_spmd(nc, [arrays], core_ids=[0])
    return result.results[0]["out_x"].reshape(B, N, D)
```

```python
from contextlib import ExitStack

import numpy as np

import concourse.bass as bass
from concourse import mybir

F32 = mybir.dt.float32
F32R = mybir.dt.float32r
I32 = mybir.dt.int32
U32 = mybir.dt.uint32
ALU = mybir.AluOpType
ACT = mybir.ActivationFunctionType
AX = mybir.AxisListType.X

P = 128
B, N, D = 16, 256, 256
KC = 120
HEADS, HD = 16, 16
EXP = 2 * HD
HG = P // EXP
G = HEADS // HG
T = N // P
KD = D // P
UNITS = T * G
E, FF = 16, 1024
M = FF // P
CAP = int(512 * 2.0 / E)
W_RING = 4
HB = 8
SINKHORN = 6
EPS = 1e-5
SCALE = 1.0 / 16.0


class Arena:

    def __init__(self, nc, start, end):
        self.nc, self.at, self.end = nc, start, end

    def take(self, name, shape, dt=F32):
        size = 4 * int(np.prod(shape[1:]))
        size += -size % 32
        assert self.at + size <= self.end, (name, self.at + size, self.end)
        tensor = self.nc.alloc_sbuf_tensor_at(name, shape, dt, offset=self.at)
        self.at += size
        return tensor



A_STEPS = [(0, "cT", 0, 1), (2, "oT", 1, -1), (2.5, "xnT", 0, 1), (3.5, "z", 0, 1), (4, "x2T", 0, -1),
           (4.5, "z", 1, 1), (5.5, "z", 2, 1), (6, "x2T", 1, -1), (6.5, "z", 3, 1), (7, "oT", 0, 0)]
B_STEPS = [(1, "fc", 0, -1), (3, "fc", 1, -1), (5, "logits", 0, -1), (6, "logits", 1, -1), (7, "v", 0, 1)]
A_PROLOGUE = [("cT", 0), ("xnT", 0), ("z", 0), ("z", 1), ("z", 2), ("z", 3)]
B_PROLOGUE = [("v", 0)]


def kept(steps, home):
    if not isinstance(home, int):
        return steps
    return [s for s in steps if 0 <= home + s[3] < B and (home < B or s[3] < 0)]


def in_slot(steps, home, slot):
    return [s[1:] for s in kept(steps, home) if s[0] == slot]


def uses_before(steps, prologue, step, part, b):
    offset = next(s[3] for s in steps if s[1:3] == (step, part))
    home = b - offset
    if isinstance(home, int) and home < 0:
        return prologue.index((step, part))
    before = len(prologue)
    if isinstance(home, int):
        before += sum(len(kept(steps, h)) for h in range(home))
    else:
        before += len(kept(steps, 0)) + len(steps) * (home - 1)
    return before + [s[1:3] for s in kept(steps, home)].index((step, part))


def use_a(step, part, b):
    return uses_before(A_STEPS, A_PROLOGUE, step, part, b)


def use_b(step, part, b):
    return uses_before(B_STEPS, B_PROLOGUE, step, part, b)


def over_batches(eng, body):
    body(0, 0)
    body(1, 1)
    with eng.Fori(2, B - 2, 2) as i:
        body(i, 0)
        body(i + 1, 1)
    body(B - 2, 0)
    body(B - 1, 1)


def attention(nc, dram, keep, arena):
    with ExitStack() as ctx:
        sb = arena.take

        def ps(name):
            return ctx.enter_context(nc.psum_tensor(name, [P, 512], F32))

        def sem(name):
            return ctx.enter_context(nc.semaphore(name))

        ident, x2_all, logits = keep["ident"], keep["x2_all"], keep["logits"]

        block_w = sb("block_w", [P, 2, P])
        block_hi = sb("block_hi", [P, 2, P], F32R)
        block_lo = sb("block_lo", [P, 2, P], F32R)
        sign = sb("sign", [P, 1])
        map_rows = sb("map_rows", [P, HD])
        row_bits = sb("row_bits", [P, 1], I32)
        row_block = sb("row_block", [P, 1])
        block_no = sb("block_no", [P, 2 * HG])
        block_mask = sb("block_mask", [P, 2 * HG])
        sign_bits = sb("sign_bits", [P, 1], I32)
        bias_b = sb("bias_b", [P, 1])
        sign_bias = sb("sign_bias", [P, 1])
        head_mask = sb("head_mask", [P, HG])
        fc_hi = sb("fc_hi", [P, G, D], F32R)
        fc_lo = sb("fc_lo", [P, G, D], F32R)
        fc_bias = sb("fc_bias", [P, D])
        gate_in = sb("gate_in", [P, 2])
        tanh_x = sb("tanh_x", [P, 1])
        log_temp = sb("log_temp", [P, 1])
        inv_temp = sb("inv_temp", [P, 1])
        router_w = sb("router_w", [P, KD, E])
        neg_half = sb("neg_half", [P, T])
        eps = sb("eps", [P, T])
        x_in = [sb(f"x_in{p}", [P, T, D]) for p in range(2)]
        ctx_in = [sb(f"ctx_in{p}", [KC, D]) for p in range(2)]
        x_bias = [sb(f"x_bias{p}", [P, T, D]) for p in range(2)]
        feat = sb("feat", [P, G, N + KC])
        f_hi = [sb(f"f_hi{p}", [P, G, N + KC], F32R) for p in range(2)]
        f_lo = [sb(f"f_lo{p}", [P, G, N + KC], F32R) for p in range(2)]
        k_hi = [sb(f"k_hi{p}", [P, G, HG * KC], F32R) for p in range(2)]
        k_lo = [sb(f"k_lo{p}", [P, G, HG * KC], F32R) for p in range(2)]
        v_one = [sb(f"v_one{p}", [KC, HEADS, EXP + 1]) for p in range(2)]
        x1_out = [sb(f"x1_out{p}", [P, T, D]) for p in range(2)]
        fc_w = x1_out
        stat1 = sb("stat1", [P, T, 6])
        mean_var1 = sb("mean_var1", [P, T, 2])
        var_eps1 = sb("var_eps1", [P, T])
        rstd1 = sb("rstd1", [P, T])
        xn = sb("xn", [P, T, D])
        xcT = sb("xcT", [P, KD, N + KC])
        xc_hi = sb("xc_hi", [P, KD, N + KC], F32R)
        xc_lo = sb("xc_lo", [P, KD, N + KC], F32R)
        row_max = [sb(f"row_max{i}", [P, HG]) for i in range(2)]
        prob = [sb(f"prob{i}", [P, HG * KC]) for i in range(4)]
        probT = [sb(f"probT{i}", [KC, HG * P]) for i in range(2)]
        recip = [sb(f"recip{i}", [P, HG]) for i in range(2)]
        attn = [sb(f"attn{t}", [P, G * P]) for t in range(T)]
        attnT = sb("attnT", [P, G * P])
        attn_hi = sb("attn_hi", [P, G * P], F32R)
        attn_lo = sb("attn_lo", [P, G * P], F32R)
        stat2 = sb("stat2", [P, 6])
        mean_var2 = [sb(f"mean_var2{t}", [P, 2]) for t in range(T)]
        var_eps2 = sb("var_eps2", [P, 1])
        rstd2 = [sb(f"rstd2{t}", [P, 1]) for t in range(T)]
        x2 = [sb(f"x2{t}", [P, D]) for t in range(T)]
        x2T = sb("x2T", [P, KD * P])

        score_ps = [ps(f"score_ps{i}") for i in range(2)]
        probT_ps = [ps(f"probT_ps{i}") for i in range(2)]
        value_ps = [ps(f"value_ps{i}") for i in range(2)]
        bank_a = ps("bank_a")
        bank_b = ps("bank_b")

        gates_in, weights_in = sem("gates_in"), sem("weights_in")
        zeroed = sem("zeroed")
        map_in, row_done, mask_done, blocks_made = (sem(n) for n in ("map_in", "row_done", "mask_done", "blocks_made"))
        made = sem("made")
        masks_made = sem("masks_made")
        dve_const = sem("dve_const")
        act_const = sem("act_const")
        x_loaded = [sem(f"x_loaded{p}") for p in range(2)]
        x1_stored = [sem(f"x1_stored{p}") for p in range(2)]
        stats1_raw, stats1_done = sem("stats1_raw"), sem("stats1_done")
        var1_done, rstd1_done, xn_done = sem("var1_done"), sem("rstd1_done"), sem("xn_done")
        x_bias_done = sem("x_bias_done")
        first_bank = dict(zip(A_PROLOGUE, (probT_ps[0], bank_a, score_ps[0], score_ps[1], value_ps[0], value_ps[1])))

        def a_bank(step, part, b):
            return first_bank.get((step, part), bank_a) if isinstance(b, int) and b == 0 else bank_a

        weights_hi, block_lo_done, fc_lo_done = sem("weights_hi"), sem("block_lo_done"), sem("fc_lo_done")
        xc_hi_done, xc_lo_done = sem("xc_hi_done"), sem("xc_lo_done")
        attn_hi_done, attn_lo_done = sem("attn_hi_done"), sem("attn_lo_done")
        f_hi_done, f_lo_done, k_block_done = sem("f_hi_done"), sem("f_lo_done"), sem("k_block_done")
        a_filled, a_emptied = sem("a_filled"), sem("a_emptied")
        b_filled, b_emptied = sem("b_filled"), sem("b_emptied")
        scored, max_done, shifted, exp_done = sem("scored"), sem("max_done"), sem("shifted"), sem("exp_done")
        turned, turned_out = sem("turned"), sem("turned_out")
        valued, recip_done, normed = sem("valued"), sem("recip_done"), sem("normed")
        x1_done, stats2_done = sem("x1_done"), sem("stats2_done")
        var2_done, rstd2_done, x2_done, x2_kept = sem("var2_done"), sem("rstd2_done"), sem("x2_done"), sem("x2_kept")

        block = ctx.enter_context(nc.Block())

        @block.sync
        def _(sp):
            def load(b, p):
                if not (isinstance(b, int) and b < 2):
                    sp.wait_ge(xn_done, b - 1)
                    sp.wait_ge(x_bias_done, b - 1)
                    sp.wait_ge(a_filled, use_a("cT", 0, b - 2) + 1)
                sp.dma_start(x_in[p][:, :, :], dram["x"][bass.ds(b * N, N), :].rearrange("(t p) d -> p t d", p=P)
                             ).then_inc(x_loaded[p], 16)
                sp.dma_start(ctx_in[p][:, :], dram["ctx"][bass.ds(b * KC, KC), :]).then_inc(x_loaded[p], 16)

            def store(b, p):
                sp.wait_ge(x1_done, T * b + T)
                sp.dma_start(dram["x1"][bass.ds(b * P, P), :], x1_out[p][:, :, :].rearrange("p t d -> p (t d)")
                             ).then_inc(x1_stored[p], 16)

            load(0, 0)
            sp.dma_start(gate_in[:, 0:1], dram["g_xattn"].partition_broadcast(P)).then_inc(gates_in, 16)
            sp.dma_start(gate_in[:, 1:2], dram["g_ffn"].partition_broadcast(P)).then_inc(gates_in, 16)
            sp.dma_start(log_temp[:, :], dram["log_temp"].partition_broadcast(P)).then_inc(gates_in, 16)
            sp.dma_start(map_rows[:, :], dram["fm_wT"]).then_inc(map_in, 16)
            sp.dma_start(bias_b[:, :], dram["fm_b"]).then_inc(map_in, 16)
            load(1, 1)
            sp.dma_start(fc_bias[:, :], dram["fc_b"].partition_broadcast(P)).then_inc(weights_in, 16)
            for i in range(2):
                sp.dma_start(fc_w[i][:, :, :], dram["fc_wT"][i * D:i * D + D, :].rearrange("(g p) d -> p g d", p=P)
                             ).then_inc(weights_in, 16)
            sp.dma_start(router_w[:, :, :], dram["gate_queryT"].rearrange("(k p) e -> p k e", p=P)
                         ).then_inc(weights_in, 16)
            load(2, 0)
            load(3, 1)
            store(0, 0)
            with sp.Fori(2, B - 3, 2) as i:
                load(i + 2, 0)
                store(i - 1, 1)
                load(i + 3, 1)
                store(i, 0)
            for b in range(B - 3, B):
                store(b, b % 2)
            for p in range(2):
                sp.wait_ge(x1_stored[p], 16 * B // 2)

        @block.gpsimd
        def _(pool):
            pool.memset(ident[:, :], 0.0).then_inc(zeroed, 1)
            pool.wait_ge(zeroed, 1)
            pool.affine_select(out=ident[:, :], in_=ident[:, :], compare_op=ALU.not_equal, fill=1.0, base=0,
                               pattern=[[-1, P]], channel_multiplier=1).then_inc(made, 1)
            pool.iota(sign_bits[:, :], [[0, 1]], base=0, channel_multiplier=1).then_inc(made, 1)
            pool.iota(block_no[:, :], [[1, 2 * HG]], base=0, channel_multiplier=0,
                      allow_small_or_imprecise_dtypes=True).then_inc(made, 1)
            pool.memset(eps[:, :], EPS).then_inc(zeroed, 1)
            pool.memset(neg_half[:, :], -0.5).then_inc(made, 1)
            pool.wait_ge(made, 4)
            pool.wait_ge(zeroed, 2)

            def inv_std1(b):
                pool.wait_ge(stats1_done, b + 1)
                pool.tensor_tensor(var_eps1[:, :], mean_var1[:, :, 1], eps[:, 0:T], ALU.add).then_inc(var1_done, 1)
                pool.wait_ge(var1_done, b + 1)
                pool.tensor_tensor(rstd1[:, :], var_eps1[:, :], neg_half[:, 0:T], ALU.pow).then_inc(rstd1_done, 1)

            def inv_std2(b, t):
                n = T * b + t + 1
                pool.wait_ge(stats2_done, n)
                pool.tensor_tensor(var_eps2[:, :], mean_var2[t][:, 1:2], eps[:, 0:1], ALU.add).then_inc(var2_done, 1)
                pool.wait_ge(var2_done, n)
                pool.tensor_tensor(rstd2[t][:, :], var_eps2[:, :], neg_half[:, 0:1], ALU.pow).then_inc(rstd2_done, 1)

            def add_bias(b, p):
                pool.wait_ge(x_loaded[p], 16 * b + 32 - 16 * p)
                if not (isinstance(b, int) and b < 2):
                    pool.wait_ge(x1_done, T * (b - 1))
                for t in range(T):
                    ins = pool.tensor_tensor(x_bias[p][:, t, :], x_in[p][:, t, :], fc_bias[:, :], ALU.add)
                ins.then_inc(x_bias_done, 1)

            def block_keys(b, p, g):
                for f, block, done in ((f_hi, k_hi, f_hi_done), (f_lo, k_lo, f_lo_done)):
                    pool.wait_ge(done, G * b + g + 1)
                    if f is f_hi and not (isinstance(b, int) and b < 2):
                        pool.wait_ge(scored, UNITS * (b - 1))
                    pool.tensor_tensor(
                        block[p][:, g, :].rearrange("p (h k) -> p h k", h=HG),
                        f[p][:, g, N:].bitcast(F32).rearrange("p (h k) -> p h k", h=1).to_broadcast([P, HG, KC]),
                        head_mask[:, :].rearrange("p (h k) -> p h k", k=1).to_broadcast([P, HG, KC]),
                        ALU.mult).then_inc(k_block_done, 1)

            def keep_x2(b, t):
                pool.wait_ge(x2_done, T * b + t + 1)
                pool.tensor_copy(x2_all[:, bass.ds(T * b + t, 1), :], x2[t][:, :].rearrange("p (a d) -> p a d", a=1)
                                 ).then_inc(x2_kept, 1)

            inv_std1(0)
            for g in range(G):
                block_keys(0, 0, g)
            pool.wait_ge(weights_hi, 3)
            for i in range(2):
                pool.tensor_tensor(fc_lo[:, 2 * i:2 * i + 2, :], fc_w[i][:, :, :],
                                   fc_hi[:, 2 * i:2 * i + 2, :].bitcast(F32), ALU.subtract).then_inc(fc_lo_done, 1)
            pool.wait_ge(dve_const, 3)
            add_bias(0, 0)

            def batch(b, p):
                first, last = isinstance(b, int) and b == 0, isinstance(b, int) and b == B - 1
                if not last:
                    inv_std1(b + 1)
                if not first:
                    inv_std2(b - 1, 0)
                    keep_x2(b - 1, 0)
                    inv_std2(b - 1, 1)
                if not last:
                    for g in range(3):
                        block_keys(b + 1, 1 - p, g)
                if not first:
                    keep_x2(b - 1, 1)
                if not last:
                    block_keys(b + 1, 1 - p, 3)
                    add_bias(b + 1, 1 - p)

            over_batches(pool, batch)
            for t in range(T):
                inv_std2(B - 1, t)
                keep_x2(B - 1, t)

        @block.scalar
        def _(act):
            act.wait_ge(gates_in, 3 * 16)
            act.activation(tanh_x[:, :], gate_in[:, 0:1], ACT.Tanh).then_inc(act_const, 1)
            act.activation(keep["tanh_f"][:, :], gate_in[:, 1:2], ACT.Tanh)
            act.preload_act_table_set("natural_log_exp_and_others")
            act.activation(inv_temp[:, :], log_temp[:, :], ACT.Exp, scale=-1.0).then_inc(act_const, 1)
            act.wait_ge(dve_const, 2)

            def exponent(s, b):
                u = UNITS * b + s
                act.wait_ge(shifted, u + 1)
                act.activation(prob[s % 4][:, :], prob[s % 4][:, :], ACT.Exp, scale=SCALE).then_inc(exp_done, 1)

            def copy_turned(s, b):
                u = UNITS * b + s
                act.wait_ge(turned, u + 1)
                if not (isinstance(b, int) and u < 2):
                    act.wait_ge(valued, u - 1)
                act.activation(probT[s % 2][:, :], probT_ps[s % 2][0:KC, :], ACT.Copy).then_inc(turned_out, 1)

            def empty_a(step, part, b, q):
                act.wait_ge(a_filled, use_a(step, part, b) + 1)
                bank = a_bank(step, part, b)
                if step == "cT":
                    ins = act.activation(xcT[:, :, N:], bank[:, 0:KD * KC].rearrange("p (k c) -> p k c", k=KD),
                                         ACT.Copy)
                elif step == "xnT":
                    ins = act.activation(xcT[:, :, 0:N], bank[:, :].rearrange("p (k n) -> p k n", k=KD), ACT.Copy)
                elif step == "z":
                    ins = act.activation(feat[:, part, :], bank[:, 0:N + KC], ACT.Exp,
                                         bias=sign_bias[:, :], scale=sign[:, :])
                elif step == "oT":
                    ins = act.activation(attnT[:, :], bank[:, :], ACT.Copy)
                else:
                    ins = act.activation(x2T[:, :], bank[:, 0:KD * P], ACT.Copy)
                ins.then_inc(a_emptied, 1)

            def take_values(b, q):
                act.wait_ge(b_filled, use_b("v", 0, b) + 1)
                act.activation(v_one[q][:, :, 0:EXP], bank_b[0:KC, :].rearrange("p (h e) -> p h e", e=EXP), ACT.Copy
                               ).then_inc(b_emptied, 1)

            def split_hi(step, part, b, q):
                if step in ("z", "xnT", "oT"):
                    act.wait_ge(a_emptied, use_a(step, part, b) + 1)
                if step == "z":
                    act.activation(f_hi[q][:, part, :], feat[:, part, :], ACT.Copy).then_inc(f_hi_done, 1)
                elif step == "xnT":
                    act.activation(xc_hi[:, :, :], xcT[:, :, :], ACT.Copy).then_inc(xc_hi_done, 1)
                elif step == "oT":
                    act.activation(attn_hi[:, :], attnT[:, :], ACT.Copy).then_inc(attn_hi_done, 1)

            act.wait_ge(blocks_made, 1)
            act.activation(block_hi[:, :, :], block_w[:, :, :], ACT.Copy).then_inc(weights_hi, 1)
            for step, part in A_PROLOGUE:
                empty_a(step, part, 0, 0)
                split_hi(step, part, 0, 0)
            take_values(0, 0)
            exponent(0, 0)
            act.wait_ge(weights_in, 4 * 16)
            for i in range(2):
                act.activation(fc_hi[:, 2 * i:2 * i + 2, :], fc_w[i][:, :, :], ACT.Copy).then_inc(weights_hi, 1)

            def batch(b, p):
                for s in range(UNITS):
                    early, late = in_slot(A_STEPS, b, s), in_slot(A_STEPS, b, s + 0.5)
                    if s == 0 and not (isinstance(b, int) and b == 0):
                        take_values(b, p)
                    for step, part, offset in early:
                        empty_a(step, part, b + offset, (p + offset) % 2)
                    if s < UNITS - 1:
                        exponent(s + 1, b)
                    elif not (isinstance(b, int) and b == B - 1):
                        exponent(0, b + 1)
                    copy_turned(s, b)
                    for step, part, offset in early:
                        split_hi(step, part, b + offset, (p + offset) % 2)
                    for step, part, offset in late:
                        empty_a(step, part, b + offset, (p + offset) % 2)
                        split_hi(step, part, b + offset, (p + offset) % 2)

            over_batches(act, batch)
            for _, step, part, _ in kept(A_STEPS, B):
                empty_a(step, part, B - 1, 1)
                split_hi(step, part, B - 1, 1)

        @block.tensor
        def _(pe):
            def scores(s, b, p):
                u, g, t = UNITS * b + s, s % G, s // G
                if not (isinstance(b, int) and u < 2):
                    pe.wait_ge(shifted, u - 1)
                if t == 0:
                    pe.wait_ge(k_block_done, 2 * (G * b + g + 1))
                for n, (q, k) in enumerate(((f_hi, k_hi), (f_hi, k_lo), (f_lo, k_hi))):
                    ins = pe.matmul(score_ps[s % 2][:, 0:HG * KC], q[p][:, g, t * P:t * P + P], k[p][:, g, :],
                                    start=(n == 0), stop=(n == 2))
                ins.then_inc(scored, 1)

            def turn(s, b):
                u = UNITS * b + s
                pe.wait_ge(exp_done, u + 1)
                if not (isinstance(b, int) and u < 2):
                    pe.wait_ge(turned_out, u - 1)
                for h in range(HG):
                    ins = pe.transpose(probT_ps[s % 2][0:KC, h * P:h * P + P],
                                       prob[s % 4][:, h * KC:h * KC + KC], ident[:, :])
                ins.then_inc(turned, 1)

            def values(s, b, p):
                u, g = UNITS * b + s, s % G
                pe.wait_ge(turned_out, u + 1)
                if not (isinstance(b, int) and u < 2):
                    pe.wait_ge(normed, u - 1)
                if s == 0:
                    pe.wait_ge(b_emptied, use_b("v", 0, b) + 1)
                for h in range(HG):
                    ins = pe.matmul(value_ps[s % 2][:, h * (EXP + 1):(h + 1) * (EXP + 1)],
                                    probT[s % 2][:, h * P:h * P + P], v_one[p][:, HG * g + h, :],
                                    start=True, stop=True)
                ins.then_inc(valued, 1)

            def fill_a(step, part, b, q):
                n = use_a(step, part, b)
                bank = a_bank(step, part, b)
                if not (isinstance(n, int) and n < len(A_PROLOGUE)):
                    pe.wait_ge(a_emptied, n)
                if step == "cT":
                    pe.wait_ge(x_loaded[q], 16 * b + 32 - 16 * q)
                    for k in range(KD):
                        ins = pe.transpose(bank[:, k * KC:k * KC + KC], ctx_in[q][:, k * P:k * P + P],
                                           ident[0:KC, 0:KC])
                elif step == "xnT":
                    pe.wait_ge(xn_done, b + 1)
                    for k in range(KD):
                        for t in range(T):
                            ins = pe.transpose(bank[:, k * N + t * P:k * N + t * P + P],
                                               xn[:, t, k * P:k * P + P], ident[:, :])
                elif step == "z":
                    k, w = part // 2, part % 2
                    if part == 0:
                        pe.wait_ge(xc_lo_done, b + 1)
                    for n, (m, x) in enumerate(((block_hi, xc_hi), (block_hi, xc_lo), (block_lo, xc_hi))):
                        ins = pe.matmul(bank[:, 0:N + KC], m[:, w, :], x[:, k, :], start=(n == 0), stop=(n == 2))
                elif step == "oT":
                    pe.wait_ge(normed, UNITS * b + G * (part + 1))
                    for g in range(G):
                        ins = pe.transpose(bank[:, g * P:g * P + P], attn[part][:, g * P:g * P + P], ident[:, :])
                else:
                    pe.wait_ge(x2_done, T * b + part + 1)
                    for k in range(KD):
                        ins = pe.transpose(bank[:, k * P:k * P + P], x2[part][:, k * P:k * P + P], ident[:, :])
                ins.then_inc(a_filled, 1)

            def fill_b(step, part, b, q):
                n = use_b(step, part, b)
                if not (isinstance(n, int) and n == 0):
                    pe.wait_ge(b_emptied, n)
                if step == "v":
                    pe.wait_ge(a_emptied, use_a("z", G - 1, b) + 1)
                    for g in range(G):
                        ins = pe.transpose(bank_b[0:KC, g * P:g * P + P], feat[:, g, N:], ident[:, :])
                elif step == "fc":
                    if isinstance(b, int) and b == 0 and part == 0:
                        pe.wait_ge(weights_in, 4 * 16)
                        pe.wait_ge(fc_lo_done, 2)
                    pe.wait_ge(attn_lo_done, T * b + part + 1)
                    for g in range(G):
                        for n, (x, m) in enumerate(((attn_hi, fc_hi), (attn_hi, fc_lo), (attn_lo, fc_hi))):
                            ins = pe.matmul(bank_b[:, 0:D], x[:, g * P:g * P + P], m[:, g, :],
                                            start=(g == 0 and n == 0), stop=(g == G - 1 and n == 2))
                else:
                    pe.wait_ge(a_emptied, use_a("x2T", part, b) + 1)
                    for k in range(KD):
                        ins = pe.matmul(bank_b[:, 0:E], x2T[:, k * P:k * P + P], router_w[:, k, :],
                                        start=(k == 0), stop=(k == KD - 1))
                ins.then_inc(b_filled, 1)

            pe.wait_ge(made, 4)
            pe.wait_ge(masks_made, 1 + HG + 2)
            for step, part in A_PROLOGUE:
                if (step, part) == ("z", 0):
                    pe.wait_ge(block_lo_done, 1)
                fill_a(step, part, 0, 0)
            fill_b("v", 0, 0, 0)
            scores(0, 0, 0)
            scores(1, 0, 0)

            def batch(b, p):
                first, last = isinstance(b, int) and b == 0, isinstance(b, int) and b == B - 1
                for s in range(UNITS):
                    if s < UNITS - 2:
                        scores(s + 2, b, p)
                    elif not last:
                        scores(s + 2 - UNITS, b + 1, 1 - p)
                    turn(s, b)
                    for step, part, offset in in_slot(A_STEPS, b, s):
                        fill_a(step, part, b + offset, (p + offset) % 2)
                    if s > 0:
                        values(s - 1, b, p)
                    elif not first:
                        values(UNITS - 1, b - 1, 1 - p)
                    for step, part, offset in in_slot(B_STEPS, b, s):
                        fill_b(step, part, b + offset, (p + offset) % 2)
                    for step, part, offset in in_slot(A_STEPS, b, s + 0.5):
                        fill_a(step, part, b + offset, (p + offset) % 2)

            over_batches(pe, batch)
            values(UNITS - 1, B - 1, 1)
            for s in range(UNITS):
                for step, part, _ in in_slot(A_STEPS, B, s):
                    fill_a(step, part, B - 1, 1)
                for step, part, _ in in_slot(B_STEPS, B, s):
                    fill_b(step, part, B - 1, 1)

        @block.vector
        def _(dve):
            def stats(b, p):
                dve.wait_ge(x_loaded[p], 16 * b + 32 - 16 * p)
                for t in range(T):
                    dve.bn_stats(stat1[:, t, :], x_in[p][:, t, :]).then_inc(stats1_raw, 1)
                dve.wait_ge(stats1_raw, 1 + T * b + T)
                dve.memset(keep["wait_carrier"][:, :], 0.0)
                for t in range(T):
                    ins = dve.bn_aggr(mean_var1[:, t, :], stat1[:, t, :])
                ins.then_inc(stats1_done, 1)

            def norm_x(b, p):
                dve.wait_ge(rstd1_done, b + 1)
                for t in range(T):
                    ins = dve.tensor_scalar(xn[:, t, :], x_in[p][:, t, :], mean_var1[:, t, 0:1], rstd1[:, t:t + 1],
                                            ALU.subtract, ALU.mult)
                ins.then_inc(xn_done, 1)

            def shift(s, b):
                u = UNITS * b + s
                tile = score_ps[s % 2][:, 0:HG * KC].rearrange("p (h k) -> p h k", h=HG)
                dve.wait_ge(scored, u + 1)
                dve.tensor_reduce(row_max[s % 2][:, :], tile, AX, ALU.max).then_inc(max_done, 1)
                dve.wait_ge(max_done, u + 1)
                if not (isinstance(b, int) and u < 4):
                    dve.wait_ge(turned, u - 3)
                dve.tensor_tensor(prob[s % 4][:, :].rearrange("p (h k) -> p h k", h=HG), tile,
                                  row_max[s % 2][:, :].rearrange("p (h k) -> p h k", k=1).to_broadcast([P, HG, KC]),
                                  ALU.subtract).then_inc(shifted, 1)

            def normalise(s, b):
                u, g, t = UNITS * b + s, s % G, s // G
                tile = value_ps[s % 2][:, 0:HG * (EXP + 1)].rearrange("p (h e) -> p h e", h=HG)
                dve.wait_ge(valued, u + 1)
                dve.reciprocal(recip[s % 2][:, :].rearrange("p (h k) -> p h k", k=1), tile[:, :, EXP:EXP + 1]
                               ).then_inc(recip_done, 1)
                dve.wait_ge(recip_done, u + 1)
                dve.tensor_tensor(attn[t][:, g * P:g * P + P].rearrange("p (h e) -> p h e", h=HG), tile[:, :, 0:EXP],
                                  recip[s % 2][:, :].rearrange("p (h k) -> p h k", k=1).to_broadcast([P, HG, EXP]),
                                  ALU.mult).then_inc(normed, 1)

            def empty_b(step, part, b, q):
                dve.wait_ge(b_filled, use_b(step, part, b) + 1)
                if step == "logits":
                    dve.tensor_scalar(logits[:, part, bass.ds(b, 1), :],
                                      bank_b[:, 0:E].rearrange("p (a e) -> p a e", a=1), inv_temp[:, 0:1], None,
                                      ALU.mult).then_inc(b_emptied, 1)
                else:
                    n = T * b + part + 1
                    dve.wait_ge(x_bias_done, b + 1)
                    if part == 0 and not (isinstance(b, int) and b < 2):
                        dve.wait_ge(x1_stored[q], 8 * b - 8 * q)
                    dve.scalar_tensor_tensor(x1_out[q][:, part, :], bank_b[:, 0:D], tanh_x[:, 0:1],
                                             x_bias[q][:, part, :], ALU.mult, ALU.add).then_inc(b_emptied, 1)
                    dve.wait_ge(b_emptied, use_b(step, part, b) + 1)
                    dve.bn_stats(stat2[:, :], x1_out[q][:, part, :]).then_inc(x1_done, 1)
                    dve.wait_ge(x1_done, n)
                    dve.memset(keep["wait_carrier"][:, :], 0.0)
                    dve.bn_aggr(mean_var2[part][:, :], stat2[:, :]).then_inc(stats2_done, 1)

            def norm_x2(b, t, q):
                n = T * b + t + 1
                dve.wait_ge(rstd2_done, n)
                if not (isinstance(b, int) and b == 0):
                    dve.wait_ge(x2_kept, n - T)
                    dve.wait_ge(a_filled, use_a("x2T", t, b - 1) + 1)
                dve.tensor_scalar(x2[t][:, :], x1_out[q][:, t, :], mean_var2[t][:, 0:1], rstd2[t][:, 0:1],
                                  ALU.subtract, ALU.mult).then_inc(x2_done, 1)

            def split_attention(b, t):
                n = T * b + t + 1
                dve.wait_ge(attn_hi_done, n)
                dve.tensor_tensor(attn_lo[:, :], attnT[:, :], attn_hi[:, :].bitcast(F32), ALU.subtract
                                  ).then_inc(attn_lo_done, 1)

            def split_inputs(b):
                dve.wait_ge(xc_hi_done, b + 1)
                dve.tensor_tensor(xc_lo[:, :, :], xcT[:, :, :], xc_hi[:, :, :].bitcast(F32), ALU.subtract
                                  ).then_inc(xc_lo_done, 1)

            def split_features(b, g, p):
                dve.wait_ge(f_hi_done, G * b + g + 1)
                dve.tensor_tensor(f_lo[p][:, g, :], feat[:, g, :], f_hi[p][:, g, :].bitcast(F32), ALU.subtract
                                  ).then_inc(f_lo_done, 1)

            dve.memset(head_mask[:, :], 0.0).then_inc(masks_made, 1)
            dve.wait_ge(masks_made, 1)
            for h in range(HG):
                dve.memset(head_mask[EXP * h:EXP * h + EXP, h:h + 1], 1.0).then_inc(masks_made, 1)
            for p in range(2):
                dve.memset(v_one[p][:, :, EXP:EXP + 1], 1.0).then_inc(masks_made, 1)
            dve.wait_ge(made, 4)
            dve.tensor_scalar(row_bits[:, :], sign_bits[:, :], 4, 2 * HG - 1, ALU.logical_shift_right, ALU.bitwise_and
                              ).then_inc(row_done, 1)
            dve.wait_ge(row_done, 1)
            dve.tensor_scalar(row_block[:, :], row_bits[:, :], 1.0, 0.0, ALU.mult, ALU.add).then_inc(row_done, 1)
            dve.wait_ge(row_done, 2)
            dve.tensor_scalar(block_mask[:, :], block_no[:, :], row_block[:, 0:1], None, ALU.is_equal
                              ).then_inc(mask_done, 1)
            dve.tensor_scalar(sign_bits[:, :], sign_bits[:, :], 4, 1, ALU.logical_shift_right, ALU.bitwise_and
                              ).then_inc(stats1_raw, 1)
            dve.wait_ge(stats1_raw, 1)
            dve.tensor_scalar(sign[:, :], sign_bits[:, :], -2.0, 1.0, ALU.mult, ALU.add).then_inc(dve_const, 1)
            dve.wait_ge(dve_const, 1)
            stats(0, 0)
            norm_x(0, 0)
            dve.wait_ge(map_in, 2 * 16)
            dve.wait_ge(mask_done, 1)
            blocks = [P, 2 * HG, 2, HD]
            dve.tensor_tensor(block_w[:, :, :].rearrange("p w (h s e) -> p (w h) s e", h=HG, s=2),
                              map_rows[:, :].rearrange("p (j s e) -> p j s e", j=1, s=1).to_broadcast(blocks),
                              block_mask[:, :].rearrange("p (j s e) -> p j s e", s=1, e=1).to_broadcast(blocks),
                              ALU.mult).then_inc(blocks_made, 1)
            dve.tensor_tensor(sign_bias[:, :], bias_b[:, :], sign[:, :], ALU.mult).then_inc(dve_const, 1)
            dve.wait_ge(weights_hi, 1)
            dve.tensor_tensor(block_lo[:, :, :], block_w[:, :, :], block_hi[:, :, :].bitcast(F32), ALU.subtract
                              ).then_inc(block_lo_done, 1)
            split_inputs(0)
            for g in range(G):
                split_features(0, g, 0)
            dve.wait_ge(act_const, 2)
            dve.wait_ge(weights_in, 4 * 16)
            dve.tensor_scalar(fc_bias[:, :], fc_bias[:, :], tanh_x[:, 0:1], None, ALU.mult).then_inc(dve_const, 1)
            shift(0, 0)

            def batch(b, p):
                first, last = isinstance(b, int) and b == 0, isinstance(b, int) and b == B - 1
                for s in range(UNITS):
                    if s < UNITS - 1:
                        shift(s + 1, b)
                    elif not last:
                        shift(0, b + 1)
                    if s in (0, 3) and not first:
                        split_attention(b - 1, s // 3)
                    if s == 3 and not last:
                        split_inputs(b + 1)
                    for step, part, offset in in_slot(B_STEPS, b, s - 1):
                        empty_b(step, part, b + offset, (p + offset) % 2)
                    if s > 1:
                        normalise(s - 2, b)
                    elif not first:
                        normalise(UNITS + s - 2, b - 1)
                    if s == 0 and not last:
                        stats(b + 1, 1 - p)
                    if s == 1 and not last:
                        norm_x(b + 1, 1 - p)
                    if s >= UNITS - G and not last:
                        split_features(b + 1, s - (UNITS - G), 1 - p)
                    if s == 3 and not first:
                        norm_x2(b - 1, 0, 1 - p)
                    if s == 5 and not first:
                        norm_x2(b - 1, 1, 1 - p)

            over_batches(dve, batch)
            split_attention(B - 1, 0)
            normalise(UNITS - 2, B - 1)
            normalise(UNITS - 1, B - 1)
            for _, step, part, _ in kept(B_STEPS, B):
                if step == "fc" and part > 0:
                    split_attention(B - 1, part)
                empty_b(step, part, B - 1, 1)
                if step == "fc":
                    norm_x2(B - 1, part, 1)



def route(nc, dram, keep, arena):
    with ExitStack() as ctx:
        def sb2(name, shape, dt=F32):
            return [arena.take(f"{name}{h}", shape, dt) for h in range(2)]

        def sem(name):
            return ctx.enter_context(nc.semaphore(name))

        ident, logits = keep["ident"], keep["logits"]
        slot_index, slot_gate = keep["slot_index"], keep["slot_gate"]
        Q = T * HB
        over_e = sb2("over_e", [P, Q, E])
        over_e_max = sb2("over_e_max", [P, Q])
        over_e_exp = sb2("over_e_exp", [P, Q, E])
        over_e_sum = sb2("over_e_sum", [P, Q])
        over_e_log = sb2("over_e_log", [P, Q])
        over_e_out = sb2("over_e_out", [P, Q, E])
        neg_max = sb2("neg_max", [P, 1])
        over_n_exp = sb2("over_n_exp", [P, N])
        over_n_sum = sb2("over_n_sum", [P, 1])
        over_n_log = sb2("over_n_log", [P, 1])
        over_n = sb2("over_n", [P, N])
        affinity = sb2("affinity", [P, N])
        top = sb2("top", [P, CAP])
        top_at = sb2("top_at", [P, CAP], U32)
        top_twice = sb2("top_twice", [P, 2, CAP])
        at_twice = sb2("at_twice", [P, 2, CAP])
        to_n_ps = [ctx.enter_context(nc.psum_tensor(f"to_n_ps{h}", [P, 512], F32)) for h in range(2)]
        to_e_ps = [ctx.enter_context(nc.psum_tensor(f"to_e_ps{h}", [P, 512], F32)) for h in range(2)]
        slot_ps = [ctx.enter_context(nc.psum_tensor(f"slot_ps{h}", [P, 512], F32)) for h in range(2)]

        e_max, e_shift, e_exp, e_sum, e_log, e_done = (
            sem(n) for n in ("e_max", "e_shift", "e_exp", "e_sum", "e_log", "e_done"))
        in_n, n_max, n_exp, n_log, n_done, in_e = (
            sem(n) for n in ("in_n", "n_max", "n_exp", "n_log", "n_done", "in_e"))
        gates_done, topped, listed, slots_turned, slots_kept, index_out = (
            sem(n) for n in ("gates_done", "topped", "listed", "slots_turned", "slots_kept", "index_out"))

        block = ctx.enter_context(nc.Block())

        def groups(tile):
            return tile.rearrange("p (q e) -> p q e", e=E)

        def wide(small):
            return small.rearrange("p (q e) -> p q e", e=1).to_broadcast([P, Q, E])

        def over_rounds(eng, body):
            body(0)
            with eng.Fori(1, SINKHORN, 1) as i:
                body(i)

        @block.vector
        def _(dve):
            def body(i):
                for h in range(2):
                    n = 2 * i + h + 1
                    if isinstance(i, int):
                        for t in range(T):
                            ins = dve.tensor_reduce(over_e_max[h][:, HB * t:HB * t + HB],
                                                    logits[:, t, HB * h:HB * h + HB, :], AX, ALU.max)
                        ins.then_inc(e_max, 1)
                        dve.wait_ge(e_max, n)
                        for t in range(T):
                            ins = dve.tensor_tensor(
                                over_e[h][:, HB * t:HB * t + HB, :], logits[:, t, HB * h:HB * h + HB, :],
                                wide(over_e_max[h][:, :])[:, HB * t:HB * t + HB, :], ALU.subtract)
                        ins.then_inc(e_shift, 1)
                    else:
                        dve.wait_ge(in_e, n - 2)
                        src = groups(to_e_ps[h][:, 0:N])
                        dve.tensor_reduce(over_e_max[h][:, :], src, AX, ALU.max).then_inc(e_max, 1)
                        dve.wait_ge(e_max, n)
                        dve.tensor_tensor(over_e[h][:, :, :], src, wide(over_e_max[h][:, :]), ALU.subtract
                                          ).then_inc(e_shift, 1)
                for h in range(2):
                    n = 2 * i + h + 1
                    dve.wait_ge(e_exp, n)
                    dve.tensor_reduce(over_e_sum[h][:, :], over_e_exp[h][:, :, :], AX, ALU.add).then_inc(e_sum, 1)
                for h in range(2):
                    n = 2 * i + h + 1
                    dve.wait_ge(e_log, n)
                    dve.tensor_tensor(over_e_out[h][:, :, :], over_e[h][:, :, :], wide(over_e_log[h][:, :]),
                                      ALU.subtract).then_inc(e_done, 1)
                for h in range(2):
                    n = 2 * i + h + 1
                    dve.wait_ge(in_n, n)
                    dve.tensor_reduce(neg_max[h][:, :], to_n_ps[h][:, 0:N], AX, ALU.max, negate=True
                                      ).then_inc(n_max, 1)
                for h in range(2):
                    n = 2 * i + h + 1
                    dve.wait_ge(n_log, n)
                    dve.tensor_scalar(over_n[h][:, :], to_n_ps[h][:, 0:N], neg_max[h][:, 0:1], over_n_log[h][:, 0:1],
                                      ALU.add, ALU.subtract).then_inc(n_done, 1)

            over_rounds(dve, body)
            steps = 0
            dve.wait_ge(gates_done, 2)
            for r in range(CAP // 8):
                eight = slice(8 * r, 8 * r + 8)
                for h in range(2):
                    if r > 0:
                        dve.wait_ge(topped, steps - 1)
                    dve.max(top[h][:, eight], affinity[h][:, :]).then_inc(topped, 1)
                    steps += 1
                for h in range(2):
                    dve.wait_ge(topped, steps - 1 + h)
                    ins = dve.max_index(top_at[h][:, eight], top[h][:, eight], affinity[h][:, :])
                    if r < CAP // 8 - 1:
                        ins = dve.match_replace(affinity[h][:, :], top[h][:, eight], affinity[h][:, :], -1.0)
                    ins.then_inc(topped, 1)
                steps += 2
            dve.wait_ge(topped, steps)
            for h in range(2):
                dve.tensor_copy(at_twice[h][:, :, :], top_at[h][:, :].rearrange("p (a c) -> p a c", a=1)
                                .to_broadcast([P, 2, CAP])).then_inc(listed, 1)
                dve.tensor_copy(top_twice[h][:, :, :], top[h][:, :].rearrange("p (a c) -> p a c", a=1)
                                .to_broadcast([P, 2, CAP])).then_inc(listed, 1)
            for h in range(2):
                dve.wait_ge(slots_turned, h + 1)
                for k, table in enumerate((slot_index, slot_gate)):
                    for u in range(2):
                        half = slice(CAP * u, CAP * u + CAP)
                        for q in range(2):
                            batch, expert = (q, q ^ u) if table is slot_index else (q ^ u, q)
                            ins = dve.tensor_copy(
                                table[half, :, HB // 2 * h:HB // 2 * (h + 1)].rearrange(
                                    "p (i q) j -> p j i q", q=2)[:, :, :, q],
                                slot_ps[h][half, k * P:k * P + P].rearrange(
                                    "p (j r i q) -> p j r i q", r=2, q=2, i=E // 2)[:, :, batch, :, expert])
                ins.then_inc(slots_kept, 1)

        @block.scalar
        def _(act):
            def body(i):
                for h in range(2):
                    act.wait_ge(e_shift, 2 * i + h + 1)
                    act.activation(over_e_exp[h][:, :, :], over_e[h][:, :, :], ACT.Exp).then_inc(e_exp, 1)
                for h in range(2):
                    act.wait_ge(e_sum, 2 * i + h + 1)
                    act.activation(over_e_log[h][:, :], over_e_sum[h][:, :], ACT.Ln).then_inc(e_log, 1)
                for h in range(2):
                    n = 2 * i + h + 1
                    act.wait_ge(n_max, n)
                    act.activation(over_n_exp[h][:, :], to_n_ps[h][:, 0:N], ACT.Exp, bias=neg_max[h][:, :],
                                   accum_out=over_n_sum[h][:, :]).then_inc(n_exp, 1)
                    act.wait_ge(n_exp, n)
                    act.activation(over_n_log[h][:, :], over_n_sum[h][:, :], ACT.Ln).then_inc(n_log, 1)

            over_rounds(act, body)
            for h in range(2):
                act.wait_ge(n_done, 2 * SINKHORN - 1 + h)
                act.activation(affinity[h][:, :], over_n[h][:, :], ACT.Exp).then_inc(gates_done, 1)

        @block.tensor
        def _(pe):
            def body(i):
                for h in range(2):
                    pe.wait_ge(e_done, 2 * i + h + 1)
                    flat = over_e_out[h][:, :, :].rearrange("p q e -> p (q e)")
                    for t in range(T):
                        ins = pe.transpose(to_n_ps[h][:, t * P:t * P + P], flat[:, t * P:t * P + P], ident[:, :])
                    ins.then_inc(in_n, 1)
                for h in range(2):
                    pe.wait_ge(n_done, 2 * i + h + 1)
                    for t in range(T):
                        ins = pe.transpose(to_e_ps[h][:, t * P:t * P + P], over_n[h][:, t * P:t * P + P], ident[:, :])
                    ins.then_inc(in_e, 1)

            over_rounds(pe, body)
            for h in range(2):
                pe.wait_ge(listed, 2 * h + 2)
                for k, twice in enumerate((at_twice, top_twice)):
                    ins = pe.transpose(slot_ps[h][:, k * P:k * P + P],
                                       twice[h][:, :, :].rearrange("p a c -> p (a c)"), ident[:, :])
                ins.then_inc(slots_turned, 1)

        @block.sync
        def _(sp):
            for h in range(2):
                sp.wait_ge(listed, 2 * h + 1)
                sp.dma_start(dram["slot_index"][h * P:h * P + P, :], at_twice[h][:, 0, :]).then_inc(index_out, 16)
            sp.wait_ge(index_out, 32)
            for b in range(2):
                load_index(sp, dram, keep, b, b)
            sp.wait_ge(slots_kept, 2)



def load_index(sp, dram, keep, b, p):
    sp.dma_start(keep["index_all"][p][:, :], dram["slot_index"].rearrange("(b e) c -> b (e c)", e=E)
                 [bass.ds(b, 1), :].to_broadcast([P, E * CAP])).then_inc(keep["index_in"][p], 16)


def gather(nc, dram, keep, arena):
    with ExitStack() as ctx:
        def sem(name):
            return ctx.enter_context(nc.semaphore(name))

        x2_all, expert_x = keep["x2_all"], keep["expert_x"]
        token_no = arena.take("token_no", [P, T])
        index_all, index_in = keep["index_all"], keep["index_in"]
        pick = [arena.take(f"pick{p}", [P, T, E * CAP], F32R) for p in range(2)]
        x_hi = [arena.take(f"x_hi{p}", [P, T, D], F32R) for p in range(2)]
        x_lo = [arena.take(f"x_lo{p}", [P, T, D], F32R) for p in range(2)]
        out_ps = [ctx.enter_context(nc.psum_tensor(f"gather_ps{i}", [P, 512], F32)) for i in range(8)]
        EC = E * CAP // 512
        EB = E // EC

        numbered = sem("numbered")
        picked, hi_done, lo_done, gathered = sem("picked"), sem("hi_done"), sem("lo_done"), sem("gathered")
        out_act, out_dve = sem("out_act"), sem("out_dve")

        block = ctx.enter_context(nc.Block())

        def early(b):
            return isinstance(b, int) and b < 2

        def over(eng, body):
            body(0, 0)
            body(1, 1)
            with eng.Fori(2, B - 1, 2) as i:
                body(i, 0)
                body(i + 1, 1)

        def home(c, b, p, k, q):
            at = b + q * (1 - 2 * p)
            return expert_x[:, EB * c:EB * c + EB, bass.ds(at, 1), k, :].rearrange(
                "p (i q) b c -> p i q (b c)", q=2)[:, :, q, :]

        def slots(bank, q):
            return out_ps[bank][:, :].rearrange("p (i q c) -> p i q c", q=2, c=CAP)[:, :, q, :]

        @block.gpsimd
        def _(pool):
            pool.iota(token_no[:, :], [[P, T]], base=0, channel_multiplier=1, allow_small_or_imprecise_dtypes=True
                      ).then_inc(numbered, 1)

        @block.sync
        def _(sp):
            def body(b, p):
                if early(b):
                    for m in range(2 * b, 2 * b + 2):
                        load_weights(sp, dram, keep, 0, m)
                else:
                    sp.wait_ge(picked, b - 1)
                    load_index(sp, dram, keep, b, p)
            over(sp, body)

        @block.scalar
        def _(act):
            def body(b, p):
                if not early(b):
                    act.wait_ge(gathered, KD * EC * (b - 1))
                act.activation(x_hi[p][:, :, :], x2_all[:, bass.ds(T * b, T), :], ACT.Copy).then_inc(hi_done, 1)
                if not (isinstance(b, int) and b == 0):
                    copy_out(b - 1, 1 - p)

            def copy_out(b, p):
                for k in range(KD):
                    act.wait_ge(gathered, KD * EC * b + EC * k + 1)
                    for q in range(2):
                        ins = act.activation(home(0, b, p, k, q), slots(4 * p + EC * k, q), ACT.Copy)
                    ins.then_inc(out_act, 1)

            over(act, body)
            copy_out(B - 1, 1)

        @block.vector
        def _(dve):
            dve.wait_ge(numbered, 1)

            def body(b, p):
                if not early(b):
                    dve.wait_ge(gathered, KD * EC * (b - 1))
                dve.wait_ge(hi_done, b + 1)
                dve.tensor_tensor(x_lo[p][:, :, :], x2_all[:, bass.ds(T * b, T), :], x_hi[p][:, :, :].bitcast(F32),
                                  ALU.subtract).then_inc(lo_done, 1)
                dve.wait_ge(index_in[p], 8 * b + 16 - 8 * p)
                for t in range(T):
                    ins = dve.tensor_scalar(pick[p][:, t, :], index_all[p][:, :], token_no[:, t:t + 1], None,
                                            ALU.is_equal)
                ins.then_inc(picked, 1)
                if not (isinstance(b, int) and b == 0):
                    copy_out(b - 1, 1 - p)

            def copy_out(b, p):
                for k in range(KD):
                    dve.wait_ge(gathered, KD * EC * b + EC * k + 2)
                    for q in range(2):
                        ins = dve.tensor_copy(home(1, b, p, k, q), slots(4 * p + EC * k + 1, q))
                    ins.then_inc(out_dve, 1)

            over(dve, body)
            copy_out(B - 1, 1)

        @block.tensor
        def _(pe):
            def body(b, p):
                pe.wait_ge(picked, b + 1)
                pe.wait_ge(lo_done, b + 1)
                for k in range(KD):
                    for c, out in enumerate((out_act, out_dve)):
                        if not early(b):
                            pe.wait_ge(out, KD * (b - 2) + k + 1)
                        for n, (t, part) in enumerate((t, part) for t in range(T) for part in (x_hi, x_lo)):
                            ins = pe.matmul(out_ps[4 * p + EC * k + c][:, :], part[p][:, t, k * P:k * P + P],
                                            pick[p][:, t, c * 512:c * 512 + 512], start=(n == 0), stop=(n == 2 * T - 1))
                        ins.then_inc(gathered, 1)
            over(pe, body)



def load_weights(sp, dram, keep, e, m):
    w_in, w_loaded = keep["w_in"][m % W_RING], keep["w_loaded"][m % W_RING]
    sp.dma_start(w_in[:, 0:D].rearrange("p (k f) -> p k f", k=KD),
                 dram["w1"][bass.ds(e * D, D), m * P:m * P + P].rearrange("(k p) f -> p k f", p=P)
                 ).then_inc(w_loaded, 16)
    sp.dma_start(w_in[:, D:2 * D], dram["w2"][bass.ds(e * FF + m * P, P), :]).then_inc(w_loaded, 16)


def experts(nc, dram, keep, arena):
    with ExitStack() as ctx:
        def sem(name):
            return ctx.enter_context(nc.semaphore(name))

        def bank(name):
            return ctx.enter_context(nc.psum_tensor(name, [P, 512], F32))

        expert_x, slot_gate = keep["expert_x"], keep["slot_gate"]
        expert_out = expert_x[:, :, :, :, :].rearrange("p e b k c -> p e (b k c)")
        HS = E * CAP // 2
        TS = HS // P
        HALF = KD * HS
        STEPS = 2 * M
        w_in, w_loaded = keep["w_in"], keep["w_loaded"]
        w_hi = arena.take("w_hi", [P, M, 2 * D], F32R)
        w_lo = arena.take("w_lo", [P, M, 2 * D], F32R)
        x_hi = [arena.take(f"ex_hi{h}", [P, KD, HS], F32R) for h in range(2)]
        x_lo = [arena.take(f"ex_lo{h}", [P, KD, HS], F32R) for h in range(2)]
        hidden = [arena.take(f"hidden{i}", [P, HS]) for i in range(2)]
        h_hi = [arena.take(f"h_hi{i}", [P, HS], F32R) for i in range(4)]
        h_lo = [arena.take(f"h_lo{i}", [P, HS], F32R) for i in range(4)]
        b1 = arena.take("b1", [P, E * M])
        b2 = arena.take("b2", [P, D])
        b1_now = [arena.take(f"b1_now{h}", [P, M]) for h in range(2)]
        hidden_ps = [bank(f"hidden_ps{i}") for i in range(4)]
        out_ps = [[bank(f"out_ps{h}{i}") for i in range(2)] for h in range(2)]

        b1_in, b2_in, b1_ready = sem("b1_in"), sem("b2_in"), sem("b1_ready")
        w_hi_done, w_done = sem("w_hi_done"), sem("w_done")
        ex_hi_done, ex_done = sem("ex_hi_done"), sem("ex_done")
        hidden_done, gelu_done = sem("hidden_done"), sem("gelu_done")
        h_hi_done, h_done = sem("h_hi_done"), sem("h_done")
        out_added, biased, out_done = sem("out_added"), sem("biased"), sem("out_done")

        block = ctx.enter_context(nc.Block())

        def over(eng, body):
            body(0, 0)
            with eng.Fori(1, E - 2, 2) as i:
                body(i, 1)
                body(i + 1, 0)
            body(E - 1, 1)

        def is0(e):
            return isinstance(e, int) and e == 0

        @block.sync
        def _(sp):
            sp.dma_start(b1[:, :], dram["b1"]).then_inc(b1_in, 16)

            def body(e, odd):
                for m in range(M):
                    if not (is0(e) and m < W_RING):
                        sp.wait_ge(w_done, M * e + m + 1 - W_RING)
                        load_weights(sp, dram, keep, e, m)
            over(sp, body)

        @block.gpsimd
        def _(pool):
            def body(e, odd):
                for m in range(M):
                    pool.wait_ge(w_hi_done, M * e + m + 1)
                    pool.tensor_tensor(w_lo[:, m, :], w_in[m % W_RING][:, :], w_hi[:, m, :].bitcast(F32), ALU.subtract
                                       ).then_inc(w_done, 1)
            over(pool, body)

        @block.scalar
        def _(act):
            def split_w_hi(e, m):
                act.wait_ge(w_loaded[m % W_RING], 32 * (M // W_RING) * e + 32 * (m // W_RING + 1))
                if not is0(e):
                    act.wait_ge(out_added, STEPS * (e - 1) + M + m + 1)
                act.activation(w_hi[:, m, :], w_in[m % W_RING][:, :], ACT.Copy).then_inc(w_hi_done, 1)

            for m in range(M // 2):
                split_w_hi(0, m)

            def body(e, odd):
                for k in range(STEPS):
                    if k < 3 and not is0(e):
                        split_w_hi(e, M - 3 + k)
                    if k >= M + 3 and not (isinstance(e, int) and e == E - 1):
                        split_w_hi(e + 1, k - M - 3)
                    if k % M == 0:
                        act.wait_ge(b1_ready, 2 * e + k // M + 1)
                    act.wait_ge(hidden_done, STEPS * e + k + 1)
                    if not (is0(e) and k < 2):
                        act.wait_ge(h_done, STEPS * e + k - 1)
                    act.activation(hidden[k % 2][:, :], hidden_ps[k % 4][:, :], ACT.Gelu_apprx_tanh,
                                   bias=b1_now[k // M][:, k % M:k % M + 1]).then_inc(gelu_done, 1)
                    if is0(e) and k < M // 2:
                        split_w_hi(e, M // 2 + k)
                    if k == 5:
                        if not is0(e):
                            act.wait_ge(out_done, 2 * e)
                        act.dma_start(b2[:, :], dram["b2"][bass.ds(e, 1), :].to_broadcast([P, D])
                                      ).then_inc(b2_in, 16)
            over(act, body)

        @block.vector
        def _(dve):
            def tokens(tile):
                return tile[:, :, :].rearrange("p k (b c) -> p k b c", c=CAP)

            def split_x_hi(e, h):
                src = expert_out[:, bass.ds(e, 1), h * HALF:(h + 1) * HALF].rearrange(
                    "p a (b k c) -> p (a k) b c", k=KD, c=CAP)
                dve.tensor_copy(tokens(x_hi[h]), src).then_inc(ex_hi_done, 1)

            def split_x_lo(e, h):
                src = expert_out[:, bass.ds(e, 1), h * HALF:(h + 1) * HALF].rearrange(
                    "p a (b k c) -> p (a k) b c", k=KD, c=CAP)
                dve.wait_ge(ex_hi_done, 2 * e + h + 1)
                dve.tensor_tensor(tokens(x_lo[h]), src, tokens(x_hi[h]).bitcast(F32), ALU.subtract
                                  ).then_inc(ex_done, 1)

            def split_hidden(e, k):
                q = STEPS * e + k
                dve.wait_ge(gelu_done, q + 1)
                if not (is0(e) and k < 4):
                    dve.wait_ge(out_added, q - 3)
                dve.tensor_copy(h_hi[k % 4][:, :], hidden[k % 2][:, :]).then_inc(h_hi_done, 1)
                dve.wait_ge(h_hi_done, q + 1)
                dve.tensor_tensor(h_lo[k % 4][:, :], hidden[k % 2][:, :], h_hi[k % 4][:, :].bitcast(F32), ALU.subtract
                                  ).then_inc(h_done, 1)

            def finish(e, h, odd, part):
                lower, upper = slice(0, CAP), slice(CAP, 2 * CAP)
                if part == 0 and odd:
                    dve.wait_ge(out_done, 2 * e + h - 1)
                    dve.tensor_copy(expert_out[upper, bass.ds(e, 1), h * HALF:(h + 1) * HALF],
                                    expert_out[upper, bass.ds(e - 1, 1), h * HALF:(h + 1) * HALF])
                if part == 0:
                    dve.wait_ge(out_added, STEPS * e + M * h + M)
                    dve.wait_ge(b2_in, 16 * e + 16)
                    for i in range(2):
                        tiles = out_ps[h][i][:, :].rearrange("p (t d) -> p t d", d=D)
                        dve.tensor_tensor(tiles, tiles, b2[:, :].rearrange("p (t d) -> p t d", t=1)
                                          .to_broadcast([P, 2, D]), ALU.add).then_inc(biased, 1)
                    return
                if part == 1:
                    dve.wait_ge(biased, 4 * e + 2 * h + 2)
                for t in range(2 * part - 2, 2 * part):
                    at = h * HALF + t * D
                    for rows, home in ((lower, e), (upper, e - 1)) if odd else ((slice(0, P), e),):
                        ins = dve.tensor_scalar(
                            expert_out[rows, bass.ds(home, 1), at:at + D].rearrange("p a d -> p (a d)"),
                            out_ps[h][t // 2][rows, t % 2 * D:t % 2 * D + D],
                            slot_gate[rows, bass.ds(e, 1), TS * h + t], None, ALU.mult)
                if part == 2:
                    ins.then_inc(out_done, 1)

            def take_b1(e, h):
                dve.tensor_copy(b1_now[h][:, :], b1[:, bass.ds(e * M, M)]).then_inc(b1_ready, 1)

            dve.wait_ge(b1_in, 16)
            take_b1(0, 0)
            split_x_hi(0, 0)
            split_x_lo(0, 0)

            def body(e, odd):
                for k in range(STEPS):
                    split_hidden(e, k)
                    if 1 <= k <= 3 and not is0(e):
                        finish(e - 1, 1, 1 - odd, k - 1)
                    if M + 1 <= k <= M + 3:
                        finish(e, 0, odd, k - M - 1)
                    if k == 4:
                        if not is0(e):
                            dve.wait_ge(hidden_done, STEPS * e)
                        split_x_hi(e, 1)
                    if k == 2:
                        take_b1(e, 1)
                    if k == 5:
                        split_x_lo(e, 1)
                    if not (isinstance(e, int) and e == E - 1):
                        if k == M + 2:
                            take_b1(e + 1, 0)
                        if k == M + 4:
                            dve.wait_ge(hidden_done, STEPS * e + M)
                            split_x_hi(e + 1, 0)
                        if k == M + 5:
                            split_x_lo(e + 1, 0)
            over(dve, body)
            for part in range(3):
                finish(E - 1, 1, 1, part)

        @block.tensor
        def _(pe):
            def hidden_step(e, k):
                q, h, m = STEPS * e + k, k // M, k % M
                if h == 0:
                    pe.wait_ge(w_done, M * e + m + 1)
                if m == 0:
                    pe.wait_ge(ex_done, 2 * e + h + 1)
                if not (is0(e) and k < 4):
                    pe.wait_ge(gelu_done, q - 3)
                for n, (d, w, x) in enumerate((d, w, x) for d in range(KD)
                                              for w, x in ((w_hi, x_hi), (w_hi, x_lo), (w_lo, x_hi))):
                    ins = pe.matmul(hidden_ps[k % 4][:, :], w[:, m, d * P:d * P + P], x[h][:, d, :],
                                    start=(n == 0), stop=(n == 3 * KD - 1))
                ins.then_inc(hidden_done, 1)

            def out_step(e, k):
                q, h, m = STEPS * e + k, k // M, k % M
                pe.wait_ge(h_done, q + 1)
                if m == 0 and not is0(e):
                    pe.wait_ge(out_done, 2 * e + h - 1)
                for t in range(TS):
                    for n, (x, w) in enumerate(((h_hi, w_hi), (h_hi, w_lo), (h_lo, w_hi))):
                        ins = pe.matmul(out_ps[h][t // 2][:, (t % 2) * D:(t % 2) * D + D],
                                        x[k % 4][:, t * P:t * P + P], w[:, m, D:2 * D],
                                        start=(m == 0 and n == 0 and t % 2 == 0), stop=(m == M - 1 and n == 2),
                                        skip_group_check=True)
                ins.then_inc(out_added, 1)

            def body(e, odd):
                for k in range(STEPS):
                    hidden_step(e, k)
                    if k >= 2:
                        out_step(e, k - 2)
                    elif not is0(e):
                        out_step(e - 1, STEPS + k - 2)
            over(pe, body)
            out_step(E - 1, STEPS - 2)
            out_step(E - 1, STEPS - 1)



def scatter(nc, dram, keep, arena):
    with ExitStack() as ctx:
        def sem(name):
            return ctx.enter_context(nc.semaphore(name))

        expert_out = keep["expert_x"][:, :, :, :, :].rearrange("p e b k c -> p e (b k c)")
        slot_index, tanh_f = keep["slot_index"], keep["tanh_f"]
        V = 4
        EQ = E // V
        column_no = arena.take("column_no", [P, N])
        out_hi = [arena.take(f"out_hi{v}", [P, EQ, D], F32R) for v in range(V)]
        out_lo = [arena.take(f"out_lo{v}", [P, EQ, D], F32R) for v in range(V)]
        place = [arena.take(f"place{v}", [P, EQ, N], F32R) for v in range(V)]
        x1 = [arena.take(f"x1_back{p}", [P, 2 * T, D]) for p in range(2)]
        sum_ps = [[ctx.enter_context(nc.psum_tensor(f"sum_ps{p}{i}", [P, 512], F32)) for i in range(2 * T)]
                  for p in range(2)]

        numbered, split_hi, split_dve, split_pool = (
            sem(n) for n in ("columns_numbered", "split_hi", "split_dve", "split_pool"))
        placed, summed, out_ready = sem("placed"), sem("summed"), sem("out_ready")
        x1_in = [sem(f"x1_in{p}") for p in range(2)]
        stored = [sem(f"stored{p}") for p in range(2)]

        block = ctx.enter_context(nc.Block())
        PAIRS = B // 2

        def over(eng, body):
            body(0, 0)
            with eng.Fori(1, PAIRS - 1, 2) as i:
                body(i, 1)
                body(i + 1, 0)
            body(PAIRS - 1, 1)

        def is0(j):
            return isinstance(j, int) and j == 0

        def quarter(j, v):
            return expert_out[:, EQ * v:EQ * v + EQ, bass.ds(j * D, D)]

        @block.gpsimd
        def _(pool):
            pool.iota(column_no[:, :], [[1, N]], base=0, channel_multiplier=0, allow_small_or_imprecise_dtypes=True
                      ).then_inc(numbered, 1)

            def body(j, p):
                for v in range(1, V):
                    if not is0(j):
                        pool.wait_ge(summed, V * (j - 1) + v + 1)
                    pool.wait_ge(split_hi, V * j + v + 1)
                    pool.tensor_tensor(out_lo[v][:, :, :], quarter(j, v), out_hi[v][:, :, :].bitcast(F32),
                                       ALU.subtract).then_inc(split_pool, 1)
            over(pool, body)

        @block.sync
        def _(sp):
            def load(j, p, wait):
                if wait:
                    sp.wait_ge(stored[p], 8 * j - 8 * p)
                sp.dma_start(x1[p][:, :, :].rearrange("p (r t) d -> p r (t d)", r=2),
                             dram["x1"][bass.ds(2 * j * P, 2 * P), :].rearrange("(r p) n -> p r n", p=P)
                             ).then_inc(x1_in[p], 16)

            def store(j, p):
                sp.wait_ge(out_ready, j + 1)
                sp.dma_start(dram["out"][bass.ds(2 * j * N, 2 * N), :].rearrange("(r p) d -> p r d", p=P),
                             x1[p][:, :, :]).then_inc(stored[p], 16)

            load(0, 0, False)
            load(1, 1, False)
            store(0, 0)
            with sp.Fori(2, PAIRS - 1, 2) as i:
                load(i, 0, True)
                store(i - 1, 1)
                load(i + 1, 1, True)
                store(i, 0)
            store(PAIRS - 1, 1)
            for p in range(2):
                sp.wait_ge(stored[p], 16 * PAIRS // 2)

        @block.scalar
        def _(act):
            def body(j, p):
                for v in range(V):
                    if not is0(j):
                        act.wait_ge(summed, V * (j - 1) + v + 1)
                    act.activation(out_hi[v][:, :, :], quarter(j, v), ACT.Copy).then_inc(split_hi, 1)
            over(act, body)

        @block.vector
        def _(dve):
            dve.wait_ge(numbered, 1)

            def find_places(j, v):
                if not is0(j):
                    dve.wait_ge(summed, V * (j - 1) + v + 1)
                for e in range(EQ):
                    ins = dve.tensor_scalar(place[v][:, e, :], column_no[:, :],
                                            slot_index[:, EQ * v + e, bass.ds(j, 1)], None, ALU.is_equal)
                ins.then_inc(placed, 1)
                if v == 0:
                    dve.wait_ge(split_hi, V * j + 1)
                    dve.tensor_tensor(out_lo[0][:, :, :], quarter(j, 0), out_hi[0][:, :, :].bitcast(F32), ALU.subtract
                                      ).then_inc(split_dve, 1)

            def finish(j, p):
                dve.wait_ge(summed, V * j + V)
                dve.wait_ge(x1_in[p], 8 * j + 16 - 8 * p)
                for i in range(2 * T):
                    ins = dve.scalar_tensor_tensor(x1[p][:, i, :], sum_ps[p][i][:, 0:D], tanh_f[:, 0:1], x1[p][:, i, :],
                                                   ALU.mult, ALU.add)
                ins.then_inc(out_ready, 1)

            def body(j, p):
                for v in range(V):
                    find_places(j, v)
                    if v == 1 and not is0(j):
                        finish(j - 1, 1 - p)
            over(dve, body)
            finish(PAIRS - 1, 1)

        @block.tensor
        def _(pe):
            def body(j, p):
                for v in range(V):
                    pe.wait_ge(placed, V * j + v + 1)
                    if v == 0:
                        pe.wait_ge(split_dve, j + 1)
                    else:
                        pe.wait_ge(split_pool, (V - 1) * j + v)
                    if v == 0 and not (isinstance(j, int) and j < 2):
                        pe.wait_ge(out_ready, j - 1)
                    for e in range(EQ):
                        for n, part in enumerate((out_hi, out_lo)):
                            for t in range(T):
                                ins = pe.matmul(sum_ps[p][T * (e % 2) + t][:, 0:D], place[v][:, e, t * P:t * P + P],
                                                part[v][:, e, :], start=(v == 0 and e < 2 and n == 0),
                                                stop=(v == V - 1 and e >= EQ - 2 and n == 1))
                    ins.then_inc(summed, 1)
            over(pe, body)


def flamingo_layer(nc, dram):
    start = nc.sbuf_base + -nc.sbuf_base % 32
    end = nc.sbuf_usable_end
    with ExitStack() as ctx:
        tables = Arena(nc, start, end)
        keep = {
            "ident": tables.take("ident", [P, P]),
            "slot_index": tables.take("slot_index_sb", [P, E, B // 2]),
            "slot_gate": tables.take("slot_gate", [P, E, B // 2]),
            "tanh_f": tables.take("tanh_f", [P, 1]),
            "wait_carrier": tables.take("wait_carrier", [P, 1]),
        }
        middle = tables.at
        keep["expert_x"] = tables.take("expert_x", [P, E, B, KD, CAP])
        keep["w_in"] = [tables.take(f"w_in{i}", [P, 2 * D]) for i in range(W_RING)]
        keep["w_loaded"] = [ctx.enter_context(nc.semaphore(f"w_loaded{i}")) for i in range(W_RING)]
        rest = tables.at
        phase3 = Arena(nc, rest, end)
        keep["x2_all"] = phase3.take("x2_all", [P, B * T, D])
        keep["logits"] = phase3.take("logits", [P, T, B, E])
        keep["index_all"] = [phase3.take(f"index_all{p}", [P, E * CAP]) for p in range(2)]
        keep["index_in"] = [ctx.enter_context(nc.semaphore(f"index_in{p}")) for p in range(2)]
        attention(nc, dram, keep, Arena(nc, middle, rest))
        route(nc, dram, keep, Arena(nc, middle, rest))
        gather(nc, dram, keep, phase3)
        experts(nc, dram, keep, Arena(nc, rest, end))
        scatter(nc, dram, keep, Arena(nc, rest - 4 * 2 * D * W_RING, end))


def kernel(**inputs):
    import concourse.bacc as bacc
    from concourse.bass_utils import run_bass_kernel_spmd

    def a(name):
        return np.asarray(inputs[name])

    arrays = {
        "x": a("x").reshape(B * N, D),
        "ctx": a("ctx_1024").reshape(B * KC, D),
        "g_xattn": a("g_xattn").reshape(1),
        "g_ffn": a("g_ffn").reshape(1),
        "fm_wT": np.tile(a("L0_xattn_fm_w").T, (P // HD, 1)),
        "fm_b": np.tile(a("L0_xattn_fm_b").reshape(HD, 1), (P // HD, 1)),
        "fc_wT": a("L0_xattn_fc_w").T,
        "fc_b": a("L0_xattn_fc_b"),
        "gate_queryT": a("L0_ffn_gate_query").T,
        "log_temp": a("L0_ffn_log_temp").reshape(1),
        "w1": a("L0_ffn_w1").reshape(E * D, FF),
        "b1": a("L0_ffn_b1").reshape(E * M, P).T,
        "w2": a("L0_ffn_w2").reshape(E * FF, D),
        "b2": a("L0_ffn_b2"),
    }
    arrays = {f"in_{n}": np.ascontiguousarray(v) for n, v in arrays.items()}
    nc = bacc.Bacc("TRN2", target_bir_lowering=False, num_devices=1)
    dram = {n[3:]: nc.dram_tensor(n, v.shape, mybir.dt.from_np(v.dtype), kind="ExternalInput").ap()
            for n, v in arrays.items()}
    dram["x1"] = nc.dram_tensor("x1_scratch", (B * P, T * D), F32, kind="Internal").ap()
    dram["slot_index"] = nc.dram_tensor("slot_index_scratch", (B * E, CAP), F32, kind="Internal").ap()
    dram["out"] = nc.dram_tensor("out_x", (B * N, D), F32, kind="ExternalOutput").ap()
    flamingo_layer(nc, dram)
    result = run_bass_kernel_spmd(nc, [arrays], core_ids=[0])
    return result.results[0]["out_x"].reshape(B, N, D)
```
